# Optimizing a Trainium2 kernel written in Bass

```python
import numpy as np
import jax
import jax.numpy as jnp

def _softmax(x, axis=-1):
    return jax.nn.softmax(x, axis=axis)

def _gelu(x):
    return jax.nn.gelu(x, approximate=True)

def _silu(x):
    return jax.nn.silu(x)

def _sigmoid(x):
    return jax.nn.sigmoid(x)

def _layernorm(x, axis=-1, eps=1e-05):
    m = jnp.mean(x, axis=axis, keepdims=True)
    v = jnp.var(x, axis=axis, keepdims=True)
    return (x - m) / jnp.sqrt(v + eps)

def _scatter_add(tgt, idx, src, axis=0):
    return tgt.at[idx].add(src)

def _segment_sum(src, seg, n):
    return jax.ops.segment_sum(src, seg, n)
kernel_name = 'mk_pixart_seq_d4_seqx_r4_bf41e4'

def setup_inputs(seed: int=0):
    np.random.seed(seed)
    _w = jnp.asarray

    def _rec_inputs():
        import jax
        import jax.numpy as jnp
        _rk = jax.random.key(seed)
        x = 7.22e-05 + 1 * jax.random.normal(jax.random.fold_in(_rk, 1), (4, 512, 256), jnp.float32)
        _lenS = 512 - jax.random.randint(jax.random.fold_in(_rk, 7), (4,), 0, max(1, 512 // 4) + 1, jnp.int32)
        _lenS2 = 64 - jax.random.randint(jax.random.fold_in(_rk, 8), (4,), 0, max(1, 64 // 4) + 1, jnp.int32)
        cond_1024 = 0.000887014 + 1.03683 * jax.random.normal(jax.random.fold_in(_rk, 11), (4, 256), jnp.float32)
        _ctx_1024P = jax.random.normal(jax.random.fold_in(_rk, 12), (4, 16, 256), jnp.float32)
        _ctx_1024c = jax.random.dirichlet(jax.random.fold_in(_rk, 512), 0.3 * jnp.ones((16,), jnp.float32), (4, 64))
        _ctx_1024t = jnp.einsum('bsk,bkd->bsd', _ctx_1024c, _ctx_1024P)
        _ctx_1024t = _ctx_1024t * jax.lax.rsqrt(jnp.mean(jnp.square(_ctx_1024t)) + 1e-12) * 0.953939
        ctx_1024 = 0.00086875 + 0.999764 * (_ctx_1024t + 0.3 * jax.random.normal(jax.random.fold_in(_rk, 612), (4, 64, 256), jnp.float32))
        _validS = jnp.arange(512)[None, :] < _lenS[:, None]
        _validS2 = jnp.arange(64)[None, :] < _lenS2[:, None]
        _causal = jnp.tril(jnp.ones((512, 512), dtype=bool))
        mask_BxS2_bf0 = jnp.logical_not(jnp.ones((4, 64), dtype=bool))
        return (x, cond_1024, ctx_1024, mask_BxS2_bf0)
    x, cond_1024, ctx_1024, mask_BxS2_bf0 = _rec_inputs()

    def _L0_xcond_setup():
        import jax, jax.numpy as jnp
        import numpy as np
        C = 256
        H = 16
        D = C // H
        WIN = 128
        SHIFT = 64
        TOPK = 16
        HID = 1024
        EPS = 1e-06

        def _ln(x):
            x32 = x.astype(jnp.float32)
            m = x32.mean(-1, keepdims=True)
            v = jnp.mean((x32 - m) ** 2, axis=-1, keepdims=True)
            return ((x32 - m) * jax.lax.rsqrt(v + EPS)).astype(x.dtype)

        def _self_attn(h, w_qkv, b_qkv, w_so, b_so):
            B, L, _ = h.shape
            qkv = h @ w_qkv + b_qkv
            qkv = jnp.roll(qkv, -SHIFT, axis=1)
            nw = L // WIN
            qkv = qkv.reshape(B, nw, WIN, 3, H, D)
            q, k, v = (qkv[:, :, :, 0], qkv[:, :, :, 1], qkv[:, :, :, 2])
            scores = jnp.einsum('bnqhd,bnkhd->bnhqk', q, k) / jnp.sqrt(jnp.float32(D)).astype(h.dtype)
            attn = jax.nn.softmax(scores, axis=-1)
            o = jnp.einsum('bnhqk,bnkhd->bnqhd', attn, v).reshape(B, L, C)
            o = jnp.roll(o, SHIFT, axis=1)
            return o @ w_so + b_so

        def _topk_cross_attn(h, ctx, w_q, b_q, w_kv, b_kv, w_co, b_co):
            B, L, _ = h.shape
            Lc = ctx.shape[1]
            q = (h @ w_q + b_q).reshape(B, L, H, D)
            kv = (ctx @ w_kv + b_kv).reshape(B, Lc, 2, H, D)
            k, v = (kv[:, :, 0], kv[:, :, 1])
            scores = jnp.einsum('bqhd,bkhd->bhqk', q, k) / jnp.sqrt(jnp.float32(D)).astype(h.dtype)
            top_s, top_i = jax.lax.top_k(scores, TOPK)
            attn = jax.nn.softmax(top_s, axis=-1)
            v_bh = jnp.transpose(v, (0, 2, 1, 3))
            vg = jnp.take_along_axis(v_bh[:, :, None, :, :], top_i[..., None], axis=3)
            o = jnp.einsum('bhqk,bhqkd->bqhd', attn, vg).reshape(B, L, C)
            return o @ w_co + b_co

        def _swiglu(h, w_m1, b_m1, w_m2, b_m2):
            u = h @ w_m1 + b_m1
            a, b = (u[..., :HID], u[..., HID:])
            return jax.nn.silu(a) * b @ w_m2 + b_m2
        key = jax.random.key(seed)
        ks = jax.random.split(key, 24)
        s = 0.02
        inp = {'x': jax.random.normal(ks[0], (2, 1024, C), jnp.float32), 'mod': jax.random.normal(ks[1], (2, C), jnp.float32), 'context': jax.random.normal(ks[2], (2, 256, C), jnp.float32), 'w_ada': jax.random.normal(ks[3], (C, 9 * C), jnp.float32) * s, 'b_ada': jnp.zeros((9 * C,), jnp.float32), 'w_qkv': jax.random.normal(ks[4], (C, 3 * C), jnp.float32) * s, 'b_qkv': jnp.zeros((3 * C,), jnp.float32), 'w_so': jax.random.normal(ks[5], (C, C), jnp.float32) * s, 'b_so': jnp.zeros((C,), jnp.float32), 'w_q': jax.random.normal(ks[6], (C, C), jnp.float32) * s, 'b_q': jnp.zeros((C,), jnp.float32), 'w_kv': jax.random.normal(ks[7], (C, 2 * C), jnp.float32) * s, 'b_kv': jnp.zeros((2 * C,), jnp.float32), 'w_co': jax.random.normal(ks[8], (C, C), jnp.float32) * s, 'b_co': jnp.zeros((C,), jnp.float32), 'w_m1': jax.random.normal(ks[9], (C, 2 * HID), jnp.float32) * s, 'b_m1': jnp.zeros((2 * HID,), jnp.float32), 'w_m2': jax.random.normal(ks[10], (HID, C), jnp.float32) * s, 'b_m2': jnp.zeros((C,), jnp.float32)}
        return inp
    _L0_xcond_all = _L0_xcond_setup()
    _L0_xcond_in = {k: v for k, v in _L0_xcond_all.items() if k in ('w_ada', 'b_ada', 'w_qkv', 'b_qkv', 'w_so', 'b_so', 'w_q', 'b_q', 'w_kv', 'b_kv', 'w_co', 'b_co', 'w_m1', 'b_m1', 'w_m2', 'b_m2')}
    del _L0_xcond_all

    def _L1_xcond_setup():
        import jax, jax.numpy as jnp
        import numpy as np
        LN_EPS = 1e-06

        def _ln(x):
            mu = jnp.mean(x, axis=-1, keepdims=True)
            var = jnp.var(x, axis=-1, keepdims=True)
            return (x - mu) * jax.lax.rsqrt(var + LN_EPS)
        key = jax.random.key(seed)
        H, NH = (256, 16)
        B, N, S = (4, 256, 77)
        MLP = int(H * 4.0)
        ks = jax.random.split(key, 20)
        s = 1.0 / np.sqrt(H)
        return {'x': jax.random.normal(ks[0], (B, N, H), jnp.float32), 'c': jax.random.normal(ks[1], (B, H), jnp.float32), 'context': jax.random.normal(ks[2], (B, S, H), jnp.float32), 'W_mod': jax.random.normal(ks[3], (H, 6 * H), jnp.float32) * s, 'b_mod': jnp.zeros((6 * H,), jnp.float32), 'W_qkv': jax.random.normal(ks[4], (H, 3 * H), jnp.float32) * s, 'b_qkv': jnp.zeros((3 * H,), jnp.float32), 'W_proj': jax.random.normal(ks[5], (H, H), jnp.float32) * s, 'b_proj': jnp.zeros((H,), jnp.float32), 'W_qc': jax.random.normal(ks[6], (H, H), jnp.float32) * s, 'b_qc': jnp.zeros((H,), jnp.float32), 'W_kvc': jax.random.normal(ks[7], (H, 2 * H), jnp.float32) * s, 'b_kvc': jnp.zeros((2 * H,), jnp.float32), 'W_cproj': jax.random.normal(ks[8], (H, H), jnp.float32) * s, 'b_cproj': jnp.zeros((H,), jnp.float32), 'W_mlp1': jax.random.normal(ks[9], (H, MLP), jnp.float32) * s, 'b_mlp1': jnp.zeros((MLP,), jnp.float32), 'W_mlp2': jax.random.normal(ks[10], (MLP, H), jnp.float32) * (1.0 / np.sqrt(MLP)), 'b_mlp2': jnp.zeros((H,), jnp.float32)}
    _L1_xcond_all = _L1_xcond_setup()
    _L1_xcond_in = {k: v for k, v in _L1_xcond_all.items() if k in ('W_mod', 'b_mod', 'W_qkv', 'b_qkv', 'W_proj', 'b_proj', 'W_qc', 'b_qc', 'W_kvc', 'b_kvc', 'W_cproj', 'b_cproj', 'W_mlp1', 'b_mlp1', 'W_mlp2', 'b_mlp2')}
    del _L1_xcond_all

    def _L2_xcond_setup():
        import jax, jax.numpy as jnp
        import numpy as np
        D, H, B, N, S = (256, 16, 4, 256, 77)
        HD = D // H
        DF = 4 * D
        EPS = 1e-06
        SCALE = HD ** (-0.5)

        def _ln(x):
            m = jnp.mean(x, axis=-1, keepdims=True)
            v = jnp.mean((x - m) ** 2, axis=-1, keepdims=True)
            return (x - m) / jnp.sqrt(v + EPS)
        key = jax.random.key(seed)
        ks = jax.random.split(key, 24)
        s = 0.02
        inp = {'x': jax.random.normal(ks[0], (B, N, D), jnp.float32), 't_emb': jax.random.normal(ks[1], (B, D), jnp.float32), 'context': jax.random.normal(ks[2], (B, S, D), jnp.float32), 'context_mask': jnp.zeros((B, S), jnp.bool_), 'ada_w': jax.random.normal(ks[3], (D, 6 * D), jnp.float32) * s, 'ada_b': jnp.zeros((6 * D,), jnp.float32), 'qkv_w': jax.random.normal(ks[4], (D, 3 * D), jnp.float32) * s, 'qkv_b': jnp.zeros((3 * D,), jnp.float32), 'sa_proj_w': jax.random.normal(ks[5], (D, D), jnp.float32) * s, 'sa_proj_b': jnp.zeros((D,), jnp.float32), 'q_w': jax.random.normal(ks[6], (D, D), jnp.float32) * s, 'q_b': jnp.zeros((D,), jnp.float32), 'kv_w': jax.random.normal(ks[7], (D, 2 * D), jnp.float32) * s, 'kv_b': jnp.zeros((2 * D,), jnp.float32), 'ca_proj_w': jax.random.normal(ks[8], (D, D), jnp.float32) * s, 'ca_proj_b': jnp.zeros((D,), jnp.float32), 'fc1_w': jax.random.normal(ks[9], (D, DF), jnp.float32) * s, 'fc1_b': jnp.zeros((DF,), jnp.float32), 'fc2_w': jax.random.normal(ks[10], (DF, D), jnp.float32) * s, 'fc2_b': jnp.zeros((D,), jnp.float32)}
        return inp
    _L2_xcond_all = _L2_xcond_setup()
    _L2_xcond_in = {k: v for k, v in _L2_xcond_all.items() if k in ('ada_w', 'ada_b', 'qkv_w', 'qkv_b', 'sa_proj_w', 'sa_proj_b', 'q_w', 'q_b', 'kv_w', 'kv_b', 'ca_proj_w', 'ca_proj_b', 'fc1_w', 'fc1_b', 'fc2_w', 'fc2_b')}
    del _L2_xcond_all

    def _L3_xcond_setup():
        import jax, jax.numpy as jnp
        import numpy as np
        H = 256
        RH = 2 * H
        E = 3
        B, T, P = (8, 512, 64)
        LN_EPS = 1e-05

        def _layer_norm(x, gamma, beta):
            mu = jnp.mean(x, axis=-1, keepdims=True)
            var = jnp.mean(jnp.square(x - mu), axis=-1, keepdims=True)
            return (x - mu) * jax.lax.rsqrt(var + LN_EPS) * gamma + beta
        key = jax.random.key(seed)
        ks = jax.random.split(key, 24)
        s = lambda fan_in: 1.0 / np.sqrt(fan_in)
        inp = {'mix_hidden_states': jax.random.normal(ks[0], (B, T, H), jnp.float32), 'global_anchor': jax.random.normal(ks[1], (B, H), jnp.float32), 'prototype_bank': jax.random.normal(ks[2], (B, P, H), jnp.float32), 'ln_gamma': jnp.ones((H,), jnp.float32), 'ln_beta': jnp.zeros((H,), jnp.float32), 'Wq': jax.random.normal(ks[3], (H, H), jnp.float32) * s(H), 'Wk': jax.random.normal(ks[4], (H, H), jnp.float32) * s(H), 'Wv': jax.random.normal(ks[5], (H, H), jnp.float32) * s(H), 'router_W': jax.random.normal(ks[6], (3 * H, E), jnp.float32) * s(3 * H), 'router_b': jnp.zeros((E,), jnp.float32), 'e_w1': jax.random.normal(ks[7], (E, 3 * H, RH), jnp.float32) * s(3 * H), 'e_b1': jnp.zeros((E, RH), jnp.float32), 'e_w2': jax.random.normal(ks[8], (E, RH, H), jnp.float32) * s(RH), 'e_b2': jnp.zeros((E, H), jnp.float32), 'gate_w1': jax.random.normal(ks[9], (3 * H, H), jnp.float32) * s(3 * H), 'gate_b1': jnp.zeros((H,), jnp.float32), 'gate_w2': jax.random.normal(ks[10], (H, H), jnp.float32) * s(H), 'gate_b2': jnp.zeros((H,), jnp.float32), 'out_w': jax.random.normal(ks[11], (H, H), jnp.float32) * s(H), 'out_b': jnp.zeros((H,), jnp.float32)}
        return inp
    _L3_xcond_all = _L3_xcond_setup()
    _L3_xcond_in = {k: v for k, v in _L3_xcond_all.items() if k in ('ln_gamma', 'ln_beta', 'Wq', 'Wk', 'Wv', 'router_W', 'router_b', 'e_w1', 'e_b1', 'e_w2', 'e_b2', 'gate_w1', 'gate_b1', 'gate_w2', 'gate_b2', 'out_w', 'out_b')}
    del _L3_xcond_all
    return {'x': x, 'cond_1024': cond_1024, 'ctx_1024': ctx_1024, 'mask_BxS2_bf0': mask_BxS2_bf0, 'L0_xcond_w_ada': _L0_xcond_in['w_ada'], 'L0_xcond_b_ada': _L0_xcond_in['b_ada'], 'L0_xcond_w_qkv': _L0_xcond_in['w_qkv'], 'L0_xcond_b_qkv': _L0_xcond_in['b_qkv'], 'L0_xcond_w_so': _L0_xcond_in['w_so'], 'L0_xcond_b_so': _L0_xcond_in['b_so'], 'L0_xcond_w_q': _L0_xcond_in['w_q'], 'L0_xcond_b_q': _L0_xcond_in['b_q'], 'L0_xcond_w_kv': _L0_xcond_in['w_kv'], 'L0_xcond_b_kv': _L0_xcond_in['b_kv'], 'L0_xcond_w_co': _L0_xcond_in['w_co'], 'L0_xcond_b_co': _L0_xcond_in['b_co'], 'L0_xcond_w_m1': _L0_xcond_in['w_m1'], 'L0_xcond_b_m1': _L0_xcond_in['b_m1'], 'L0_xcond_w_m2': _L0_xcond_in['w_m2'], 'L0_xcond_b_m2': _L0_xcond_in['b_m2'], 'L1_xcond_W_mod': _L1_xcond_in['W_mod'], 'L1_xcond_b_mod': _L1_xcond_in['b_mod'], 'L1_xcond_W_qkv': _L1_xcond_in['W_qkv'], 'L1_xcond_b_qkv': _L1_xcond_in['b_qkv'], 'L1_xcond_W_proj': _L1_xcond_in['W_proj'], 'L1_xcond_b_proj': _L1_xcond_in['b_proj'], 'L1_xcond_W_qc': _L1_xcond_in['W_qc'], 'L1_xcond_b_qc': _L1_xcond_in['b_qc'], 'L1_xcond_W_kvc': _L1_xcond_in['W_kvc'], 'L1_xcond_b_kvc': _L1_xcond_in['b_kvc'], 'L1_xcond_W_cproj': _L1_xcond_in['W_cproj'], 'L1_xcond_b_cproj': _L1_xcond_in['b_cproj'], 'L1_xcond_W_mlp1': _L1_xcond_in['W_mlp1'], 'L1_xcond_b_mlp1': _L1_xcond_in['b_mlp1'], 'L1_xcond_W_mlp2': _L1_xcond_in['W_mlp2'], 'L1_xcond_b_mlp2': _L1_xcond_in['b_mlp2'], 'L2_xcond_ada_w': _L2_xcond_in['ada_w'], 'L2_xcond_ada_b': _L2_xcond_in['ada_b'], 'L2_xcond_qkv_w': _L2_xcond_in['qkv_w'], 'L2_xcond_qkv_b': _L2_xcond_in['qkv_b'], 'L2_xcond_sa_proj_w': _L2_xcond_in['sa_proj_w'], 'L2_xcond_sa_proj_b': _L2_xcond_in['sa_proj_b'], 'L2_xcond_q_w': _L2_xcond_in['q_w'], 'L2_xcond_q_b': _L2_xcond_in['q_b'], 'L2_xcond_kv_w': _L2_xcond_in['kv_w'], 'L2_xcond_kv_b': _L2_xcond_in['kv_b'], 'L2_xcond_ca_proj_w': _L2_xcond_in['ca_proj_w'], 'L2_xcond_ca_proj_b': _L2_xcond_in['ca_proj_b'], 'L2_xcond_fc1_w': _L2_xcond_in['fc1_w'], 'L2_xcond_fc1_b': _L2_xcond_in['fc1_b'], 'L2_xcond_fc2_w': _L2_xcond_in['fc2_w'], 'L2_xcond_fc2_b': _L2_xcond_in['fc2_b'], 'L3_xcond_ln_gamma': _L3_xcond_in['ln_gamma'], 'L3_xcond_ln_beta': _L3_xcond_in['ln_beta'], 'L3_xcond_Wq': _L3_xcond_in['Wq'], 'L3_xcond_Wk': _L3_xcond_in['Wk'], 'L3_xcond_Wv': _L3_xcond_in['Wv'], 'L3_xcond_router_W': _L3_xcond_in['router_W'], 'L3_xcond_router_b': _L3_xcond_in['router_b'], 'L3_xcond_e_w1': _L3_xcond_in['e_w1'], 'L3_xcond_e_b1': _L3_xcond_in['e_b1'], 'L3_xcond_e_w2': _L3_xcond_in['e_w2'], 'L3_xcond_e_b2': _L3_xcond_in['e_b2'], 'L3_xcond_gate_w1': _L3_xcond_in['gate_w1'], 'L3_xcond_gate_b1': _L3_xcond_in['gate_b1'], 'L3_xcond_gate_w2': _L3_xcond_in['gate_w2'], 'L3_xcond_gate_b2': _L3_xcond_in['gate_b2'], 'L3_xcond_out_w': _L3_xcond_in['out_w'], 'L3_xcond_out_b': _L3_xcond_in['out_b']}

def reference(x, cond_1024, ctx_1024, mask_BxS2_bf0, L0_xcond_w_ada, L0_xcond_b_ada, L0_xcond_w_qkv, L0_xcond_b_qkv, L0_xcond_w_so, L0_xcond_b_so, L0_xcond_w_q, L0_xcond_b_q, L0_xcond_w_kv, L0_xcond_b_kv, L0_xcond_w_co, L0_xcond_b_co, L0_xcond_w_m1, L0_xcond_b_m1, L0_xcond_w_m2, L0_xcond_b_m2, L1_xcond_W_mod, L1_xcond_b_mod, L1_xcond_W_qkv, L1_xcond_b_qkv, L1_xcond_W_proj, L1_xcond_b_proj, L1_xcond_W_qc, L1_xcond_b_qc, L1_xcond_W_kvc, L1_xcond_b_kvc, L1_xcond_W_cproj, L1_xcond_b_cproj, L1_xcond_W_mlp1, L1_xcond_b_mlp1, L1_xcond_W_mlp2, L1_xcond_b_mlp2, L2_xcond_ada_w, L2_xcond_ada_b, L2_xcond_qkv_w, L2_xcond_qkv_b, L2_xcond_sa_proj_w, L2_xcond_sa_proj_b, L2_xcond_q_w, L2_xcond_q_b, L2_xcond_kv_w, L2_xcond_kv_b, L2_xcond_ca_proj_w, L2_xcond_ca_proj_b, L2_xcond_fc1_w, L2_xcond_fc1_b, L2_xcond_fc2_w, L2_xcond_fc2_b, L3_xcond_ln_gamma, L3_xcond_ln_beta, L3_xcond_Wq, L3_xcond_Wk, L3_xcond_Wv, L3_xcond_router_W, L3_xcond_router_b, L3_xcond_e_w1, L3_xcond_e_b1, L3_xcond_e_w2, L3_xcond_e_b2, L3_xcond_gate_w1, L3_xcond_gate_b1, L3_xcond_gate_w2, L3_xcond_gate_b2, L3_xcond_out_w, L3_xcond_out_b):
    import jax
    import jax.numpy as jnp

    def _L0_xcond_ref(x, mod, context, w_ada, b_ada, w_qkv, b_qkv, w_so, b_so, w_q, b_q, w_kv, b_kv, w_co, b_co, w_m1, b_m1, w_m2, b_m2):
        import jax, jax.numpy as jnp
        import numpy as np
        C = 256
        H = 16
        D = C // H
        WIN = 128
        SHIFT = 64
        TOPK = 16
        HID = 1024
        EPS = 1e-06

        def _ln(x):
            x32 = x.astype(jnp.float32)
            m = x32.mean(-1, keepdims=True)
            v = jnp.mean((x32 - m) ** 2, axis=-1, keepdims=True)
            return ((x32 - m) * jax.lax.rsqrt(v + EPS)).astype(x.dtype)

        def _self_attn(h, w_qkv, b_qkv, w_so, b_so):
            B, L, _ = h.shape
            qkv = h @ w_qkv + b_qkv
            qkv = jnp.roll(qkv, -SHIFT, axis=1)
            nw = L // WIN
            qkv = qkv.reshape(B, nw, WIN, 3, H, D)
            q, k, v = (qkv[:, :, :, 0], qkv[:, :, :, 1], qkv[:, :, :, 2])
            scores = jnp.einsum('bnqhd,bnkhd->bnhqk', q, k) / jnp.sqrt(jnp.float32(D)).astype(h.dtype)
            attn = jax.nn.softmax(scores, axis=-1)
            o = jnp.einsum('bnhqk,bnkhd->bnqhd', attn, v).reshape(B, L, C)
            o = jnp.roll(o, SHIFT, axis=1)
            return o @ w_so + b_so

        def _topk_cross_attn(h, ctx, w_q, b_q, w_kv, b_kv, w_co, b_co):
            B, L, _ = h.shape
            Lc = ctx.shape[1]
            q = (h @ w_q + b_q).reshape(B, L, H, D)
            kv = (ctx @ w_kv + b_kv).reshape(B, Lc, 2, H, D)
            k, v = (kv[:, :, 0], kv[:, :, 1])
            scores = jnp.einsum('bqhd,bkhd->bhqk', q, k) / jnp.sqrt(jnp.float32(D)).astype(h.dtype)
            top_s, top_i = jax.lax.top_k(scores, TOPK)
            attn = jax.nn.softmax(top_s, axis=-1)
            v_bh = jnp.transpose(v, (0, 2, 1, 3))
            vg = jnp.take_along_axis(v_bh[:, :, None, :, :], top_i[..., None], axis=3)
            o = jnp.einsum('bhqk,bhqkd->bqhd', attn, vg).reshape(B, L, C)
            return o @ w_co + b_co

        def _swiglu(h, w_m1, b_m1, w_m2, b_m2):
            u = h @ w_m1 + b_m1
            a, b = (u[..., :HID], u[..., HID:])
            return jax.nn.silu(a) * b @ w_m2 + b_m2
        m = jax.nn.silu(mod) @ w_ada + b_ada
        sh_msa, sc_msa, g_msa, sh_mca, sc_mca, g_mca, sh_mlp, sc_mlp, g_mlp = [m[:, i * C:(i + 1) * C][:, None, :] for i in range(9)]
        h = _ln(x) * (1 + sc_msa) + sh_msa
        h = _self_attn(h, w_qkv, b_qkv, w_so, b_so)
        x = x + h * g_msa
        h = _ln(x) * (1 + sc_mca) + sh_mca
        h = _topk_cross_attn(h, context, w_q, b_q, w_kv, b_kv, w_co, b_co)
        x = x + h * g_mca
        h = _ln(x) * (1 + sc_mlp) + sh_mlp
        h = _swiglu(h, w_m1, b_m1, w_m2, b_m2)
        x = x + h * g_mlp
        return x

    def _L1_xcond_ref(x, c, context, W_mod, b_mod, W_qkv, b_qkv, W_proj, b_proj, W_qc, b_qc, W_kvc, b_kvc, W_cproj, b_cproj, W_mlp1, b_mlp1, W_mlp2, b_mlp2):
        import jax, jax.numpy as jnp
        import numpy as np
        LN_EPS = 1e-06

        def _ln(x):
            mu = jnp.mean(x, axis=-1, keepdims=True)
            var = jnp.var(x, axis=-1, keepdims=True)
            return (x - mu) * jax.lax.rsqrt(var + LN_EPS)
        B, N, H = x.shape
        NH = 16
        hd = H // NH
        scale = hd ** (-0.5)
        c_proj = jax.nn.silu(c) @ W_mod + b_mod
        shift_a, scale_a, gate_a, shift_m, scale_m, gate_m = jnp.split(c_proj, 6, axis=-1)

        def modulate(t, shift, sc):
            return t * (1 + sc[:, None]) + shift[:, None]
        x_norm = modulate(_ln(x), shift_a, scale_a)
        qkv = x_norm @ W_qkv + b_qkv
        q, k, v = jnp.split(qkv, 3, axis=-1)
        q = q.reshape(B, N, NH, hd).transpose(0, 2, 1, 3)
        k = k.reshape(B, N, NH, hd).transpose(0, 2, 1, 3)
        v = v.reshape(B, N, NH, hd).transpose(0, 2, 1, 3)
        attn_w = jax.nn.softmax(jnp.einsum('bhqd,bhkd->bhqk', q, k) * scale, axis=-1)
        attn_out = jnp.einsum('bhqk,bhkd->bhqd', attn_w, v)
        attn_out = attn_out.transpose(0, 2, 1, 3).reshape(B, N, H)
        attn_out = attn_out @ W_proj + b_proj
        x = x + gate_a[:, None] * attn_out
        S = context.shape[1]
        q_c = _ln(x) @ W_qc + b_qc
        kv_c = _ln(context) @ W_kvc + b_kvc
        k_c, v_c = jnp.split(kv_c, 2, axis=-1)
        q_c = q_c.reshape(B, N, NH, hd).transpose(0, 2, 1, 3)
        k_c = k_c.reshape(B, S, NH, hd).transpose(0, 2, 1, 3)
        v_c = v_c.reshape(B, S, NH, hd).transpose(0, 2, 1, 3)
        c_attn_w = jax.nn.softmax(jnp.einsum('bhqd,bhsd->bhqs', q_c, k_c) * scale, axis=-1)
        c_attn_out = jnp.einsum('bhqs,bhsd->bhqd', c_attn_w, v_c)
        c_attn_out = c_attn_out.transpose(0, 2, 1, 3).reshape(B, N, H)
        c_attn_out = c_attn_out @ W_cproj + b_cproj
        x = x + c_attn_out
        x_norm2 = modulate(_ln(x), shift_m, scale_m)
        h = jax.nn.gelu(x_norm2 @ W_mlp1 + b_mlp1)
        h = h @ W_mlp2 + b_mlp2
        x = x + gate_m[:, None] * h
        return x

    def _L2_xcond_ref(x, t_emb, context, context_mask, ada_w, ada_b, qkv_w, qkv_b, sa_proj_w, sa_proj_b, q_w, q_b, kv_w, kv_b, ca_proj_w, ca_proj_b, fc1_w, fc1_b, fc2_w, fc2_b):
        import jax, jax.numpy as jnp
        import numpy as np
        D, H, B, N, S = (256, 16, 4, 256, 77)
        HD = D // H
        DF = 4 * D
        EPS = 1e-06
        SCALE = HD ** (-0.5)

        def _ln(x):
            m = jnp.mean(x, axis=-1, keepdims=True)
            v = jnp.mean((x - m) ** 2, axis=-1, keepdims=True)
            return (x - m) / jnp.sqrt(v + EPS)
        Bx, Nx, C = x.shape
        Sx = context.shape[1]
        mod = jax.nn.silu(t_emb) @ ada_w + ada_b
        shift_sa, scale_sa, gate_sa, shift_ff, scale_ff, gate_ff = [m[:, None, :] for m in jnp.split(mod, 6, axis=-1)]
        xm1 = _ln(x) * (1 + scale_sa) + shift_sa
        qkv = (xm1 @ qkv_w + qkv_b).reshape(Bx, Nx, 3, H, HD)
        q, k, v = (qkv[:, :, 0], qkv[:, :, 1], qkv[:, :, 2])
        attn = jnp.einsum('bnhd,bmhd->bhnm', q, k) * SCALE
        attn = jax.nn.softmax(attn, axis=-1)
        sa = jnp.einsum('bhnm,bmhd->bnhd', attn, v).reshape(Bx, Nx, C)
        sa = sa @ sa_proj_w + sa_proj_b
        x = x + gate_sa * sa
        xn2 = _ln(x)
        qc = (xn2 @ q_w + q_b).reshape(Bx, Nx, H, HD)
        kvc = (context @ kv_w + kv_b).reshape(Bx, Sx, 2, H, HD)
        kc, vc = (kvc[:, :, 0], kvc[:, :, 1])
        attn_c = jnp.einsum('bnhd,bshd->bhns', qc, kc) * SCALE
        attn_c = jnp.where(context_mask[:, None, None, :], -jnp.inf, attn_c)
        attn_c = jax.nn.softmax(attn_c, axis=-1)
        ca = jnp.einsum('bhns,bshd->bnhd', attn_c, vc).reshape(Bx, Nx, C)
        ca = ca @ ca_proj_w + ca_proj_b
        x = x + ca
        xm3 = _ln(x) * (1 + scale_ff) + shift_ff
        h = jax.nn.gelu(xm3 @ fc1_w + fc1_b, approximate=False)
        ff = h @ fc2_w + fc2_b
        x = x + gate_ff * ff
        return x

    def _L3_xcond_ref(mix_hidden_states, global_anchor, prototype_bank, ln_gamma, ln_beta, Wq, Wk, Wv, router_W, router_b, e_w1, e_b1, e_w2, e_b2, gate_w1, gate_b1, gate_w2, gate_b2, out_w, out_b):
        import jax, jax.numpy as jnp
        import numpy as np
        H = 256
        RH = 2 * H
        E = 3
        B, T, P = (8, 512, 64)
        LN_EPS = 1e-05

        def _layer_norm(x, gamma, beta):
            mu = jnp.mean(x, axis=-1, keepdims=True)
            var = jnp.mean(jnp.square(x - mu), axis=-1, keepdims=True)
            return (x - mu) * jax.lax.rsqrt(var + LN_EPS) * gamma + beta
        x = mix_hidden_states
        nx = _layer_norm(x, ln_gamma, ln_beta)
        q = nx @ Wq
        k = prototype_bank @ Wk
        v = prototype_bank @ Wv
        scores = jnp.einsum('bth,bph->btp', q, k) * H ** (-0.5)
        weights = jax.nn.softmax(scores, axis=-1)
        evidence = jnp.einsum('btp,bph->bth', weights, v)
        anchor = jnp.broadcast_to(global_anchor[:, None, :], nx.shape)
        combined = jnp.concatenate([nx, evidence, anchor], axis=-1)
        router_logits = combined @ router_W + router_b
        router_probs = jax.nn.softmax(router_logits, axis=-1)
        h = jax.nn.silu(jnp.einsum('btc,ecr->bter', combined, e_w1) + e_b1)
        expert_out = jnp.einsum('bter,erh->bteh', h, e_w2) + e_b2
        routed = jnp.sum(expert_out * router_probs[..., None], axis=-2)
        g = jax.nn.sigmoid(jax.nn.silu(combined @ gate_w1 + gate_b1) @ gate_w2 + gate_b2)
        refined_delta = g * (routed @ out_w + out_b)
        return x + refined_delta
    x = _L0_xcond_ref(x, cond_1024, ctx_1024, L0_xcond_w_ada, L0_xcond_b_ada, L0_xcond_w_qkv, L0_xcond_b_qkv, L0_xcond_w_so, L0_xcond_b_so, L0_xcond_w_q, L0_xcond_b_q, L0_xcond_w_kv, L0_xcond_b_kv, L0_xcond_w_co, L0_xcond_b_co, L0_xcond_w_m1, L0_xcond_b_m1, L0_xcond_w_m2, L0_xcond_b_m2)
    x = _L1_xcond_ref(x, cond_1024, ctx_1024, L1_xcond_W_mod, L1_xcond_b_mod, L1_xcond_W_qkv, L1_xcond_b_qkv, L1_xcond_W_proj, L1_xcond_b_proj, L1_xcond_W_qc, L1_xcond_b_qc, L1_xcond_W_kvc, L1_xcond_b_kvc, L1_xcond_W_cproj, L1_xcond_b_cproj, L1_xcond_W_mlp1, L1_xcond_b_mlp1, L1_xcond_W_mlp2, L1_xcond_b_mlp2)
    x = _L2_xcond_ref(x, cond_1024, ctx_1024, mask_BxS2_bf0, L2_xcond_ada_w, L2_xcond_ada_b, L2_xcond_qkv_w, L2_xcond_qkv_b, L2_xcond_sa_proj_w, L2_xcond_sa_proj_b, L2_xcond_q_w, L2_xcond_q_b, L2_xcond_kv_w, L2_xcond_kv_b, L2_xcond_ca_proj_w, L2_xcond_ca_proj_b, L2_xcond_fc1_w, L2_xcond_fc1_b, L2_xcond_fc2_w, L2_xcond_fc2_b)
    x = _L3_xcond_ref(x, cond_1024, ctx_1024, L3_xcond_ln_gamma, L3_xcond_ln_beta, L3_xcond_Wq, L3_xcond_Wk, L3_xcond_Wv, L3_xcond_router_W, L3_xcond_router_b, L3_xcond_e_w1, L3_xcond_e_b1, L3_xcond_e_w2, L3_xcond_e_b2, L3_xcond_gate_w1, L3_xcond_gate_b1, L3_xcond_gate_w2, L3_xcond_gate_b2, L3_xcond_out_w, L3_xcond_out_b)
    return x

_drawn_inputs = setup_inputs


def setup_inputs(seed=0):
    import zlib

    import numpy as np

    out = dict(_drawn_inputs(seed))
    spreads = {'L0_xcond_b_ada': (0.0, 0.396),
     'L0_xcond_b_qkv': (0.0, 0.8),
     'L0_xcond_b_so': (0.0, 0.384),
     'L0_xcond_b_q': (0.0, 0.8),
     'L0_xcond_b_kv': (0.0, 0.8),
     'L0_xcond_b_co': (0.0, 0.407),
     'L0_xcond_b_m1': (0.0, 0.8),
     'L0_xcond_b_m2': (0.0, 2.0),
     'L1_xcond_b_mod': (0.0, 0.676),
     'L1_xcond_b_qkv': (0.0, 0.8),
     'L1_xcond_b_proj': (0.0, 0.8),
     'L1_xcond_b_qc': (0.0, 2.0),
     'L1_xcond_b_kvc': (0.0, 0.8),
     'L1_xcond_b_cproj': (0.0, 0.8),
     'L1_xcond_b_mlp1': (0.0, 0.8),
     'L1_xcond_b_mlp2': (0.0, 0.8),
     'L2_xcond_ada_b': (0.0, 0.563),
     'L2_xcond_qkv_b': (0.0, 0.8),
     'L2_xcond_sa_proj_b': (0.0, 1.867),
     'L2_xcond_q_b': (0.0, 2.0),
     'L2_xcond_kv_b': (0.0, 2.0),
     'L2_xcond_ca_proj_b': (0.0, 0.8),
     'L2_xcond_fc1_b': (0.0, 0.8),
     'L2_xcond_fc2_b': (0.0, 1.854),
     'L3_xcond_ln_gamma': (1.0, 0.6),
     'L3_xcond_ln_beta': (0.0, 2.0),
     'L3_xcond_router_b': (0.0, 2.0),
     'L3_xcond_e_b1': (0.0, 2.0),
     'L3_xcond_e_b2': (0.0, 2.0),
     'L3_xcond_gate_b1': (0.0, 2.0),
     'L3_xcond_gate_b2': (0.0, 2.0),
     'L3_xcond_out_b': (0.0, 0.8)}
    factors = {'L0_xcond_w_qkv': 8.0,
     'L0_xcond_w_so': 5.733,
     'L0_xcond_w_q': 8.0,
     'L0_xcond_w_kv': 4.169,
     'L0_xcond_w_co': 3.605,
     'L0_xcond_w_m1': 7.41,
     'L0_xcond_w_m2': 7.402,
     'L2_xcond_qkv_w': 5.426,
     'L2_xcond_sa_proj_w': 4.461,
     'L2_xcond_q_w': 64.0,
     'L2_xcond_fc1_w': 3.214,
     'L2_xcond_fc2_w': 2.998,
     'L1_xcond_W_qc': 3.998,
     'L2_xcond_kv_w': 8.0,
     'L2_xcond_ca_proj_w': 6.222,
     'L3_xcond_Wq': 8.0,
     'L3_xcond_Wk': 8.0,
     'L3_xcond_Wv': 7.413,
     'L3_xcond_router_W': 5.04,
     'L3_xcond_e_w1': 2.861,
     'L3_xcond_gate_w1': 8.0,
     'L3_xcond_gate_w2': 7.236}
    for name, (base, spread) in spreads.items():
        noise = np.random.default_rng([zlib.crc32(name.encode()), seed]).standard_normal(out[name].shape)
        drawn = base * np.exp(spread * noise) if base else spread * noise
        out[name] = jnp.asarray(drawn.astype(out[name].dtype))
    for name, factor in factors.items():
        out[name] = (out[name] * factor).astype(out[name].dtype)
    return out
```

```python
from contextlib import ExitStack

import numpy as np

import concourse.bass as bass
from concourse import mybir

F32 = mybir.dt.float32
F32R = mybir.dt.float32r
U8 = mybir.dt.uint8
U32 = mybir.dt.uint32
ALU = mybir.AluOpType
ACT = mybir.ActivationFunctionType
AX = mybir.AxisListType

P = 128
NB, T, C = 4, 512, 256
NT, KC = T // P, C // P
NH, HD = 16, 16
NQ = NH // 4
S2 = 64
SHIFT, TOPK = 64, 16
SCALE = float(HD) ** -0.5
LARGE = float(np.float32(3.0e38))
MASKED = -1.0e30
EPS = [1e-6, 1e-6, 1e-6, 1e-5]
NX = 3
RH = 512
RC = RH // P

VECS = {}
_at = 0
for _name, _inp, _first, _n in [
    ("ada0", "L0_xcond_b_ada", 0, 18), ("qk0", "L0_xcond_b_qkv", 0, 4), ("qx0", "L0_xcond_b_q", 0, 2),
    ("kx0", "L0_xcond_b_kv", 0, 2), ("m10", "L0_xcond_b_m1", 0, 16),
    ("ada1", "L1_xcond_b_mod", 0, 12), ("qk1", "L1_xcond_b_qkv", 0, 4), ("qx1", "L1_xcond_b_qc", 0, 2),
    ("kx1", "L1_xcond_b_kvc", 0, 2), ("m11", "L1_xcond_b_mlp1", 0, 8),
    ("ada2", "L2_xcond_ada_b", 0, 12), ("qk2", "L2_xcond_qkv_b", 0, 4), ("qx2", "L2_xcond_q_b", 0, 2),
    ("kx2", "L2_xcond_kv_b", 0, 2), ("m12", "L2_xcond_fc1_b", 0, 8),
    ("gamma", "L3_xcond_ln_gamma", 0, 2), ("beta", "L3_xcond_ln_beta", 0, 2),
    ("gb1", "L3_xcond_gate_b1", 0, 2), ("eb1", "L3_xcond_e_b1", 0, NX * RC), ("cond", "cond_1024", 0, NB * KC),
]:
    VECS[_name] = (_inp, _at, _n)
    _at += _n
NVEC = _at
assert NVEC <= P

ADA = [18, 12, 12]
ADA_AT = [0, 18, 30]
SHIFT_OF = [(0, 6, 12), (0, None, 6), (0, None, 6)]
SCALE_OF = [(2, 8, 14), (2, None, 8), (2, None, 8)]
GATE_OF = [(4, 10, 16), (4, None, 10), (4, None, 10)]
GATES = [[0, 1, 2], [0, 2], [0, 2]]
HIDC = 8
UP = [16, 8, 8]

UNITS = [4, 16, 16]
KCH = [1, 4, 4]


class Signal:

    def __init__(self, sem, per, first=0):
        self.sem, self.per, self.first = sem, per, first

    def at(self, layer, b, k):
        base = self.first + sum(NB * n for n in self.per[:layer])
        assert base + k > 0
        return b * self.per[layer] + (base + k)

    def end(self, layer):
        return self.first + sum(NB * n for n in self.per[: layer + 1])


def build(nc, a, out):
    with ExitStack() as ctx:
        def sb(name, shape, dt=F32):
            return ctx.enter_context(nc.sbuf_tensor(name, shape, dt))

        def sem(name):
            return ctx.enter_context(nc.semaphore(name))

        def sig(name, *per, first=0):
            return Signal(sem(name), per, first)

        x_all = sb("x_all", [P, NB * NT * C])
        weights = sb("weights", [P, 23826])
        q_stack = sb("q_stack", [P, 2, 4, T], F32R)
        k_stack = sb("k_stack", [P, 2, 4, T], F32R)
        probs = sb("probs", [P, 2, 4, T])
        work = sb("work", [P, 4, T])
        hT = sb("hT", [P, KC, T])
        xn = sb("xn", [P, NT, C])
        v_aug = sb("v_aug", [P, NT, NH, 2 * HD])
        k_bd = sb("k_bd", [P, KC, 8, S2])
        v_bd = sb("v_bd", [P, 8, 2 * HD])
        gate_rows = sb("gate_rows", [P, 3, C])
        bg_rows = sb("bg_rows", [P, 2, C])
        ident = sb("ident", [P, P])
        ones = sb("ones", [P, P])
        zeros = sb("zeros", [P, C])
        ones_pair = sb("ones_pair", [P, 2 * HD])
        head_mask = sb("head_mask", [P, 8])
        vec_rows = hT[:, 0, 0:P]
        vecs = sb("vecs", [P, NVEC])
        cond_s = sb("cond_s", [P, KC, NB])
        cond_r = sb("cond_r", [P, KC, NB])
        mod = sb("mod", [P, sum(ADA), NB])
        mod_now = sb("mod_now", [P, 18])
        ctx_tm = xn
        ctxT = sb("ctxT", [P, 2, KC, NB * S2])
        ctx_two = sb("ctx_two", [P, KC, 2, S2])
        kxT = sb("kxT", [P, KC, S2])
        stats = sb("stats", [P, NT, 6])
        mv = sb("mv", [P, NT, 2])
        var_eps = sb("var_eps", [P, NT])
        rstd = sb("rstd", [P, NT])
        half_neg = sb("half_neg", [P, NT])
        nm = sb("nm", [P, NT, NH])
        diag = hT[:, 0, 0:KC * P].rearrange("p (k n) -> p k n", k=KC)
        top = sb("top", [P, 8, 2, 8])
        mrow_words = sb("mrow_words", [1, NB * S2 // 4], U32)
        mask_row = sb("mask_row", [P, NB, S2], F32R)
        one_row = sb("one_row", [P, P], F32R)
        anchor_b = sb("anchor_b", [P, 14, NB])
        anchor_now = sb("anchor_now", [P, 14])
        router_b = sb("router_b", [NX, NB])
        router_now = sb("router_now", [NX, 1])
        router_in = sb("router_in", [NX, 1])
        lg = sb("lg", [P, NT, NX])
        pr = sb("pr", [P, NT, NX])
        sm = sb("sm", [P, 6, NT])

        bank = ctx.enter_context(nc.psum_tensor("bank", [P, 8, T], F32))
        A, B, O, X = 0, 2, 6, 7

        def place(at, *shape):
            n = int(np.prod(shape))
            v = weights[:, at:at + n]
            if len(shape) == 2:
                v = v.rearrange("p (k n) -> p k n", k=shape[0])
            if len(shape) == 3:
                v = v.rearrange("p (e k n) -> p e k n", e=shape[0], k=shape[1])
            return v, at + n

        W = [dict() for _ in range(4)]
        START = [0, 11776, 0, 9728]
        ends = []
        for L in range(3):
            at = START[L]
            for name, shape in [("qkv", (KC, 3 * C)), ("so", (NQ, C)), ("qx", (KC, C)), ("kvx", (KC, 2 * C)),
                                ("co", (KC, C)), ("m1", (KC, UP[L] * P)), ("m2", (HIDC, C)),
                                ("bv", (C,)), ("bvx", (C,)), ("bco", (C,)), ("bm2", (C,))]:
                W[L][name], at = place(at, *shape)
            ends.append(at)
        at = START[3]
        for name, shape in [("q", (KC, C)), ("k", (KC, C)), ("v", (KC, C)), ("w1", (NX, 4, RH)), ("w2", (NX, RC, C)),
                            ("g1", (4, C)), ("g2", (KC, C)), ("o", (KC, C)), ("r", (6, NX)),
                            ("b2", (NX, C)), ("gb2", (C,)), ("ob", (C,))]:
            W[3][name], at = place(at, *shape)
        ends.append(at)
        assert ends[0] <= START[1] and ends[2] <= START[3] and max(ends) <= 23826, ends
        ADA_N = [n * P for n in ADA]
        ada_w = [None, None, None]
        w1_at = START[1]
        ada_w[0], w1_at = place(w1_at, KC, ADA_N[0])
        ada_w[1], w1_at = place(w1_at, KC, ADA_N[1])
        assert w1_at <= 23826
        ada_w[2] = probs[:, :, :, :].rearrange("p a b t -> p (a b t)")[:, 0:KC * ADA_N[2]].rearrange(
            "p (k n) -> p k n", k=KC)
        pf = probs[:, :, :, :].rearrange("p a b t -> p (a b t)")
        w1_anchor = [pf[:, e * KC * RH:(e + 1) * KC * RH].rearrange("p (k n) -> p k n", k=KC) for e in range(NX)]
        g1_anchor = pf[:, NX * KC * RH:NX * KC * RH + KC * C].rearrange("p (k n) -> p k n", k=KC)

        split = pf[:, 0:4 * T].rearrange("p (r s t) -> p r s t", r=2, s=2)
        hid = pf.rearrange("p (m t) -> p m t", m=8)
        wf = work[:, :, :].rearrange("p a t -> p (a t)")
        score_sb = wf[:, 0:T]
        rest_sb = wf[:, T:2 * T]
        exp_sb = wf[:, 2 * T:3 * T]
        xT = work[:, 0:2, :]
        uT = work[:, 2:4, :]
        xf = xn[:, :, :].rearrange("p t c -> p (t c)")
        m_hi, m_lo = xf[0:4, 0:T], xf[0:4, T:2 * T]
        logT = xf[0:NX, 0:T]
        qT = xn[:, :, :].rearrange("p (k t) c -> p k (t c)", k=KC)
        g_tm = k_bd[:, :, :, :].rearrange("p k h s -> p (k h s)").rearrange("p (t c) -> p t c", t=NT)
        p_one = sb("p_one", [P, T])
        p_tm = [p_one[:, :], wf[:, 3 * T:4 * T]]
        p_tm3 = p_one[:, 0:NT * S2].rearrange("p (t s) -> p t s", t=NT)
        pT3 = p_tm[1]
        v3 = v_aug[:, 0, :, :].rearrange("p h d -> p (h d)")[:, 0:C]

        scratch = nc.dram_tensor("scratch", [2, 2, KC, P, T], F32, kind="Internal").ap()
        m_scratch = nc.dram_tensor("m_scratch", [2, 2, 4, T], F32, kind="Internal").ap()
        stack_src = scratch.rearrange("w s c (h d) t -> w s c d h t", d=HD)

        d_vecs = sem("d_vecs"); d_ctx = sem("d_ctx"); d_x = sem("d_x"); d_mask = sem("d_mask")
        d_ada = [sem(f"d_ada{i}") for i in range(3)]
        d_w = [sem(f"d_w{i}") for i in range(4)]
        d_anchor = sem("d_anchor")
        d_split = [sem("d_split0"), sem("d_split1")]; d_stack = [sem("d_stack0"), sem("d_stack1")]
        d_mput = [sem("d_mput0"), sem("d_mput1")]; d_mget = [sem("d_mget0"), sem("d_mget1")]
        d_out = sem("d_out")
        pool_chain = sem("pool_chain"); dve_chain = sem("dve_chain"); act_chain = sem("act_chain")
        apart_pe = sem("apart_pe"); apart_pool = sem("apart_pool"); apart_dve = sem("apart_dve"); apart_sp = sem("apart_sp")
        consts = sem("consts"); const_r = sem("const_r")
        vecs_ps = sem("vecs_ps"); vecs_ok = sem("vecs_ok"); cond_ok = sem("cond_ok")
        ctx_ps = sem("ctx_ps"); ctx_ok = sem("ctx_ok"); ctx_var = sem("ctx_var"); ctx_rstd = sem("ctx_rstd")
        ctx_n = sem("ctx_n")
        ada_ps = sem("ada_ps"); ada_ok = sem("ada_ok"); mask_ok = sem("mask_ok")
        so_zero = sem("so_zero")
        anc_ps = sem("anc_ps"); anc_ok = sem("anc_ok")
        d_rb = sem("d_rb")

        n_ln = (3, 3, 3, 1)
        now_ok = sig("now_ok", 1, 1, 1, 1)
        ln_var = sig("ln_var", *n_ln)
        ln_rstd = sig("ln_rstd", *n_ln)
        xn_ok = sig("xn_ok", *n_ln)
        ln_T = sig("ln_T", *(2 * n for n in n_ln))
        h_ok = sig("h_ok", *(2 * n for n in n_ln))
        diag_ok = sig("diag_ok", 3, 2, 2, 0)
        gate_ps = sig("gate_ps", 3, 2, 2, 0)
        gate_ok = sig("gate_ok", 3, 2, 2, 0)
        bg_ok = sig("bg_ok", 2, 1, 1, 0)
        qk_ps = sig("qk_ps", 4, 4, 4, 0)
        qk_hi = sig("qk_hi", 4, 4, 4, 0)
        qk_lo = sig("qk_lo", 4, 4, 4, 0)
        v_ps = sig("v_ps", 2, 2, 2, 0)
        v_ok = sig("v_ok", 2, 2, 2, 0)
        s_ps = sig("s_ps", *(NQ * u for u in UNITS), 0)
        s_max = sig("s_max", *(NQ * u for u in UNITS), 0)
        mT_ps = sig("mT_ps", NQ, NQ, NQ, 0)
        mT_hi = sig("mT_hi", NQ, NQ, NQ, 0)
        mT_lo = sig("mT_lo", NQ, NQ, NQ, 0)
        st_ps = sig("st_ps", *(NQ * 2 * k for k in KCH), 0)
        p_ok = sig("p_ok", *(NQ * 2 * k for k in KCH), 0)
        p_used = sig("p_used", *(NQ * k for k in KCH), 0, first=1)
        o_ok = sig("o_ok", NQ, NQ, NQ, 0)
        y_ps = sig("y_ps", 6, 6, 6, 0)
        y_ok = sig("y_ok", 3, 3, 3, 0, first=1)
        xb_ok = sig("xb_ok", 2, 2, 2, 0)
        ctx2_ok = sig("ctx2_ok", 1, 1, 1, 1)
        kx_ps = sig("kx_ps", 1, 1, 1, 1)
        kx_ok = sig("kx_ok", 1, 1, 1, 1)
        kbd_ok = sig("kbd_ok", 1, 1, 1, 0)
        vx_ps = sig("vx_ps", 1, 1, 1, 1, first=1)
        vx_ok = sig("vx_ok", 1, 1, 1, 1)
        qx_ps = sig("qx_ps", 2, 2, 2, 2)
        qx_ok = sig("qx_ok", 2, 2, 2, 2)
        sx_ps = sig("sx_ps", 8, 8, 8, 1)
        sx_sb = sig("sx_sb", 8, 0, 0, 0)
        sx_max = sig("sx_max", 8, 8, 8, 1)
        ex_ok = sig("ex_ok", 8, 8, 8, 1)
        px_tm = sig("px_tm", 8, 0, 0, 1)
        pxT_ps = sig("pxT_ps", 8, 8, 8, 1)
        px_ok = sig("px_ok", 8, 8, 8, 1)
        ox_ps = sig("ox_ps", 2, 2, 2, 0)
        ox_ok = sig("ox_ok", 2, 2, 2, 0, first=1)
        up_ps = sig("up_ps", 16, 8, 8, NX * RC + 2)
        act_ok = sig("act_ok", 8, 8, 8, NX * RC + 2)
        hid_ok = sig("hid_ok", 8, 0, 0, 0)
        ev_ps = sig("ev_ps", 0, 0, 0, 2); ev_ok = sig("ev_ok", 0, 0, 0, 2)
        rl_ps = sig("rl_ps", 0, 0, 0, 1); rl_ok = sig("rl_ok", 0, 0, 0, 1)
        rlT_ps = sig("rlT_ps", 0, 0, 0, 1); re_ok = sig("re_ok", 0, 0, 0, 1); rm_ok = sig("rm_ok", 0, 0, 0, 1)
        ex_out = sig("ex_out", 0, 0, 0, 2 * NX); acc_ok = sig("acc_ok", 0, 0, 0, 2 * NX)
        g_ps = sig("g_ps", 0, 0, 0, 2); gs_in = sig("gs_in", 0, 0, 0, 1); gs_ok = sig("gs_ok", 0, 0, 0, 1)
        rT_ps = sig("rT_ps", 0, 0, 0, 2); rT_ok = sig("rT_ok", 0, 0, 0, 2)
        f_ps = sig("f_ps", 0, 0, 0, 2); f_ok = sig("f_ok", 0, 0, 0, 1, first=1)

        n_w = [0, 0, 0, 0]
        blk = ctx.enter_context(nc.Block())

        def kxn(ap):
            return ap.rearrange("(k p) n -> p k n", p=P)

        LOADS = [
            [("qkv", kxn(a["L0_xcond_w_qkv"])), ("qx", kxn(a["L0_xcond_w_q"])), ("kvx", kxn(a["L0_xcond_w_kv"])),
             ("co", kxn(a["L0_xcond_w_co"])), ("m1", kxn(a["L0_xcond_w_m1"])), ("m2", kxn(a["L0_xcond_w_m2"]))],
            [("qkv", kxn(a["L1_xcond_W_qkv"])), ("qx", kxn(a["L1_xcond_W_qc"])), ("kvx", kxn(a["L1_xcond_W_kvc"])),
             ("co", kxn(a["L1_xcond_W_cproj"])), ("m1", kxn(a["L1_xcond_W_mlp1"])), ("m2", kxn(a["L1_xcond_W_mlp2"]))],
            [("qkv", kxn(a["L2_xcond_qkv_w"])), ("qx", kxn(a["L2_xcond_q_w"])), ("kvx", kxn(a["L2_xcond_kv_w"])),
             ("co", kxn(a["L2_xcond_ca_proj_w"])), ("m1", kxn(a["L2_xcond_fc1_w"])), ("m2", kxn(a["L2_xcond_fc2_w"]))],
            [("q", kxn(a["L3_xcond_Wq"])), ("k", kxn(a["L3_xcond_Wk"])), ("v", kxn(a["L3_xcond_Wv"])),
             ("g1", kxn(a["L3_xcond_gate_w1"][0:4 * P, :])), ("g2", kxn(a["L3_xcond_gate_w2"])),
             ("o", kxn(a["L3_xcond_out_w"])), ("r", kxn(a["L3_xcond_router_W"]))],
        ]
        SO = [a["L0_xcond_w_so"], a["L1_xcond_W_proj"], a["L2_xcond_sa_proj_w"]]
        BSO = [a["L0_xcond_b_so"], a["L1_xcond_b_proj"], a["L2_xcond_sa_proj_b"]]
        ROWS = [
            [("bv", a["L0_xcond_b_qkv"][2 * C:]), ("bvx", a["L0_xcond_b_kv"][C:]), ("bco", a["L0_xcond_b_co"]),
             ("bm2", a["L0_xcond_b_m2"])],
            [("bv", a["L1_xcond_b_qkv"][2 * C:]), ("bvx", a["L1_xcond_b_kvc"][C:]), ("bco", a["L1_xcond_b_cproj"]),
             ("bm2", a["L1_xcond_b_mlp2"])],
            [("bv", a["L2_xcond_qkv_b"][2 * C:]), ("bvx", a["L2_xcond_kv_b"][C:]), ("bco", a["L2_xcond_ca_proj_b"]),
             ("bm2", a["L2_xcond_fc2_b"])],
            [("gb2", a["L3_xcond_gate_b2"]), ("ob", a["L3_xcond_out_b"])],
        ]
        N_LOADS = [len(LOADS[L]) + 5 + len(ROWS[L]) for L in range(3)] + [len(LOADS[3]) + len(ROWS[3]) + 3 * NX]

        def load_layer(eng, L):
            for name, src in LOADS[L]:
                eng.dma_start(W[L][name], src).then_inc(d_w[L], 16)
            for name, src in ROWS[L]:
                eng.dma_start(W[L][name], src.partition_broadcast(P)).then_inc(d_w[L], 16)
            if L < 3:
                eng.wait_ge(so_zero, L + 1)
                so = SO[L].rearrange("(q j d) n -> j d q n", j=4, d=HD)
                for j in range(4):
                    eng.dma_start(W[L]["so"][32 * j:32 * j + HD, :, :], so[j]).then_inc(d_w[L], 16)
                eng.dma_start(W[L]["so"][HD:HD + 1, 0, :], BSO[L].rearrange("(a n) -> a n", a=1)).then_inc(d_w[L], 16)
            else:
                for e in range(NX):
                    eng.dma_start(W[3]["w1"][:, e, :, :], kxn(a["L3_xcond_e_w1"][e, 0:4 * P, :])).then_inc(d_w[3], 16)
                    eng.dma_start(W[3]["w2"][:, e, :, :], kxn(a["L3_xcond_e_w2"][e])).then_inc(d_w[3], 16)
                    eng.dma_start(W[3]["b2"][:, e, :], a["L3_xcond_e_b2"][e].partition_broadcast(P)).then_inc(d_w[3], 16)

        ADA_SRC = [a["L0_xcond_w_ada"], a["L1_xcond_W_mod"], a["L2_xcond_ada_w"]]
        FULL = slice(SHIFT, T - SHIFT)

        @blk.sync
        def _(sp):
            for name, (inp, at, n) in VECS.items():
                src = a[inp]
                if len(src.shape) == 2:
                    src = src.rearrange("b n -> (b n)")
                sp.dma_start(vec_rows[at:at + n, :], src[0:n * P].rearrange("(m p) -> m p", p=P)).then_inc(d_vecs, 16)
            for k in range(KC):
                sp.dma_start(ada_w[0][:, k, :], kxn(ADA_SRC[0])[:, k, :]).then_inc(d_ada[0], 16)
            sp.dma_start(ctx_tm[:, 0:2, :], a["ctx_1024"].rearrange("(g b) s c -> (b s) g c", g=2)).then_inc(d_ctx, 16)
            for b in range(NB):
                xv = x_all[:, b * NT * C:(b + 1) * NT * C].rearrange("p (t c) -> p t c", t=NT)
                sp.dma_start(xv[:, 0:NT - 1, :], a["x"][b, FULL, :].rearrange("(t p) c -> p t c", p=P)).then_inc(d_x, 16)
                sp.dma_start(xv[0:SHIFT, NT - 1, :], a["x"][b, T - SHIFT:, :]).then_inc(d_x, 16)
                sp.dma_start(xv[SHIFT:P, NT - 1, :], a["x"][b, 0:SHIFT, :]).then_inc(d_x, 16)
            sp.dma_start(mrow_words[:, :], a["mask_BxS2_bf0"].rearrange("(o b) s -> o (b s)", o=1)).then_inc(d_mask, 16)
            for L in (1, 2):
                sp.dma_start(ada_w[L], kxn(ADA_SRC[L])).then_inc(d_ada[L], 16)
            for L in range(3):
                if L == 0:
                    sp.wait_ge(const_r, 1)
                with sp.Fori(0, NB) as b:
                    for i in range(4):
                        sp.wait_ge(qk_hi.sem, qk_hi.at(L, b, i + 1))
                        sp.wait_ge(qk_lo.sem, qk_lo.at(L, b, i + 1))
                        if i < 2:
                            sp.wait_ge(p_used.sem, p_used.at(L, b, 0))
                        for s in range(2):
                            sp.dma_start(scratch[i % 2, s, i // 2], split[:, i % 2, s, :]).then_inc(d_split[i % 2], 16)
                    for s in range(2):
                        sp.wait_ge(d_split[s], b * 64 + (L * NB * 64 + 64))

                    def stack(g):
                        c, h0 = g // 2, 4 * (g % 2)
                        if g >= 2:
                            sp.wait_ge(p_used.sem, p_used.at(L, b, (g - 1) * KCH[L]))
                        sp.dma_start(q_stack[64:66, g % 2, :, :].bitcast(F32).rearrange("p h (a t) -> p (h a) t", a=2),
                                     zeros[64:66, :].unsqueeze(1).to_broadcast([2, 8, C])).then_inc(d_stack[g % 2], 16)
                        for r in range(4):
                            sp.dma_start(q_stack[16 * r:16 * r + 16, g % 2, :, :].bitcast(F32),
                                         stack_src[0, r % 2, c, :, h0:h0 + 4, :]).then_inc(d_stack[g % 2], 16)
                            sp.dma_start(k_stack[16 * r:16 * r + 16, g % 2, :, :].bitcast(F32),
                                         stack_src[1, r // 2, c, :, h0:h0 + 4, :]).then_inc(d_stack[g % 2], 16)

                    def maxima(g):
                        sp.wait_ge(mT_hi.sem, mT_hi.at(L, b, g + 1))
                        sp.wait_ge(mT_lo.sem, mT_lo.at(L, b, g + 1))
                        for s, src in enumerate((m_hi, m_lo)):
                            sp.dma_start(m_scratch[g % 2, s], src).then_inc(d_mput[g % 2], 16)
                        sp.wait_ge(d_mput[g % 2], b * 64 + (L * NB * 64 + 32 * (g // 2 + 1)))
                        sp.dma_start(q_stack[64:66, g % 2, :, :].bitcast(F32), m_scratch[g % 2]).then_inc(d_mget[g % 2], 16)

                    stack(0)
                    stack(1)
                    for g in range(NQ):
                        maxima(g)
                        if g + 2 < NQ:
                            stack(g + 2)
            with sp.Fori(0, NB) as b:
                sp.wait_ge(f_ok.sem, f_ok.at(3, b, 1))
                sp.sem_inc(apart_sp, 1)
                xv = x_all[:, bass.ds(b * (NT * C), NT * C)].rearrange("p (t c) -> p t c", t=NT)
                ob = out[bass.ds(b, 1), :, :].rearrange("o s c -> (o s) c")
                sp.dma_start(ob[FULL, :].rearrange("(t p) c -> p t c", p=P), xv[:, 0:NT - 1, :]).then_inc(d_out, 16)
                sp.dma_start(ob[T - SHIFT:T, :], xv[0:SHIFT, NT - 1, :]).then_inc(d_out, 16)
                sp.dma_start(ob[0:SHIFT, :], xv[SHIFT:P, NT - 1, :]).then_inc(d_out, 16)
            sp.wait_ge(d_out, 16 * 3 * NB)

        @blk.gpsimd
        def _(po):
            n = [0]

            def link(ins):
                n[0] += 1
                ins.then_inc(pool_chain, 1)
                po.wait_ge(pool_chain, n[0])

            def fresh():
                n[0] = 0
                po.sem_clear(pool_chain)

            def apart():
                po.sem_inc(apart_pool, 1)

            def band(t, groups, width, step, base):
                link(po.affine_select(out=t, in_=t, compare_op=ALU.is_ge, fill=0.0, base=base,
                                      pattern=[[-step, groups]], channel_multiplier=1))
                link(po.affine_select(out=t, in_=t, compare_op=ALU.is_ge, fill=0.0, base=width - 1 - base,
                                      pattern=[[step, groups]], channel_multiplier=-1))

            link(po.memset(ident[:, :], 1.0))
            link(po.affine_select(out=ident[:, :], in_=ident[:, :], compare_op=ALU.is_equal, fill=0.0, base=0,
                                  pattern=[[-1, P]], channel_multiplier=1))
            link(po.memset(ones[:, :], 1.0))
            link(po.memset(zeros[:, :], 0.0))
            po.memset(W[0]["so"], 0.0).then_inc(so_zero, 1)
            po.wait_ge(so_zero, 1)
            link(po.memset(head_mask[:, :], 1.0))
            band(head_mask[:, :], 8, HD, HD, 0)
            link(po.memset(ones_pair[:, :], 0.0))
            link(po.memset(ones_pair[0:S2, 0:HD], 1.0))
            link(po.memset(ones_pair[S2:P, HD:2 * HD], 1.0))
            link(po.memset(v_bd[:, :, :], 0.0))
            link(po.memset(half_neg[:, :], -0.5))
            link(po.memset(v_aug[:, :, :, HD:2 * HD], 1.0))
            po.sem_inc(consts, 1)
            po.wait_ge(ctx_var, 1)
            link(po.tensor_scalar(var_eps[:, 0:2], mv[:, 0:2, 1], EPS[1], None, ALU.add))
            po.tensor_tensor(rstd[:, 0:2], var_eps[:, 0:2], half_neg[:, 0:2], ALU.pow).then_inc(ctx_rstd, 1)
            fresh()
            po.wait_ge(ada_ps, 3)
            po.memset(W[1]["so"], 0.0).then_inc(so_zero, 1)

            for L in range(4):
                if L == 1:
                    po.wait_ge(so_zero, 2)
                    po.wait_ge(y_ps.sem, y_ps.end(0))
                    po.memset(W[2]["so"], 0.0).then_inc(so_zero, 1)
                    po.wait_ge(so_zero, 3)
                with po.Fori(0, NB) as b:
                    xv = x_all[:, bass.ds(b * (NT * C), NT * C)].rearrange("p (t c) -> p t c", t=NT)

                    def context():
                        po.wait_ge(vx_ps.sem, vx_ps.at(L, b, 0))
                        po.wait_ge(ctx_ok, 4)
                        for k in range(KC):
                            for h in range(2):
                                i = po.tensor_copy(ctx_two[:, k, h, :],
                                                   ctxT[:, 1 if L == 1 else 0, k, bass.ds(b * S2, S2)])
                                if 2 * k + h < 3:
                                    link(i)
                        i.then_inc(ctx2_ok.sem, 1)

                    def norm(j):
                        po.wait_ge(ln_var.sem, ln_var.at(L, b, j + 1))
                        apart()
                        link(po.tensor_scalar(var_eps[:, :], mv[:, :, 1], EPS[L], None, ALU.add))
                        po.tensor_tensor(rstd[:, :], var_eps[:, :], half_neg[:, :], ALU.pow).then_inc(ln_rstd.sem, 1)

                    def add_bias(j, blk_no):
                        po.wait_ge(xn_ok.sem, xn_ok.at(L, b, blk_no + 1))
                        apart()
                        if blk_no in GATES[L]:
                            row = bg_rows[:, blk_no - 1, :]
                        else:
                            row = W[L]["bco"]
                        i = po.tensor_tensor(xv, xv, row.unsqueeze(1).to_broadcast([P, NT, C]), ALU.add)
                        i.then_inc(xb_ok.sem, 1)

                    if L == 3:
                        context()
                        norm(0)
                    else:
                        if L < 3:
                            po.wait_ge(d_w[L], 16 * N_LOADS[L])
                        context()
                        norm(0)
                        j = 0
                        for g, blk_no in enumerate(GATES[L]):
                            if blk_no == 0:
                                continue
                            po.wait_ge(gate_ok.sem, gate_ok.at(L, b, g + 1))
                            row = W[L]["bco"] if blk_no == 1 else W[L]["bm2"]
                            po.tensor_tensor(bg_rows[:, blk_no - 1, :], row, gate_rows[:, blk_no, :], ALU.mult).then_inc(bg_ok.sem, 1)
                            j += 1
                            po.wait_ge(bg_ok.sem, bg_ok.at(L, b, j))
                        po.wait_ge(kx_ok.sem, kx_ok.at(L, b, 1))
                        for k in range(KC):
                            i = po.tensor_tensor(k_bd[:, k, :, :], kxT[:, k, :].unsqueeze(1).to_broadcast([P, 8, S2]),
                                                 head_mask[:, :].unsqueeze(2).to_broadcast([P, 8, S2]), ALU.mult)
                            if k == 0:
                                link(i)
                        i.then_inc(kbd_ok.sem, 1)
                        norm(1)
                        add_bias(0, 1)
                        norm(2)
                        add_bias(1, 2)
                    fresh()

        @blk.tensor
        def _(pe):
            mm = nc.tensor.matmul

            def wait(s, L, b, k):
                pe.wait_ge(s.sem, s.at(L, b, k))

            def apart():
                pe.sem_inc(apart_pe, 1)

            pe.sem_inc(p_used.sem, 1)
            pe.sem_inc(vx_ps.sem, 1)

            pe.wait_ge(consts, 1)
            pe.wait_ge(d_vecs, 16 * len(VECS))
            nc.tensor.transpose(bank[:, X, 0:NVEC], vec_rows[0:NVEC, :], ident[0:NVEC, 0:NVEC]).then_inc(vecs_ps, 1)

            pe.wait_ge(cond_ok, 1)
            for L in range(3):
                pe.wait_ge(d_ada[L], 16 * (KC if L == 0 else 1))
                for m in range(ADA[L]):
                    for k in range(KC):
                        i = mm(bank[:, B + L, m * NB:(m + 1) * NB], ada_w[L][:, k, m * P:(m + 1) * P], cond_s[:, k, :],
                               start=(k == 0), stop=(k == KC - 1))
                i.then_inc(ada_ps, 1)
            pe.wait_ge(d_ctx, 16)
            for v in range(2):
                if v == 1:
                    pe.wait_ge(ctx_n, 1)
                    pe.wait_ge(ctx_ok, 2)
                for k in range(KC):
                    for g in range(2):
                        i = nc.tensor.transpose(bank[:, A + k, g * P:(g + 1) * P], ctx_tm[:, 2 * v + g, k * P:(k + 1) * P], ident[:, :])
                    i.then_inc(ctx_ps, 1)

            def transposes(L, b, j):
                wait(xn_ok, L, b, j + 1)
                for k in range(KC):
                    for t in range(NT):
                        i = nc.tensor.transpose(bank[:, A + k, t * P:(t + 1) * P], xn[:, t, k * P:(k + 1) * P], ident[:, :])
                    i.then_inc(ln_T.sem, 1)

            def tm_out(L, b, lhs, rhs, kn, done):
                for t in range(NT):
                    for k in range(kn):
                        i = mm(bank[:, A + t // 2, (t % 2) * C:(t % 2 + 1) * C], lhs(k, t), rhs(k),
                               start=(k == 0), stop=(k == kn - 1))
                    if t % 2:
                        i.then_inc(done.sem, 1)

            for L in range(3):
                w = W[L]
                pe.wait_ge(d_w[L], 16 * N_LOADS[L])
                with pe.Fori(0, NB) as b:
                    for g, blk_no in enumerate(GATES[L]):
                        wait(diag_ok, L, b, g + 1)
                        if g == 0:
                            wait(ox_ok, L, b, 0)
                        else:
                            wait(gate_ok, L, b, g)
                        for k in range(KC):
                            i = mm(bank[:, X, k * P:(k + 1) * P], ones[:, :], diag[:, k, :], start=True, stop=True)
                        i.then_inc(gate_ps.sem, 1)
                    wait(ctx2_ok, L, b, 1)
                    wait(gate_ok, L, b, len(GATES[L]))
                    for m in range(KC):
                        for k in range(KC):
                            i = mm(bank[:, X, m * S2:(m + 1) * S2], w["kvx"][:, k, m * P:(m + 1) * P], ctx_two[:, k, 0, :],
                                   start=(k == 0), stop=(k == KC - 1))
                    i.then_inc(kx_ps.sem, 1)
                    wait(kx_ok, L, b, 1)
                    for k in range(KC):
                        i = mm(bank[:, X, 0:C], ctx_two[:, k, :, :], w["kvx"][:, k, C:2 * C], start=(k == 0), stop=(k == KC - 1))
                    i.then_inc(vx_ps.sem, 1)

                    wait(y_ok, L, b, 0)
                    transposes(L, b, 0)
                    wait(h_ok, L, b, 2)
                    for i4 in range(4):
                        m = (i4 % 2) * KC + i4 // 2
                        for k in range(KC):
                            i = mm(bank[:, B + i4, :], w["qkv"][:, k, m * P:(m + 1) * P], hT[:, k, :], start=(k == 0), stop=(k == KC - 1))
                        i.then_inc(qk_ps.sem, 1)
                    for t in range(NT):
                        for k in range(KC):
                            i = mm(bank[:, A + t // 2, (t % 2) * C:(t % 2 + 1) * C], hT[:, k, t * P:(t + 1) * P], w["qkv"][:, k, 2 * C:3 * C],
                                   start=(k == 0), stop=(k == KC - 1))
                        if t % 2:
                            i.then_inc(v_ps.sem, 1)

                    def scores(g):
                        s = g % 2
                        pe.wait_ge(d_stack[s], b * 288 + (L * NB * 288 + 144 * (g // 2 + 1)))
                        for u in range(UNITS[L]):
                            n = g * UNITS[L] + u
                            if g == 0 and u < 2:
                                wait(v_ok, L, b, u + 1)
                            else:
                                wait(s_max, L, b, n - 1)
                            if L == 0:
                                for j in range(4):
                                    cols = slice(u * P, (u + 1) * P)
                                    i = mm(bank[:, A + u % 2, j * P:(j + 1) * P], q_stack[0:66, s, j, cols], k_score[0:66, s, j, cols],
                                           start=True, stop=True)
                            else:
                                j, t = u // 4, u % 4
                                i = mm(bank[:, A + u % 2, :], q_stack[0:66, s, j, t * P:(t + 1) * P], k_stack[0:66, s, j, :],
                                       start=True, stop=True)
                            i.then_inc(s_ps.sem, 1)
                        wait(s_max, L, b, (g + 1) * UNITS[L])
                        if g > 0:
                            wait(mT_hi, L, b, g)
                            wait(mT_lo, L, b, g)
                        else:
                            wait(vx_ok, L, b, 1)
                        for t in range(NT):
                            i = nc.tensor.transpose(bank[0:4, X, t * P:(t + 1) * P], nm[:, t, 4 * g:4 * g + 4], ident[:, :])
                        i.then_inc(mT_ps.sem, 1)

                    k_score = k_stack

                    def weigh(g):
                        s = g % 2
                        pe.wait_ge(d_mget[s], b * 32 + (L * NB * 32 + 16 * (g // 2 + 1)))
                        n2 = 2 * KCH[L]

                        def key_scores(c):
                            for hp in range(2):
                                n = g * n2 + 2 * c + hp
                                if n < 2:
                                    wait(qk_lo, L, b, 4)
                                else:
                                    wait(p_ok, L, b, n - 1)
                                for j in (2 * hp, 2 * hp + 1):
                                    if L == 0:
                                        for u in range(NT):
                                            cols = slice(u * P, (u + 1) * P)
                                            i = mm(bank[:, B + j, cols], k_stack[0:66, s, j, cols], q_stack[0:66, s, j, cols],
                                                   start=True, stop=True)
                                    else:
                                        i = mm(bank[:, B + j, :], k_stack[0:66, s, j, c * P:(c + 1) * P], q_stack[0:66, s, j, :],
                                               start=True, stop=True)
                                i.then_inc(st_ps.sem, 1)

                        key_scores(0)
                        for c in range(KCH[L]):
                            if c + 1 < KCH[L]:
                                key_scores(c + 1)
                            wait(p_ok, L, b, g * n2 + 2 * c + 2)
                            n = g * KCH[L] + c
                            if c == 0 and g > 0:
                                wait(o_ok, L, b, g)
                            if L == 0:
                                for u in range(NT):
                                    for j in range(4):
                                        cols = slice(u * P, (u + 1) * P)
                                        i = mm(bank[32 * j:32 * j + 32, O, cols], v_aug[:, u, 4 * g + j, :], probs[:, n % 2, j, cols],
                                               start=True, stop=True)
                            else:
                                for j in range(4):
                                    i = mm(bank[32 * j:32 * j + 32, O, :], v_aug[:, c, 4 * g + j, :], probs[:, n % 2, j, :],
                                           start=(c == 0), stop=(c == KCH[L] - 1))
                            i.then_inc(p_used.sem, 1)

                    scores(0)
                    for g in range(NQ):
                        if g + 1 < NQ:
                            scores(g + 1)
                        weigh(g)
                    wait(o_ok, L, b, NQ)
                    wait(s_max, L, b, NQ * UNITS[L])
                    tm_out(L, b, lambda k, t: work[:, k, t * P:(t + 1) * P], lambda k: w["so"][:, k, :], NQ, y_ps)

                    transposes(L, b, 1)
                    wait(h_ok, L, b, 4)
                    for m in range(KC):
                        for k in range(KC):
                            i = mm(bank[:, B + m, :], w["qx"][:, k, m * P:(m + 1) * P], hT[:, k, :], start=(k == 0), stop=(k == KC - 1))
                        i.then_inc(qx_ps.sem, 1)
                    wait(qx_ok, L, b, 2)
                    wait(kbd_ok, L, b, 1)

                    def cross_scores(n):
                        t, k = n // KC, n % KC
                        if n >= 2:
                            wait(sx_sb if L == 0 else sx_max, L, b, n - 1)
                        i = mm(bank[:, A + n % 2, :], qT[:, k, t * P:(t + 1) * P], k_bd[:, k, :, :], start=True, stop=(L != 2))
                        if L == 2:
                            i = mm(bank[:, A + n % 2, :].rearrange("p (h s) -> p h s", h=8), one_row[:, :],
                                   mask_row[:, bass.ds(b, 1), :].to_broadcast([P, 8, S2]),
                                   start=False, stop=True)
                        i.then_inc(sx_ps.sem, 1)

                    cross_scores(0)
                    for n in range(NT * KC):
                        if n + 1 < NT * KC:
                            cross_scores(n + 1)
                        wait(px_tm if L == 0 else ex_ok, L, b, n + 1)
                        if n >= 2:
                            wait(px_ok, L, b, n - 1)
                        for r in range(4):
                            i = nc.tensor.transpose(bank[:, B + n % 2, r * P:(r + 1) * P], p_tm[n % 2][:, r * P:(r + 1) * P], ident[:, :])
                        i.then_inc(pxT_ps.sem, 1)
                    wait(px_ok, L, b, 8)
                    for c in range(KC):
                        if c > 0:
                            wait(ox_ok, L, b, c)
                        for r in range(4):
                            mm(bank[32 * r:32 * r + 32, O, :], v_bd[:, 4 * c + r, :], hid[:, 4 * c + r, :], start=True, stop=True)
                        for r in range(4):
                            i = mm(bank[32 * r:32 * r + 32, X, :], ones_pair[:, :], hid[:, 4 * c + r, :], start=True, stop=True)
                        i.then_inc(ox_ps.sem, 1)
                    wait(ox_ok, L, b, 2)
                    tm_out(L, b, lambda k, t: xT[:, k, t * P:(t + 1) * P], lambda k: w["co"][:, k, :], KC, y_ps)

                    transposes(L, b, 2)
                    wait(h_ok, L, b, 6)
                    for m in range(UP[L]):
                        mc = (m % 2) * HIDC + m // 2 if L == 0 else m
                        if m >= 4:
                            if L == 0:
                                wait(hid_ok, L, b, (m - 4) // 2 + 1)
                            else:
                                wait(act_ok, L, b, m - 3)
                        for k in range(KC):
                            i = mm(bank[:, B + m % 4, :], w["m1"][:, k, mc * P:(mc + 1) * P], hT[:, k, :], start=(k == 0), stop=(k == KC - 1))
                        i.then_inc(up_ps.sem, 1)
                    wait(hid_ok if L == 0 else act_ok, L, b, 8)
                    tm_out(L, b, lambda k, t: hid[:, k, t * P:(t + 1) * P], lambda k: w["m2"][:, k, :], HIDC, y_ps)

            L, w = 3, W[3]
            pe.wait_ge(d_w[3], 16 * N_LOADS[3])
            pe.wait_ge(d_anchor, 16 * (NX + 1))
            pe.wait_ge(y_ok.sem, y_ok.end(2))
            pe.wait_ge(act_chain, 1)
            for m in range(NX * RC + 2):
                for k in range(KC):
                    e = m // RC
                    lhs = g1_anchor[:, k, (m - NX * RC) * P:(m - NX * RC + 1) * P] if m >= NX * RC else w1_anchor[e][:, k, (m % RC) * P:(m % RC + 1) * P]
                    mm(bank[:, B, m * NB:(m + 1) * NB], lhs, cond_r[:, k, :], start=(k == 0), stop=(k == KC - 1))
            for k in range(KC):
                i = mm(bank[0:NX, B + 1, 0:NB], w["r"][:, 4 + k, :], cond_r[:, k, :], start=(k == 0), stop=(k == KC - 1))
            i.then_inc(anc_ps, 1)
            pe.wait_ge(anc_ok, 2)
            comb = lambda k: hT[:, k, :] if k < 2 else xT[:, k - 2, :]
            with pe.Fori(0, NB) as b:
                wait(ctx2_ok, L, b, 1)
                wait(f_ok, L, b, 0)
                for m in range(KC):
                    for k in range(KC):
                        i = mm(bank[:, X, m * S2:(m + 1) * S2], w["k"][:, k, m * P:(m + 1) * P], ctx_two[:, k, 0, :],
                               start=(k == 0), stop=(k == KC - 1))
                i.then_inc(kx_ps.sem, 1)
                wait(kx_ok, L, b, 1)
                for k in range(KC):
                    i = mm(bank[0:S2, X, 0:C], ctx_two[:, k, 0, :], w["v"][:, k, :], start=(k == 0), stop=(k == KC - 1))
                i.then_inc(vx_ps.sem, 1)
                transposes(L, b, 0)
                wait(h_ok, L, b, 2)
                for m in range(KC):
                    for k in range(KC):
                        i = mm(bank[:, B + m, :], w["q"][:, k, m * P:(m + 1) * P], hT[:, k, :], start=(k == 0), stop=(k == KC - 1))
                    i.then_inc(qx_ps.sem, 1)
                wait(qx_ok, L, b, 2)
                for t in range(NT):
                    for k in range(KC):
                        i = mm(bank[:, A, t * S2:(t + 1) * S2], qT[:, k, t * P:(t + 1) * P], kxT[:, k, :], start=(k == 0), stop=(k == KC - 1))
                i.then_inc(sx_ps.sem, 1)
                wait(px_tm, L, b, 1)
                wait(vx_ok, L, b, 1)
                apart()
                for t in range(NT):
                    i = nc.tensor.transpose(bank[0:S2, X, t * P:(t + 1) * P], p_tm3[:, t, :], ident[:, :])
                i.then_inc(pxT_ps.sem, 1)
                wait(px_ok, L, b, 1)
                for m in range(KC):
                    mm(bank[:, B + m, :], v3[0:S2, m * P:(m + 1) * P], pT3[0:S2, :], start=True, stop=True).then_inc(ev_ps.sem, 1)
                wait(ev_ok, L, b, 2)
                for k in range(4):
                    i = mm(bank[0:NX, X, :], w["r"][:, k, :], comb(k), start=(k == 0), stop=(k == 3))
                i.then_inc(rl_ps.sem, 1)

                def hidden(m):
                    if m >= 4:
                        wait(act_ok, L, b, m - 3)
                    for k in range(4):
                        lhs = w["w1"][:, m // RC, k, (m % RC) * P:(m % RC + 1) * P] if m < NX * RC else w["g1"][:, k, (m - NX * RC) * P:(m - NX * RC + 1) * P]
                        i = mm(bank[:, B + m % 4, :], lhs, comb(k), start=(k == 0), stop=(k == 3))
                    i.then_inc(up_ps.sem, 1)

                def expert(e):
                    wait(act_ok, L, b, RC * (e + 1))
                    for t in range(NT):
                        if t % 2 == 0 and e > 0:
                            wait(acc_ok, L, b, 2 * (e - 1) + t // 2 + 1)
                        for k in range(RC):
                            i = mm(bank[:, A + t // 2, (t % 2) * C:(t % 2 + 1) * C], hid[:, (e % 2) * RC + k, t * P:(t + 1) * P], w["w2"][:, e, k, :],
                                   start=(k == 0), stop=(k == RC - 1))
                        if t % 2:
                            i.then_inc(ex_out.sem, 1)

                for m in range(RC):
                    hidden(m)
                wait(rl_ok, L, b, 1)
                apart()
                for t in range(NT):
                    i = nc.tensor.transpose(bank[:, X, t * NX:(t + 1) * NX], logT[:, t * P:(t + 1) * P], ident[0:NX, 0:NX])
                i.then_inc(rlT_ps.sem, 1)
                for e in range(NX):
                    if e + 1 < NX:
                        for m in range(RC):
                            hidden(RC * (e + 1) + m)
                    else:
                        hidden(NX * RC)
                        hidden(NX * RC + 1)
                    expert(e)
                wait(acc_ok, L, b, 2 * NX)
                wait(act_ok, L, b, NX * RC + 2)
                tm_out(L, b, lambda k, t: uT[:, k, t * P:(t + 1) * P], lambda k: w["g2"][:, k, :], KC, g_ps)
                for k in range(KC):
                    for t in range(NT):
                        i = nc.tensor.transpose(bank[:, B + k, t * P:(t + 1) * P], xn[:, t, k * P:(k + 1) * P], ident[:, :])
                    i.then_inc(rT_ps.sem, 1)
                wait(rT_ok, L, b, 2)
                wait(gs_in, L, b, 1)
                tm_out(L, b, lambda k, t: hT[:, k, t * P:(t + 1) * P], lambda k: w["o"][:, k, :], KC, f_ps)

        @blk.scalar
        def _(ac):
            act = nc.scalar.activation

            def wait(s, L, b, k):
                ac.wait_ge(s.sem, s.at(L, b, k))

            load_layer(ac, 0)
            ac.wait_ge(vecs_ps, 1)
            nc.scalar.copy(vecs[:, :], bank[:, X, 0:NVEC]).then_inc(vecs_ok, 1)
            ac.wait_ge(vecs_ok, 1)
            cv = VECS["cond"][1]
            cond_cols = vecs[:, cv:cv + NB * KC].rearrange("p (b k) -> p k b", b=NB)
            act(cond_s[:, :, :], cond_cols, ACT.Silu).then_inc(cond_ok, 1)
            act(cond_r[:, :, :], cond_cols, ACT.Copy).then_inc(act_chain, 1)
            for n in range(4):
                ac.wait_ge(ctx_ps, n + 1)
                nc.scalar.copy(ctxT[:, n // 2, n % 2, :], bank[:, A + n % 2, 0:NB * S2]).then_inc(ctx_ok, 1)
            ac.wait_ge(ada_ps, 3)
            load_layer(ac, 1)

            def to_feature(L, b, j):
                for k in range(KC):
                    wait(ln_T, L, b, 2 * j + k + 1)
                    if L == 3:
                        g, be = VECS["gamma"][1] + k, VECS["beta"][1] + k
                        s, o = vecs[:, g:g + 1], vecs[:, be:be + 1]
                    elif SCALE_OF[L][j] is None:
                        s, o = 1.0, 0.0
                    else:
                        if j == 0 and k == 0:
                            wait(now_ok, L, b, 1)
                        sc, sh = SCALE_OF[L][j] + k, SHIFT_OF[L][j] + k
                        s, o = mod_now[:, sc:sc + 1], mod_now[:, sh:sh + 1]
                    act(hT[:, k, :], bank[:, A + k, :], ACT.Identity, bias=o, scale=s).then_inc(h_ok.sem, 1)

            for L in range(3):
                if L == 1:
                    ac.wait_ge(y_ps.sem, y_ps.end(0))
                    load_layer(ac, 2)
                if L == 2:
                    ac.wait_ge(y_ps.sem, y_ps.end(1))
                    load_layer(ac, 3)
                with ac.Fori(0, NB) as b:
                    for g, blk_no in enumerate(GATES[L]):
                        wait(gate_ps, L, b, g + 1)
                        nc.scalar.copy(gate_rows[:, blk_no, :], bank[:, X, 0:C]).then_inc(gate_ok.sem, 1)
                    wait(kx_ps, L, b, 1)
                    kv = VECS[f"kx{L}"][1]
                    for m in range(KC):
                        i = act(kxT[:, m, :], bank[:, X, m * S2:(m + 1) * S2], ACT.Identity, bias=vecs[:, kv + m:kv + m + 1])
                    i.then_inc(kx_ok.sem, 1)
                    to_feature(L, b, 0)
                    qv = VECS[f"qk{L}"][1]
                    for i4 in range(4):
                        wait(qk_ps, L, b, i4 + 1)
                        if i4 >= 2:
                            ac.wait_ge(d_split[i4 % 2], b * 64 + (L * NB * 64 + 32))
                        m = qv + (i4 % 2) * KC + i4 // 2
                        act(split[:, i4 % 2, 0, :].bitcast(F32R), bank[:, B + i4, :], ACT.Identity, bias=vecs[:, m:m + 1]).then_inc(qk_hi.sem, 1)
                    for s in range(2):
                        ac.wait_ge(d_split[s], b * 64 + (L * NB * 64 + 64))

                    def max_high(g):
                        wait(mT_ps, L, b, g + 1)
                        if g > 0:
                            s = (g - 1) % 2
                            ac.wait_ge(d_mput[s], b * 64 + (L * NB * 64 + 32 * ((g - 1) // 2 + 1)))
                        nc.scalar.copy(m_hi.bitcast(F32R), bank[0:4, X, :]).then_inc(mT_hi.sem, 1)

                    max_high(0)
                    for g in range(NQ):
                        if g + 1 < NQ:
                            max_high(g + 1)
                        for c in range(KCH[L]):
                            n = g * KCH[L] + c
                            for hp in range(2):
                                wait(st_ps, L, b, 2 * n + hp + 1)
                                if n >= 2 and hp == 0:
                                    wait(p_used, L, b, n - 1)
                                act(probs[:, n % 2, 2 * hp:2 * hp + 2, :], bank[:, B + 2 * hp:B + 2 * hp + 2, :], ACT.Exp, scale=SCALE).then_inc(p_ok.sem, 1)
                    to_feature(L, b, 1)
                    qv = VECS[f"qx{L}"][1]
                    for m in range(KC):
                        wait(qx_ps, L, b, m + 1)
                        act(qT[:, m, :], bank[:, B + m, :], ACT.Identity, bias=vecs[:, qv + m:qv + m + 1]).then_inc(qx_ok.sem, 1)
                    def probs_T(n):
                        t, c = n // KC, n % KC
                        wait(pxT_ps, L, b, n + 1)
                        i = nc.scalar.copy(hid[:, 4 * c:4 * c + 4, t * P:(t + 1) * P],
                                           bank[:, B + n % 2, :].rearrange("p (r t) -> p r t", r=4))
                        i.then_inc(px_ok.sem, 1)

                    for n in range(NT * KC):
                        if L == 0:
                            wait(sx_ps, L, b, n + 1)
                            if n > 0:
                                wait(sx_max, L, b, n)
                            nc.scalar.copy(score_sb, bank[:, A + n % 2, :]).then_inc(sx_sb.sem, 1)
                        wait(sx_max, L, b, n + 1)
                        e = exp_sb if L == 0 else p_tm[n % 2]
                        act(e, e, ACT.Exp, scale=SCALE).then_inc(ex_ok.sem, 1)
                        if n > 0:
                            probs_T(n - 1)
                    probs_T(NT * KC - 1)
                    to_feature(L, b, 2)
                    mv_ = VECS[f"m1{L}"][1]
                    fn = [ACT.Silu, ACT.Gelu_apprx_tanh, ACT.Gelu][L]
                    for m in range(HIDC):
                        at = 2 * m if L == 0 else m
                        wait(up_ps, L, b, at + 1)
                        if m == 0:
                            wait(ox_ps, L, b, 2)
                        act(hid[:, m, :], bank[:, B + at % 4, :], fn, bias=vecs[:, mv_ + m:mv_ + m + 1]).then_inc(act_ok.sem, 1)
            L = 3
            ac.dma_start(router_in[:, :], a["L3_xcond_router_b"].rearrange("(e o) -> e o", o=1), allow_slow_non_contiguous=True).then_inc(d_rb, 16)
            ac.wait_ge(y_ps.sem, y_ps.end(2))
            for e in range(NX):
                ac.dma_start(w1_anchor[e], kxn(a["L3_xcond_e_w1"][e, 4 * P:6 * P, :])).then_inc(d_anchor, 16)
            ac.dma_start(g1_anchor, kxn(a["L3_xcond_gate_w1"][4 * P:6 * P, :])).then_inc(d_anchor, 16)
            with ac.Fori(0, NB) as b:
                wait(kx_ps, L, b, 1)
                nc.scalar.copy(kxT[:, :, :], bank[:, X, 0:KC * S2].rearrange("p (k s) -> p k s", k=KC)).then_inc(kx_ok.sem, 1)
                to_feature(L, b, 0)
                for m in range(KC):
                    wait(qx_ps, L, b, m + 1)
                    nc.scalar.copy(qT[:, m, :], bank[:, B + m, :]).then_inc(qx_ok.sem, 1)
                wait(sx_max, L, b, 1)
                for t in range(NT):
                    i = act(p_tm3[:, t, :], bank[:, A, t * S2:(t + 1) * S2], ACT.Exp, bias=sm[:, 1, t:t + 1], scale=float(C) ** -0.5,
                            accum_out=sm[:, 2, t:t + 1])
                i.then_inc(ex_ok.sem, 1)
                wait(pxT_ps, L, b, 1)
                nc.scalar.copy(pT3[0:S2, :], bank[0:S2, X, :]).then_inc(px_ok.sem, 1)
                for m in range(KC):
                    wait(ev_ps, L, b, m + 1)
                    nc.scalar.copy(xT[:, m, :], bank[:, B + m, :]).then_inc(ev_ok.sem, 1)
                wait(rl_ps, L, b, 1)
                act(logT, bank[0:NX, X, :], ACT.Identity, bias=router_now[:, :]).then_inc(rl_ok.sem, 1)
                wait(rm_ok, L, b, 1)
                act(pr[:, :, :], lg[:, :, :], ACT.Exp).then_inc(re_ok.sem, 1)
                for m in range(NX * RC + 2):
                    wait(up_ps, L, b, m + 1)
                    if m < NX * RC:
                        e = m // RC
                        if e >= 2 and m % RC == 0:
                            wait(ex_out, L, b, 2 * (e - 1))
                        dst = hid[:, (e % 2) * RC + m % RC, :]
                    else:
                        dst = uT[:, m - NX * RC, :]
                    act(dst, bank[:, B + m % 4, :], ACT.Silu, bias=anchor_now[:, m:m + 1]).then_inc(act_ok.sem, 1)
                for k in range(KC):
                    wait(rT_ps, L, b, k + 1)
                    nc.scalar.copy(hT[:, k, :], bank[:, B + k, :]).then_inc(rT_ok.sem, 1)
                wait(gs_in, L, b, 1)
                act(g_tm, g_tm, ACT.Sigmoid).then_inc(gs_ok.sem, 1)

        @blk.vector
        def _(dv):
            n = [0]
            V = nc.vector

            def link(ins):
                n[0] += 1
                ins.then_inc(dve_chain, 1)
                dv.wait_ge(dve_chain, n[0])

            def fresh():
                n[0] = 0
                dv.sem_clear(dve_chain)

            def wait(s, L, b, k):
                dv.wait_ge(s.sem, s.at(L, b, k))

            def apart():
                dv.sem_inc(apart_dve, 1)

            dv.sem_inc(ox_ok.sem, 1)
            dv.sem_inc(y_ok.sem, 1)
            dv.sem_inc(f_ok.sem, 1)
            dv.wait_ge(consts, 1)
            for s in range(2):
                link(V.tensor_scalar(k_stack[64:P, s, :, :].rearrange("p h (a t) -> p (h a) t", a=2), zeros[64:P, :].unsqueeze(1).to_broadcast([64, 8, C]), 1.0, None, ALU.add))
            link(V.tensor_scalar(one_row[:, :], zeros[:, 0:P], ident[:, 0:1], None, ALU.add))
            dv.wait_ge(d_mask, 16)
            link(V.tensor_copy(mask_row[:, :, :], zeros[:, 0:NB * S2].rearrange("p (b s) -> p b s", b=NB)))
            link(V.tensor_scalar(mask_row[0:1, :, :], mrow_words[:, :].bitcast(U8).rearrange("p (b s) -> p b s", b=NB), MASKED, None, ALU.mult))
            V.memset(sm[:, :, :], 0.0).then_inc(const_r, 1)
            dv.wait_ge(d_ctx, 16)
            for g in range(2):
                link(V.bn_stats(stats[:, g, :], ctx_tm[:, g, :]))
            link(V.bn_aggr(mv[:, 0, :], stats[:, 0, :]))
            V.bn_aggr(mv[:, 1, :], stats[:, 1, :]).then_inc(ctx_var, 1)
            dv.wait_ge(ctx_rstd, 1)
            for g in range(2):
                i = V.tensor_scalar(ctx_tm[:, 2 + g, :], ctx_tm[:, g, :], mv[:, g, 0:1], rstd[:, g:g + 1], ALU.subtract, ALU.mult)
                if g == 0:
                    link(i)
            i.then_inc(ctx_n, 1)
            dv.wait_ge(vecs_ok, 1)
            for L in range(3):
                dv.wait_ge(ada_ps, L + 1)
                av = VECS[f"ada{L}"][1]
                ms = mod[:, ADA_AT[L]:ADA_AT[L] + ADA[L], :]
                link(V.tensor_tensor(ms, bank[:, B + L, 0:ADA[L] * NB].rearrange("p (m b) -> p m b", b=NB),
                                     vecs[:, av:av + ADA[L]].unsqueeze(2).to_broadcast([P, ADA[L], NB]), ALU.add))
                for j in range(3):
                    if SCALE_OF[L][j] is not None:
                        sc = ADA_AT[L] + SCALE_OF[L][j]
                        link(V.tensor_scalar(mod[:, sc:sc + KC, :], mod[:, sc:sc + KC, :], 1.0, None, ALU.add))
            dv.wait_ge(ctx_ok, 4)
            dv.wait_ge(d_x, 16 * 3 * NB)

            def norm(L, b, j, xv):
                for t in range(NT):
                    V.bn_stats(stats[:, t, :], xv[:, t, :]).then_inc(dve_chain, 1)
                n[0] += NT
                dv.wait_ge(dve_chain, n[0])
                for t in range(NT):
                    i = V.bn_aggr(mv[:, t, :], stats[:, t, :])
                    if t + 1 < NT:
                        i.then_inc(dve_chain, 1)
                n[0] += NT - 1
                i.then_inc(ln_var.sem, 1)
                wait(ln_rstd, L, b, j + 1)
                for t in range(NT):
                    i = V.tensor_scalar(xn[:, t, :], xv[:, t, :], mv[:, t, 0:1], rstd[:, t:t + 1], ALU.subtract, ALU.mult)
                i.then_inc(xn_ok.sem, 1)

            def residual(L, b, j, xv):
                if j > 0:
                    wait(xb_ok, L, b, j)
                for h in range(2):
                    wait(y_ps, L, b, 2 * j + h + 1)
                    ps = bank[:, A + h, :].rearrange("p (t c) -> p t c", t=2)
                    if j in GATES[L]:
                        link(V.tensor_tensor(ps, ps, gate_rows[:, j, :].unsqueeze(1).to_broadcast([P, 2, C]), ALU.mult))
                    link(V.tensor_tensor(xv[:, 2 * h:2 * h + 2, :], ps, xv[:, 2 * h:2 * h + 2, :], ALU.add))
                dv.sem_inc(y_ok.sem, 1)

            for L in range(3):
                w = W[L]
                dv.wait_ge(d_w[L], 16 * N_LOADS[L])
                fresh()
                with dv.Fori(0, NB) as b:
                    xv = x_all[:, bass.ds(b * (NT * C), NT * C)].rearrange("p (t c) -> p t c", t=NT)
                    V.tensor_copy(mod_now[:, 0:ADA[L]], mod[:, ADA_AT[L]:ADA_AT[L] + ADA[L], bass.ds(b, 1)].rearrange("p m o -> p (m o)")).then_inc(now_ok.sem, 1)
                    wait(now_ok, L, b, 1)
                    for g, blk_no in enumerate(GATES[L]):
                        gc = GATE_OF[L][blk_no]
                        if g > 0:
                            wait(gate_ps, L, b, g)
                        link(V.tensor_scalar(diag[:, 0, :], ident[:, :], mod_now[:, gc:gc + 1], None, ALU.mult))
                        V.tensor_scalar(diag[:, 1, :], ident[:, :], mod_now[:, gc + 1:gc + 2], None, ALU.mult).then_inc(diag_ok.sem, 1)
                    norm(L, b, 0, xv)
                    wait(vx_ps, L, b, 1)
                    for h in range(2):
                        ps = bank[h * S2:(h + 1) * S2, X, 0:C].rearrange("p (r e d) -> p r e d", e=2, d=HD)[:, :, h, :]
                        bv = w["bvx"].rearrange("p (r e d) -> p r e d", e=2, d=HD)[h * S2:(h + 1) * S2, :, h, :]
                        i = V.tensor_tensor(v_bd[h * S2:(h + 1) * S2, :, h * HD:(h + 1) * HD], ps, bv, ALU.add)
                        if h == 0:
                            link(i)
                    i.then_inc(vx_ok.sem, 1)
                    qv = VECS[f"qk{L}"][1]
                    for i4 in range(4):
                        wait(qk_hi, L, b, i4 + 1)
                        m = qv + (i4 % 2) * KC + i4 // 2
                        V.scalar_tensor_tensor(out=split[:, i4 % 2, 1, :].bitcast(F32R), in0=bank[:, B + i4, :], scalar=vecs[:, m:m + 1],
                                               in1=split[:, i4 % 2, 0, :], op0=ALU.add, op1=ALU.subtract).then_inc(qk_lo.sem, 1)
                    for h in range(2):
                        wait(v_ps, L, b, h + 1)
                        for t in range(2):
                            i = V.tensor_tensor(v_aug[:, 2 * h + t, :, 0:HD],
                                                bank[:, A + h, t * C:(t + 1) * C].rearrange("p (h d) -> p h d", d=HD),
                                                w["bv"].rearrange("p (h d) -> p h d", d=HD), ALU.add)
                            if t == 0:
                                link(i)
                        i.then_inc(v_ok.sem, 1)

                    def maxima(g):
                        for u in range(UNITS[L]):
                            wait(s_ps, L, b, g * UNITS[L] + u + 1)
                            if L == 0:
                                i = V.tensor_reduce(nm[:, u, 4 * g:4 * g + 4], bank[:, A + u % 2, :].rearrange("p (h s) -> p h s", h=4),
                                                    AX.X, ALU.max, negate=True)
                            else:
                                h, t = 4 * g + u // 4, u % 4
                                i = V.tensor_reduce(nm[:, t, h:h + 1], bank[:, A + u % 2, :], AX.X, ALU.max, negate=True)
                            i.then_inc(s_max.sem, 1)
                        wait(mT_hi, L, b, g + 1)
                        if g > 0:
                            s = (g - 1) % 2
                            dv.wait_ge(d_mput[s], b * 64 + (L * NB * 64 + 32 * ((g - 1) // 2 + 1)))
                        V.tensor_tensor(m_lo.bitcast(F32R), bank[0:4, X, :], m_hi, ALU.subtract).then_inc(mT_lo.sem, 1)

                    def heads(g):
                        wait(p_used, L, b, (g + 1) * KCH[L])
                        apart()
                        link(V.stream_shuffle(p_tm[0], bank[:, O, :], [HD + i % HD for i in range(32)]))
                        link(V.reciprocal(p_tm[0], p_tm[0]))
                        V.tensor_tensor(work[:, g, :], bank[:, O, :], p_tm[0], ALU.mult).then_inc(o_ok.sem, 1)

                    maxima(0)
                    for g in range(NQ):
                        if g + 1 < NQ:
                            maxima(g + 1)
                        heads(g)
                    residual(L, b, 0, xv)
                    norm(L, b, 1, xv)
                    if L == 0:
                        for t in range(NT):
                            for c in range(KC):
                                m = t * KC + c
                                wait(sx_sb, L, b, m + 1)
                                sc = score_sb.rearrange("p (h s) -> p h s", h=8)
                                rs = rest_sb.rearrange("p (h s) -> p h s", h=8)
                                if m > 0:
                                    wait(px_tm, L, b, m)
                                apart()
                                for step in range(4):
                                    for h in range(8):
                                        if step == 0:
                                            i = V.max(top[:, h, 0, :], sc[:, h, :])
                                        elif step == 1:
                                            i = V.match_replace(rs[:, h, :], top[:, h, 0, :], sc[:, h, :], -LARGE)
                                        elif step == 2:
                                            i = V.max(top[:, h, 1, :], rs[:, h, :])
                                        else:
                                            i = V.match_replace(rs[:, h, :], top[:, h, 1, :], rs[:, h, :], -LARGE)
                                        i.then_inc(dve_chain, 1)
                                    n[0] += 8
                                    dv.wait_ge(dve_chain, n[0])
                                V.tensor_tensor(exp_sb.rearrange("p (h s) -> p h s", h=8), sc,
                                                top[:, :, 0, 0:1].to_broadcast([P, 8, S2]), ALU.subtract).then_inc(sx_max.sem, 1)
                                wait(ex_ok, L, b, m + 1)
                                if m >= 2:
                                    wait(pxT_ps, L, b, m - 1)
                                V.scalar_tensor_tensor(out=p_tm[m % 2], in0=rest_sb, scalar=-LARGE, in1=exp_sb,
                                                       op0=ALU.is_equal, op1=ALU.mult).then_inc(px_tm.sem, 1)
                    else:
                        for m in range(8):
                            wait(sx_ps, L, b, m + 1)
                            ps = bank[:, A + m % 2, :].rearrange("p (h s) -> p h s", h=8)
                            mx = nm[:, m // KC, 8 * (m % KC):8 * (m % KC) + 8]
                            link(V.tensor_reduce(mx, ps, AX.X, ALU.max, negate=True))
                            if m >= 2:
                                wait(pxT_ps, L, b, m - 1)
                            V.tensor_tensor(p_tm[m % 2].rearrange("p (h s) -> p h s", h=8), ps,
                                            mx.unsqueeze(2).to_broadcast([P, 8, S2]), ALU.add).then_inc(sx_max.sem, 1)
                    for c in range(KC):
                        wait(ox_ps, L, b, c + 1)
                        link(V.reciprocal(p_tm[0], bank[:, X, :]))
                        V.tensor_tensor(xT[:, c, :], bank[:, O, :], p_tm[0], ALU.mult).then_inc(ox_ok.sem, 1)
                    residual(L, b, 1, xv)
                    norm(L, b, 2, xv)
                    if L == 0:
                        mv_ = VECS["m10"][1] + HIDC
                        for m in range(HIDC):
                            wait(up_ps, L, b, 2 * m + 2)
                            wait(act_ok, L, b, m + 1)
                            V.scalar_tensor_tensor(out=hid[:, m, :], in0=bank[:, B + (2 * m + 1) % 4, :], scalar=vecs[:, mv_ + m:mv_ + m + 1],
                                                   in1=hid[:, m, :], op0=ALU.add, op1=ALU.mult).then_inc(hid_ok.sem, 1)
                    residual(L, b, 2, xv)
                    fresh()

            L, w = 3, W[3]
            dv.wait_ge(d_w[3], 16 * N_LOADS[3])
            dv.wait_ge(anc_ps, 1)
            ev = VECS["eb1"][1]
            V.tensor_tensor(anchor_b[:, 0:NX * RC, :], bank[:, B, 0:NX * RC * NB].rearrange("p (m b) -> p m b", b=NB),
                            vecs[:, ev:ev + NX * RC].unsqueeze(2).to_broadcast([P, NX * RC, NB]), ALU.add).then_inc(dve_chain, 1)
            gv = VECS["gb1"][1]
            V.tensor_tensor(anchor_b[:, NX * RC:, :], bank[:, B, NX * RC * NB:(NX * RC + 2) * NB].rearrange("p (m b) -> p m b", b=NB),
                            vecs[:, gv:gv + 2].unsqueeze(2).to_broadcast([P, 2, NB]), ALU.add).then_inc(anc_ok, 1)
            V.tensor_copy(router_b[:, :], bank[0:NX, B + 1, 0:NB]).then_inc(anc_ok, 1)
            dv.wait_ge(anc_ok, 2)
            dv.wait_ge(dve_chain, 1)
            dv.wait_ge(d_rb, 16)
            n[0] = 1
            link(V.tensor_scalar(router_b[:, :], router_b[:, :], router_in[:, :], None, ALU.add))
            fresh()
            with dv.Fori(0, NB) as b:
                xv = x_all[:, bass.ds(b * (NT * C), NT * C)].rearrange("p (t c) -> p t c", t=NT)
                link(V.tensor_copy(anchor_now[:, :], anchor_b[:, :, bass.ds(b, 1)].rearrange("p m o -> p (m o)")))
                V.tensor_copy(router_now[:, :], router_b[:, bass.ds(b, 1)]).then_inc(now_ok.sem, 1)
                norm(L, b, 0, xv)
                wait(vx_ps, L, b, 1)
                V.tensor_copy(v3[0:S2, :], bank[0:S2, X, 0:C]).then_inc(vx_ok.sem, 1)
                wait(sx_ps, L, b, 1)
                link(V.tensor_reduce(sm[:, 0, :], bank[:, A, 0:NT * S2].rearrange("p (t s) -> p t s", t=NT), AX.X, ALU.max, negate=True))
                V.tensor_scalar(sm[:, 1, :], sm[:, 0, :], float(C) ** -0.5, None, ALU.mult).then_inc(sx_max.sem, 1)
                wait(ex_ok, L, b, 1)
                link(V.reciprocal(sm[:, 3, :], sm[:, 2, :]))
                V.tensor_tensor(p_tm3, p_tm3, sm[:, 3, :].unsqueeze(2).to_broadcast([P, NT, S2]), ALU.mult).then_inc(px_tm.sem, 1)
                wait(rlT_ps, L, b, 1)
                link(V.tensor_copy(lg[:, :, :], bank[:, X, 0:NT * NX].rearrange("p (t e) -> p t e", t=NT)))
                link(V.tensor_reduce(sm[:, 4, :], lg[:, :, :], AX.X, ALU.max))
                V.tensor_tensor(lg[:, :, :], lg[:, :, :], sm[:, 4, :].unsqueeze(2).to_broadcast([P, NT, NX]), ALU.subtract).then_inc(rm_ok.sem, 1)
                wait(re_ok, L, b, 1)
                link(V.tensor_reduce(sm[:, 5, :], pr[:, :, :], AX.X, ALU.add))
                link(V.reciprocal(sm[:, 5, :], sm[:, 5, :]))
                link(V.tensor_tensor(pr[:, :, :], pr[:, :, :], sm[:, 5, :].unsqueeze(2).to_broadcast([P, NT, NX]), ALU.mult))
                for e in range(NX):
                    for t in range(NT):
                        if e == 0:
                            V.tensor_scalar(xn[:, t, :], w["b2"][:, 0, :], pr[:, t, 0:1], None, ALU.mult).then_inc(dve_chain, 1)
                        else:
                            V.scalar_tensor_tensor(out=xn[:, t, :], in0=w["b2"][:, e, :], scalar=pr[:, t, e:e + 1], in1=xn[:, t, :],
                                                   op0=ALU.mult, op1=ALU.add).then_inc(dve_chain, 1)
                    n[0] += NT
                    dv.wait_ge(dve_chain, n[0])
                for e in range(NX):
                    for h in range(2):
                        wait(ex_out, L, b, 2 * e + h + 1)
                        if e > 0:
                            wait(acc_ok, L, b, 2 * (e - 1) + h + 1)
                        for t in (2 * h, 2 * h + 1):
                            i = V.scalar_tensor_tensor(out=xn[:, t, :], in0=bank[:, A + h, (t % 2) * C:(t % 2 + 1) * C], scalar=pr[:, t, e:e + 1],
                                                       in1=xn[:, t, :], op0=ALU.mult, op1=ALU.add)
                            if t % 2 == 0:
                                link(i)
                        i.then_inc(acc_ok.sem, 1)
                for h in range(2):
                    wait(g_ps, L, b, h + 1)
                    i = V.tensor_tensor(g_tm[:, 2 * h:2 * h + 2, :], bank[:, A + h, :].rearrange("p (t c) -> p t c", t=2),
                                        w["gb2"].unsqueeze(1).to_broadcast([P, 2, C]), ALU.add)
                    if h == 0:
                        link(i)
                i.then_inc(gs_in.sem, 1)
                wait(gs_ok, L, b, 1)
                for h in range(2):
                    wait(f_ps, L, b, h + 1)
                    ps = bank[:, A + h, :].rearrange("p (t c) -> p t c", t=2)
                    xh = xv[:, 2 * h:2 * h + 2, :]
                    link(V.tensor_tensor(ps, ps, w["ob"].unsqueeze(1).to_broadcast([P, 2, C]), ALU.add))
                    link(V.tensor_tensor(ps, ps, g_tm[:, 2 * h:2 * h + 2, :], ALU.mult))
                    i = V.tensor_tensor(xh, ps, xh, ALU.add)
                    if h == 0:
                        link(i)
                i.then_inc(f_ok.sem, 1)
                fresh()


_OUT = (NB, T, C)


def kernel(**inputs):
    import concourse.bacc as bacc
    from concourse.bass_utils import run_bass_kernel_spmd as run

    nc = bacc.Bacc("TRN2", target_bir_lowering=False, num_devices=1)
    arrays, aps = {}, {}
    for name, v in inputs.items():
        v = np.ascontiguousarray(v)
        if v.dtype == np.bool_:
            v = v.view(np.uint32)
        arrays[f"in_{name}"] = v
        aps[name] = nc.dram_tensor(f"in_{name}", v.shape, mybir.dt.from_np(v.dtype), kind="ExternalInput").ap()
    out = nc.dram_tensor("out_x", _OUT, F32, kind="ExternalOutput").ap()
    build(nc, aps, out)
    r = run(nc, [arrays], core_ids=[0])
    return r.results[0]["out_x"]
```

```python
from contextlib import ExitStack

import numpy as np

import concourse.bass as bass
from concourse import mybir

F32 = mybir.dt.float32
F32R = mybir.dt.float32r
U8 = mybir.dt.uint8
U32 = mybir.dt.uint32
ALU = mybir.AluOpType
ACT = mybir.ActivationFunctionType
AX = mybir.AxisListType

P = 128
NB, T, C = 4, 512, 256
NT, KC = T // P, C // P
NH, HD = 16, 16
NQ = NH // 4
S2 = 64
SHIFT, TOPK = 64, 16
SCALE = float(HD) ** -0.5
LARGE = float(np.float32(3.0e38))
MASKED = -1.0e30
EPS = [1e-6, 1e-6, 1e-6, 1e-5]
NX = 3
RH = 512
RC = RH // P

VECS = {}
_at = 0
for _name, _inp, _first, _n in [
    ("ada0", "L0_xcond_b_ada", 0, 18), ("qk0", "L0_xcond_b_qkv", 0, 4), ("qx0", "L0_xcond_b_q", 0, 2),
    ("kx0", "L0_xcond_b_kv", 0, 2), ("m10", "L0_xcond_b_m1", 0, 16),
    ("ada1", "L1_xcond_b_mod", 0, 12), ("qk1", "L1_xcond_b_qkv", 0, 4), ("qx1", "L1_xcond_b_qc", 0, 2),
    ("kx1", "L1_xcond_b_kvc", 0, 2), ("m11", "L1_xcond_b_mlp1", 0, 8),
    ("ada2", "L2_xcond_ada_b", 0, 12), ("qk2", "L2_xcond_qkv_b", 0, 4), ("qx2", "L2_xcond_q_b", 0, 2),
    ("kx2", "L2_xcond_kv_b", 0, 2), ("m12", "L2_xcond_fc1_b", 0, 8),
    ("gamma", "L3_xcond_ln_gamma", 0, 2), ("beta", "L3_xcond_ln_beta", 0, 2),
    ("gb1", "L3_xcond_gate_b1", 0, 2), ("eb1", "L3_xcond_e_b1", 0, NX * RC), ("cond", "cond_1024", 0, NB * KC),
]:
    VECS[_name] = (_inp, _at, _n)
    _at += _n
NVEC = _at
assert NVEC <= P

ADA = [18, 12, 12]
ADA_AT = [0, 18, 30]
SHIFT_OF = [(0, 6, 12), (0, None, 6), (0, None, 6)]
SCALE_OF = [(2, 8, 14), (2, None, 8), (2, None, 8)]
GATE_OF = [(4, 10, 16), (4, None, 10), (4, None, 10)]
GATES = [[0, 1, 2], [0, 2], [0, 2]]
HIDC = 8
UP = [16, 8, 8]

UNITS = [4, 16, 16]
KCH = [1, 4, 4]
HT = T // 2
UNITS_UP = [8, 4, 4]
NCT = NT * KC
EARLY = 1536 + NQ * C + 2 * C + 4 * C + 2 * C + 4 * C
EARLY1 = EARLY + UP[0] * KC * P + HIDC * C
WORDS = EARLY1 + EARLY
SLOTS = 3
KS = 96
MAX_ROW = 64
LEAD = [8, 12, 12]


OUT_DELAY, LOW_DELAY = 1, [1, 2, 2]


def tiles_before(L, w):
    return min(NQ * UNITS[L], UNITS[L] * (w // KCH[L] + 1) + (w % KCH[L]) * UNITS[L] // KCH[L] + LEAD[L])


def tile_range(L, w):
    return range(tiles_before(L, w - 1) if w > 0 else 0, tiles_before(L, w))


def due_after(L, n, delay):
    return [g for g in range(NQ) if n == min(NQ * UNITS[L] - 1, (g + 1) * UNITS[L] - 1 + delay)]


def outs_in(L, w):
    return [g for n in tile_range(L, w) for g in due_after(L, n, OUT_DELAY)]


class Signal:

    def __init__(self, sem, per, first=0):
        self.sem, self.per, self.first = sem, per, first

    def at(self, layer, b, k):
        base = self.first + sum(NB * n for n in self.per[:layer])
        assert base + k > 0
        return b * self.per[layer] + (base + k)

    def end(self, layer):
        return self.first + sum(NB * n for n in self.per[: layer + 1])


def build(nc, a, out):
    with ExitStack() as ctx:
        def sb(name, shape, dt=F32):
            return ctx.enter_context(nc.sbuf_tensor(name, shape, dt))

        def sem(name):
            return ctx.enter_context(nc.semaphore(name))

        def sig(name, *per, first=0):
            return Signal(sem(name), per, first)

        x_all = sb("x_all", [P, NB * NT * C])
        weights = sb("weights", [P, WORDS])
        q_stack = sb("q_stack", [P, SLOTS, 4, T], F32R)
        k_stack = sb("k_stack", [P, SLOTS, 4, T], F32R)
        probs = sb("probs", [P, 2, 4, T])
        work = sb("work", [P, 4, T])
        hT = sb("hT", [P, KC, T])
        xn = sb("xn", [P, NT, C])
        v_aug = sb("v_aug", [P, NT, NH, 2 * HD])
        k_bd = sb("k_bd", [P, KC, 8, S2])
        v_bd = sb("v_bd", [P, 8, 2 * HD])
        gate_rows = sb("gate_rows", [P, 3, C])
        bg_rows = sb("bg_rows", [P, 2, C])
        ident = sb("ident", [P, P])
        ones = sb("ones", [P, P])
        zeros = sb("zeros", [P, C])
        ones_pair = sb("ones_pair", [P, 2 * HD])
        head_mask = sb("head_mask", [P, 8])
        vec_rows = hT[:, 0, 0:P]
        vecs = sb("vecs", [P, NVEC])
        cond_s = sb("cond_s", [P, KC, NB])
        cond_r = sb("cond_r", [P, KC, NB])
        mod = sb("mod", [P, sum(ADA), NB])
        mod_now = sb("mod_now", [P, 18])
        ctx_tm = xn
        ctxT = sb("ctxT", [P, 2, KC, NB * S2])
        ctx_two = sb("ctx_two", [P, KC, 2, S2])
        kxT = sb("kxT", [P, KC, S2])
        stats = sb("stats", [P, NT, 6])
        mv = sb("mv", [P, NT, 2])
        var_eps = sb("var_eps", [P, NT])
        rstd = sb("rstd", [P, NT])
        half_neg = sb("half_neg", [P, NT])
        block_r = sb("block_r", [P, T // 32])
        nm = sb("nm", [P, NT, NH])
        diag = hT[:, 0, 0:KC * P].rearrange("p (k n) -> p k n", k=KC)
        top = sb("top", [P, 8, 2, 8])
        mrow_words = sb("mrow_words", [1, NB * S2 // 4], U32)
        mask_row = sb("mask_row", [P, NB, S2], F32R)
        one_row = sb("one_row", [P, P], F32R)
        anchor_b = sb("anchor_b", [P, 14, NB])
        anchor_now = sb("anchor_now", [P, 14])
        router_b = sb("router_b", [NX, NB])
        router_now = sb("router_now", [NX, 1])
        router_in = sb("router_in", [NX, 1])
        lg = sb("lg", [P, NT, NX])
        pr = sb("pr", [P, NT, NX])
        sm = sb("sm", [P, 6, NT])

        bank = ctx.enter_context(nc.psum_tensor("bank", [P, 8, T], F32))
        A, B, O, X = 0, 2, 6, 7

        def place(at, *shape):
            n = int(np.prod(shape))
            v = weights[:, at:at + n]
            if len(shape) == 2:
                v = v.rearrange("p (k n) -> p k n", k=shape[0])
            if len(shape) == 3:
                v = v.rearrange("p (e k n) -> p e k n", e=shape[0], k=shape[1])
            return v, at + n

        W = [dict() for _ in range(4)]
        for L in range(3):
            at = (0, EARLY1, 0)[L]
            for name, shape in [("qkv", (KC, 3 * C)), ("so", (NQ, C)), ("qx", (KC, C)), ("kvx", (KC, 2 * C)),
                                ("co", (KC, C)), ("bv", (C,)), ("bvx", (C,)), ("bco", (C,)), ("bm2", (C,))]:
                W[L][name], at = place(at, *shape)
            assert at == (0, EARLY1, 0)[L] + EARLY
            if L == 1:
                at = EARLY
            if L == 2:
                at = EARLY + 2 * 2048
            W[L]["m1"], at = place(at, KC, UP[L] * P)
            if L == 2:
                at = EARLY1
            W[L]["m2"], at = place(at, HIDC, C)
        at = EARLY
        for name, shape in [("q", (KC, C)), ("k", (KC, C)), ("v", (KC, C)), ("g1", (4, C)), ("g2", (KC, C)), ("o", (KC, C)),
                            ("gb2", (C,)), ("ob", (C,))]:
            W[3][name], at = place(at, *shape)
        assert at <= EARLY + 2 * 2048
        at = EARLY1 + 2048
        for name, shape in [("w1_0", (4, RH)), ("r", (6, NX)), ("b2", (NX, C))]:
            W[3][name], at = place(at, *shape)
        assert at <= WORDS
        W[3]["w2"], at = place(0, NX, RC, C)
        assert at <= EARLY
        at = EARLY + 2 * 2048
        for e in (1, 2):
            W[3][f"w1_{e}"], at = place(at, 4, RH)
        assert at <= EARLY1 + 2048
        pf = probs[:, :, :, :].rearrange("p a b t -> p (a b t)")
        wf = work[:, :, :].rearrange("p a t -> p (a t)")
        n0, n1 = ADA[0] * P, ADA[1] * P
        spare = weights[:, EARLY1:WORDS]
        ada_w = [[spare[:, 0:n0], pf[:, 0:n0]],
                 [spare[:, n0:n0 + n1], spare[:, n0 + n1:n0 + 2 * n1]],
                 [pf[:, n0:n0 + n1], wf[:, 0:n1]]]
        assert n0 + 2 * n1 <= EARLY and n0 + n1 <= 8 * T
        w1_anchor = [pf[:, e * KC * RH:(e + 1) * KC * RH].rearrange("p (k n) -> p k n", k=KC) for e in range(NX)]
        g1_anchor = pf[:, NX * KC * RH:NX * KC * RH + KC * C].rearrange("p (k n) -> p k n", k=KC)

        split = pf[:, 0:4 * T].rearrange("p (r s t) -> p r s t", r=2, s=2)
        hid = pf.rearrange("p (m t) -> p m t", m=8)
        score_sb = wf[:, 0:T]
        rest_sb = wf[:, T:2 * T]
        exp_sb = wf[:, 2 * T:3 * T]
        xT = hT
        evT = work[:, 0:2, :]
        uT = work[:, 2:4, :]
        xf = xn[:, :, :].rearrange("p t c -> p (t c)")
        m_hi, m_lo = xf[0:4, 0:T], xf[0:4, T:2 * T]
        logT = xf[0:NX, 0:T]
        qT = sb("qT", [P, KC, T])
        xsum = sb("xsum", [P, T])
        g_tm = k_bd[:, :, :, :].rearrange("p k h s -> p (k h s)").rearrange("p (t c) -> p t c", t=NT)
        p_one = sb("p_one", [P, T])
        p_tm = [p_one[:, :], wf[:, 3 * T:4 * T]]
        p_tm3 = p_one[:, 0:NT * S2].rearrange("p (t s) -> p t s", t=NT)
        pT3 = p_tm[1]
        v3 = v_aug[:, 0, :, :].rearrange("p h d -> p (h d)")[:, 0:C]

        q_scratch = nc.dram_tensor("q_scratch", [KC, P, 2, T], F32, kind="Internal").ap()
        k_scratch = nc.dram_tensor("k_scratch", [KC, P, 2, T], F32, kind="Internal").ap()
        kl_scratch = nc.dram_tensor("kl_scratch", [KC, P, T], F32, kind="Internal").ap()
        m_scratch = nc.dram_tensor("m_scratch", [2, 2, 4, T], F32, kind="Internal").ap()
        q_src = q_scratch.rearrange("c (h d) s t -> c (d s) h t", d=HD)
        q_hi_src = q_scratch.rearrange("c (h d) s t -> c s d h t", d=HD)
        k_src = k_scratch.rearrange("c (h d) s t -> c (d s) h t", d=HD)
        kl_src = kl_scratch.rearrange("c (h d) t -> c d h t", d=HD)

        d_vecs = sem("d_vecs"); d_ctx = sem("d_ctx"); d_x = sem("d_x"); d_mask = sem("d_mask")
        d_ada = [sem(f"d_ada{i}") for i in range(3)]
        d_w = [sem(f"d_w{i}") for i in range(4)]
        d_late = [sem(f"d_late{i}") for i in range(4)]
        d_anchor = sem("d_anchor")
        d_split = [sem("d_split0"), sem("d_split1")]; d_stack = [sem(f"d_stack{i}") for i in range(SLOTS)]
        d_mput = [sem("d_mput0"), sem("d_mput1")]; d_mget = [sem(f"d_mget{i}") for i in range(SLOTS)]
        d_out = sem("d_out")
        pool_chain = sem("pool_chain"); dve_chain = sem("dve_chain"); act_chain = sem("act_chain")
        apart_pe = sem("apart_pe"); apart_pool = sem("apart_pool"); apart_dve = sem("apart_dve"); apart_sp = sem("apart_sp")
        consts = sem("consts"); const_r = sem("const_r")
        vecs_ps = sem("vecs_ps"); vecs_ok = sem("vecs_ok"); cond_ok = sem("cond_ok")
        ctx_ps = sem("ctx_ps"); ctx_ok = sem("ctx_ok"); ctx_var = sem("ctx_var"); ctx_rstd = sem("ctx_rstd")
        ctx_n = sem("ctx_n")
        ada_ps = sem("ada_ps"); ada_ok = sem("ada_ok"); mask_ok = sem("mask_ok")
        so_zero = sem("so_zero")
        anc_ps = sem("anc_ps"); anc_ok = sem("anc_ok")
        d_rb = sem("d_rb")

        def stack_done(L, b, g):
            uses = len(range(g % SLOTS, NQ, SLOTS))
            return b * (uses * 80) + (L * NB * uses * 80 + 80 * (g // SLOTS + 1))

        def mget_done(L, b, g):
            uses = len(range(g % SLOTS, NQ, SLOTS))
            return b * (uses * 16) + (L * NB * uses * 16 + 16 * (g // SLOTS + 1))

        def split_done(L, b, q_or_k, half):
            each = 16 * (1 + q_or_k)
            return b * (2 * each) + (L * NB * 2 * each + each * half)

        n_ln = (6, 6, 6, 2)
        now_ok = sig("now_ok", 1, 1, 1, 1)
        ln_var = sig("ln_var", *n_ln)
        ln_rstd = sig("ln_rstd", *n_ln)
        xn_ok = sig("xn_ok", *n_ln)
        ln_T = sig("ln_T", *n_ln)
        h_ok = sig("h_ok", *n_ln)
        diag_ok = sig("diag_ok", 3, 2, 2, 0)
        gate_ps = sig("gate_ps", 3, 2, 2, 0)
        gate_ok = sig("gate_ok", 3, 2, 2, 0)
        bg_ok = sig("bg_ok", 2, 1, 1, 0)
        qk_ps = sig("qk_ps", 4, 4, 4, 0)
        qk_hi = sig("qk_hi", 4, 4, 4, 0)
        qk_lo = sig("qk_lo", 4, 4, 4, 0)
        v_ps = sig("v_ps", 2, 2, 2, 0)
        v_ok = sig("v_ok", 2, 2, 2, 0)
        s_ps = sig("s_ps", *(NQ * u for u in UNITS), 0)
        s_max = sig("s_max", *(NQ * u for u in UNITS), 0)
        mT_ps = sig("mT_ps", NQ, NQ, NQ, 0)
        mT_hi = sig("mT_hi", NQ, NQ, NQ, 0)
        mT_lo = sig("mT_lo", NQ, NQ, NQ, 0)
        st_ps = sig("st_ps", *(NQ * 2 * k for k in KCH), 0)
        p_ok = sig("p_ok", *(NQ * 2 * k for k in KCH), 0)
        p_used = sig("p_used", *(NQ * k for k in KCH), 0, first=1)
        o_ok = sig("o_ok", NQ, NQ, NQ, 0)
        hd_ok = sig("hd_ok", NQ, NQ, NQ, 0)
        y_ps = sig("y_ps", 6, 6, 6, 0)
        y_ok = sig("y_ok", 6, 6, 6, 0, first=1)
        xb_ok = sig("xb_ok", 4, 4, 4, 0)
        ctx2_ok = sig("ctx2_ok", 1, 1, 1, 1)
        kx_ps = sig("kx_ps", 1, 1, 1, 1)
        kx_ok = sig("kx_ok", 1, 1, 1, 1)
        kbd_ok = sig("kbd_ok", 1, 1, 1, 0)
        vx_ps = sig("vx_ps", 1, 1, 1, 1, first=1)
        vx_ok = sig("vx_ok", 1, 1, 1, 1)
        qx_ps = sig("qx_ps", 2, 2, 2, 2)
        qx_ok = sig("qx_ok", 2, 2, 2, 2)
        sx_ps = sig("sx_ps", 8, 8, 8, 1)
        sx_sb = sig("sx_sb", 8, 0, 0, 0)
        sx_max = sig("sx_max", 8, 8, 8, 1)
        ex_ok = sig("ex_ok", 8, 8, 8, 1)
        px_tm = sig("px_tm", 8, 0, 0, 1)
        pxT_ps = sig("pxT_ps", 8, 8, 8, 1)
        px_ok = sig("px_ok", 8, 8, 8, 1)
        ox_ps = sig("ox_ps", 2, 2, 2, 0)
        ox_ok = sig("ox_ok", 2, 2, 2, 0, first=1)
        up_ps = sig("up_ps", 16, 8, 8, NX * RC + 2)
        act_ok = sig("act_ok", 16, 8, 8, NX * RC + 2)
        hid_ok = sig("hid_ok", 16, 0, 0, 0)
        ev_ps = sig("ev_ps", 0, 0, 0, 2); ev_ok = sig("ev_ok", 0, 0, 0, 2)
        rl_ps = sig("rl_ps", 0, 0, 0, 1); rl_ok = sig("rl_ok", 0, 0, 0, 1)
        rlT_ps = sig("rlT_ps", 0, 0, 0, 1); re_ok = sig("re_ok", 0, 0, 0, 1); rm_ok = sig("rm_ok", 0, 0, 0, 1)
        ex_out = sig("ex_out", 0, 0, 0, 2 * NX); acc_ok = sig("acc_ok", 0, 0, 0, 2 * NX)
        g_ps = sig("g_ps", 0, 0, 0, 2); gs_in = sig("gs_in", 0, 0, 0, 1); gs_ok = sig("gs_ok", 0, 0, 0, 1)
        rT_ps = sig("rT_ps", 0, 0, 0, 2); rT_ok = sig("rT_ok", 0, 0, 0, 2)
        f_ps = sig("f_ps", 0, 0, 0, 2); f_ok = sig("f_ok", 0, 0, 0, 1, first=1)

        n_w = [0, 0, 0, 0]
        blk = ctx.enter_context(nc.Block())

        def kxn(ap):
            return ap.rearrange("(k p) n -> p k n", p=P)

        LOADS = [
            [("qkv", kxn(a["L0_xcond_w_qkv"])), ("qx", kxn(a["L0_xcond_w_q"])), ("kvx", kxn(a["L0_xcond_w_kv"])),
             ("co", kxn(a["L0_xcond_w_co"]))],
            [("qkv", kxn(a["L1_xcond_W_qkv"])), ("qx", kxn(a["L1_xcond_W_qc"])), ("kvx", kxn(a["L1_xcond_W_kvc"])),
             ("co", kxn(a["L1_xcond_W_cproj"]))],
            [("qkv", kxn(a["L2_xcond_qkv_w"])), ("qx", kxn(a["L2_xcond_q_w"])), ("kvx", kxn(a["L2_xcond_kv_w"])),
             ("co", kxn(a["L2_xcond_ca_proj_w"]))],
            [("q", kxn(a["L3_xcond_Wq"])), ("k", kxn(a["L3_xcond_Wk"])), ("v", kxn(a["L3_xcond_Wv"])),
             ("g1", kxn(a["L3_xcond_gate_w1"][0:4 * P, :])), ("g2", kxn(a["L3_xcond_gate_w2"])),
             ("o", kxn(a["L3_xcond_out_w"])), ("r", kxn(a["L3_xcond_router_W"])),
             ("w1_0", kxn(a["L3_xcond_e_w1"][0, 0:4 * P, :]))],
        ]
        LATE = [
            [("m1", kxn(a["L0_xcond_w_m1"])), ("m2", kxn(a["L0_xcond_w_m2"]))],
            [("m1", kxn(a["L1_xcond_W_mlp1"])), ("m2", kxn(a["L1_xcond_W_mlp2"]))],
            [("m1", kxn(a["L2_xcond_fc1_w"])), ("m2", kxn(a["L2_xcond_fc2_w"]))],
            [("w1_1", kxn(a["L3_xcond_e_w1"][1, 0:4 * P, :])), ("w1_2", kxn(a["L3_xcond_e_w1"][2, 0:4 * P, :]))],
        ]
        SO = [a["L0_xcond_w_so"], a["L1_xcond_W_proj"], a["L2_xcond_sa_proj_w"]]
        BSO = [a["L0_xcond_b_so"], a["L1_xcond_b_proj"], a["L2_xcond_sa_proj_b"]]
        ROWS = [
            [("bv", a["L0_xcond_b_qkv"][2 * C:]), ("bvx", a["L0_xcond_b_kv"][C:]), ("bco", a["L0_xcond_b_co"]),
             ("bm2", a["L0_xcond_b_m2"])],
            [("bv", a["L1_xcond_b_qkv"][2 * C:]), ("bvx", a["L1_xcond_b_kvc"][C:]), ("bco", a["L1_xcond_b_cproj"]),
             ("bm2", a["L1_xcond_b_mlp2"])],
            [("bv", a["L2_xcond_qkv_b"][2 * C:]), ("bvx", a["L2_xcond_kv_b"][C:]), ("bco", a["L2_xcond_ca_proj_b"]),
             ("bm2", a["L2_xcond_fc2_b"])],
            [("gb2", a["L3_xcond_gate_b2"]), ("ob", a["L3_xcond_out_b"])],
        ]
        N_LOADS = [len(LOADS[L]) + 5 + len(ROWS[L]) for L in range(3)] + [len(LOADS[3]) + len(ROWS[3]) + NX]
        N_LATE = [2, 2, 2, 2 + NX]

        def load_layer(eng, L):
            for name, src in LOADS[L]:
                eng.dma_start(W[L][name], src).then_inc(d_w[L], 16)
            for name, src in ROWS[L]:
                eng.dma_start(W[L][name], src.partition_broadcast(P)).then_inc(d_w[L], 16)
            if L < 3:
                eng.wait_ge(so_zero, L + 1)
                so = SO[L].rearrange("(q j d) n -> j d q n", j=4, d=HD)
                for j in range(4):
                    eng.dma_start(W[L]["so"][32 * j:32 * j + HD, :, :], so[j]).then_inc(d_w[L], 16)
                eng.dma_start(W[L]["so"][HD:HD + 1, 0, :], BSO[L].rearrange("(a n) -> a n", a=1)).then_inc(d_w[L], 16)
            else:
                for e in range(NX):
                    eng.dma_start(W[3]["b2"][:, e, :], a["L3_xcond_e_b2"][e].partition_broadcast(P)).then_inc(d_w[3], 16)

        def load_late(eng, L):
            for name, src in LATE[L]:
                eng.dma_start(W[L][name], src).then_inc(d_late[L], 16)
            if L == 3:
                for e in range(NX):
                    eng.dma_start(W[3]["w2"][:, e, :, :], kxn(a["L3_xcond_e_w2"][e])).then_inc(d_late[3], 16)

        ADA_SRC = [a["L0_xcond_w_ada"], a["L1_xcond_W_mod"], a["L2_xcond_ada_w"]]
        FULL = slice(SHIFT, T - SHIFT)

        @blk.sync
        def _(sp):
            for name, (inp, at, n) in VECS.items():
                src = a[inp]
                if len(src.shape) == 2:
                    src = src.rearrange("b n -> (b n)")
                sp.dma_start(vec_rows[at:at + n, :], src[0:n * P].rearrange("(m p) -> m p", p=P)).then_inc(d_vecs, 16)
            for k in range(KC):
                sp.dma_start(ada_w[0][k], kxn(ADA_SRC[0])[:, k, :]).then_inc(d_ada[0], 16)
            sp.dma_start(ctx_tm[:, 0:2, :], a["ctx_1024"].rearrange("(g b) s c -> (b s) g c", g=2)).then_inc(d_ctx, 16)
            for b in range(NB):
                xv = x_all[:, b * NT * C:(b + 1) * NT * C].rearrange("p (t c) -> p t c", t=NT)
                sp.dma_start(xv[:, 0:NT - 1, :], a["x"][b, FULL, :].rearrange("(t p) c -> p t c", p=P)).then_inc(d_x, 16)
                sp.dma_start(xv[0:SHIFT, NT - 1, :], a["x"][b, T - SHIFT:, :]).then_inc(d_x, 16)
                sp.dma_start(xv[SHIFT:P, NT - 1, :], a["x"][b, 0:SHIFT, :]).then_inc(d_x, 16)
            sp.dma_start(mrow_words[:, :], a["mask_BxS2_bf0"].rearrange("(o b) s -> o (b s)", o=1)).then_inc(d_mask, 16)
            for L in (1, 2):
                for k in range(KC):
                    sp.dma_start(ada_w[L][k], kxn(ADA_SRC[L])[:, k, :]).then_inc(d_ada[L], 16)
            for L in range(3):
                if L == 0:
                    sp.wait_ge(const_r, 1)
                with sp.Fori(0, NB) as b:
                    for i in range(4):
                        sp.wait_ge(qk_hi.sem, qk_hi.at(L, b, i + 1))
                        sp.wait_ge(qk_lo.sem, qk_lo.at(L, b, i + 1))
                        if i < 2:
                            sp.wait_ge(p_used.sem, p_used.at(L, b, 0))
                        c = i // 2
                        if i % 2 == 0:
                            sp.dma_start(q_scratch[c], split[:, 0, :, :]).then_inc(d_split[0], 16)
                        else:
                            sp.dma_start(k_scratch[c], split[:, 1, 0:1, :].to_broadcast([P, 2, T])).then_inc(d_split[1], 16)
                            sp.dma_start(kl_scratch[c], split[:, 1, 1, :]).then_inc(d_split[1], 16)

                    def stack(g):
                        c, h0, s = g // 2, 4 * (g % 2), g % SLOTS
                        if g % 2 == 0:
                            for i in range(2):
                                sp.wait_ge(d_split[i], split_done(L, b, i, c + 1))
                                sp.sem_inc(apart_sp, 1)
                        if g >= SLOTS:
                            sp.wait_ge(st_ps.sem, st_ps.at(L, b, (g - SLOTS + 1) * 2 * KCH[L]))
                        sp.dma_start(q_stack[MAX_ROW:MAX_ROW + 2, s, :, :].bitcast(F32).rearrange("p h (a t) -> p (h a) t", a=2),
                                     zeros[64:66, :].unsqueeze(1).to_broadcast([2, 8, C])).then_inc(d_stack[s], 16)
                        sp.dma_start(q_stack[0:32, s, :, :].bitcast(F32), q_src[c, :, h0:h0 + 4, :]).then_inc(d_stack[s], 16)
                        sp.dma_start(k_stack[0:32, s, :, :].bitcast(F32), k_src[c, :, h0:h0 + 4, :]).then_inc(d_stack[s], 16)
                        sp.dma_start(q_stack[32:48, s, :, :].bitcast(F32), q_hi_src[c, 0, :, h0:h0 + 4, :]).then_inc(d_stack[s], 16)
                        sp.dma_start(k_stack[32:48, s, :, :].bitcast(F32), kl_src[c, :, h0:h0 + 4, :]).then_inc(d_stack[s], 16)

                    def maxima(g):
                        sp.wait_ge(mT_hi.sem, mT_hi.at(L, b, g + 1))
                        sp.wait_ge(mT_lo.sem, mT_lo.at(L, b, g + 1))
                        for s, src in enumerate((m_hi, m_lo)):
                            sp.dma_start(m_scratch[g % 2, s], src).then_inc(d_mput[g % 2], 16)
                        sp.wait_ge(d_mput[g % 2], b * 64 + (L * NB * 64 + 32 * (g // 2 + 1)))
                        sp.dma_start(q_stack[MAX_ROW:MAX_ROW + 2, g % SLOTS, :, :].bitcast(F32), m_scratch[g % 2]).then_inc(d_mget[g % SLOTS], 16)

                    for g in range(SLOTS):
                        stack(g)
                    for g in range(NQ):
                        maxima(g)
                        if g == 1:
                            for later in range(SLOTS, NQ):
                                stack(later)
            with sp.Fori(0, NB) as b:
                sp.wait_ge(f_ok.sem, f_ok.at(3, b, 1))
                sp.sem_inc(apart_sp, 1)
                xv = x_all[:, bass.ds(b * (NT * C), NT * C)].rearrange("p (t c) -> p t c", t=NT)
                ob = out[bass.ds(b, 1), :, :].rearrange("o s c -> (o s) c")
                sp.dma_start(ob[FULL, :].rearrange("(t p) c -> p t c", p=P), xv[:, 0:NT - 1, :]).then_inc(d_out, 16)
                sp.dma_start(ob[T - SHIFT:T, :], xv[0:SHIFT, NT - 1, :]).then_inc(d_out, 16)
                sp.dma_start(ob[0:SHIFT, :], xv[SHIFT:P, NT - 1, :]).then_inc(d_out, 16)
            sp.wait_ge(d_out, 16 * 3 * NB)

        @blk.gpsimd
        def _(po):
            n = [0]

            def link(ins):
                n[0] += 1
                ins.then_inc(pool_chain, 1)
                po.wait_ge(pool_chain, n[0])

            def fresh():
                n[0] = 0
                po.sem_clear(pool_chain)

            def apart():
                po.sem_inc(apart_pool, 1)

            def band(t, groups, width, step, base):
                link(po.affine_select(out=t, in_=t, compare_op=ALU.is_ge, fill=0.0, base=base,
                                      pattern=[[-step, groups]], channel_multiplier=1))
                link(po.affine_select(out=t, in_=t, compare_op=ALU.is_ge, fill=0.0, base=width - 1 - base,
                                      pattern=[[step, groups]], channel_multiplier=-1))

            link(po.memset(ident[:, :], 1.0))
            link(po.affine_select(out=ident[:, :], in_=ident[:, :], compare_op=ALU.is_equal, fill=0.0, base=0,
                                  pattern=[[-1, P]], channel_multiplier=1))
            link(po.memset(ones[:, :], 1.0))
            link(po.memset(zeros[:, :], 0.0))
            po.memset(W[0]["so"], 0.0).then_inc(so_zero, 1)
            po.wait_ge(so_zero, 1)
            link(po.memset(head_mask[:, :], 1.0))
            band(head_mask[:, :], 8, HD, HD, 0)
            link(po.memset(ones_pair[:, :], 0.0))
            link(po.memset(ones_pair[0:S2, 0:HD], 1.0))
            link(po.memset(ones_pair[S2:P, HD:2 * HD], 1.0))
            link(po.memset(v_bd[:, :, :], 0.0))
            link(po.memset(half_neg[:, :], -0.5))
            link(po.memset(v_aug[:, :, :, HD:2 * HD], 1.0))
            po.sem_inc(consts, 1)
            po.wait_ge(ctx_var, 1)
            link(po.tensor_scalar(var_eps[:, 0:2], mv[:, 0:2, 1], EPS[1], None, ALU.add))
            po.tensor_tensor(rstd[:, 0:2], var_eps[:, 0:2], half_neg[:, 0:2], ALU.pow).then_inc(ctx_rstd, 1)
            fresh()
            po.wait_ge(ada_ps, 3)
            po.memset(W[1]["so"], 0.0).then_inc(so_zero, 1)

            for L in range(4):
                if L == 1:
                    po.wait_ge(so_zero, 2)
                    po.wait_ge(y_ps.sem, y_ps.end(0))
                    po.memset(W[2]["so"], 0.0).then_inc(so_zero, 1)
                    po.wait_ge(so_zero, 3)
                with po.Fori(0, NB) as b:
                    xv = x_all[:, bass.ds(b * (NT * C), NT * C)].rearrange("p (t c) -> p t c", t=NT)

                    def context():
                        po.wait_ge(vx_ps.sem, vx_ps.at(L, b, 0))
                        po.wait_ge(ctx_ok, 4)
                        for k in range(KC):
                            for h in range(2):
                                i = po.tensor_copy(ctx_two[:, k, h, :],
                                                   ctxT[:, 1 if L == 1 else 0, k, bass.ds(b * S2, S2)])
                                if 2 * k + h < 3:
                                    link(i)
                        i.then_inc(ctx2_ok.sem, 1)

                    def norm(j, h):
                        po.wait_ge(ln_var.sem, ln_var.at(L, b, 2 * j + h + 1))
                        apart()
                        ts = slice(2 * h, 2 * h + 2)
                        link(po.tensor_scalar(var_eps[:, ts], mv[:, ts, 1], EPS[L], None, ALU.add))
                        po.tensor_tensor(rstd[:, ts], var_eps[:, ts], half_neg[:, ts], ALU.pow).then_inc(ln_rstd.sem, 1)

                    def add_bias(j, h):
                        po.wait_ge(xn_ok.sem, xn_ok.at(L, b, 2 * j + h + 1))
                        apart()
                        row = bg_rows[:, j - 1, :] if j in GATES[L] else W[L]["bco"]
                        xh = xv[:, 2 * h:2 * h + 2, :]
                        po.tensor_tensor(xh, xh, row.unsqueeze(1).to_broadcast([P, 2, C]), ALU.add).then_inc(xb_ok.sem, 1)

                    if L == 3:
                        context()
                        norm(0, 0)
                        norm(0, 1)
                    else:
                        if L < 3:
                            po.wait_ge(d_w[L], 16 * N_LOADS[L])
                        context()
                        norm(0, 0)
                        norm(0, 1)
                        j = 0
                        for g, blk_no in enumerate(GATES[L]):
                            if blk_no == 0:
                                continue
                            po.wait_ge(gate_ok.sem, gate_ok.at(L, b, g + 1))
                            row = W[L]["bco"] if blk_no == 1 else W[L]["bm2"]
                            po.tensor_tensor(bg_rows[:, blk_no - 1, :], row, gate_rows[:, blk_no, :], ALU.mult).then_inc(bg_ok.sem, 1)
                            j += 1
                            po.wait_ge(bg_ok.sem, bg_ok.at(L, b, j))
                        po.wait_ge(kx_ok.sem, kx_ok.at(L, b, 1))
                        for k in range(KC):
                            i = po.tensor_tensor(k_bd[:, k, :, :], kxT[:, k, :].unsqueeze(1).to_broadcast([P, 8, S2]),
                                                 head_mask[:, :].unsqueeze(2).to_broadcast([P, 8, S2]), ALU.mult)
                            if k == 0:
                                link(i)
                        i.then_inc(kbd_ok.sem, 1)
                        norm(1, 0)
                        norm(1, 1)
                        add_bias(1, 0)
                        add_bias(1, 1)
                        for h in range(2):
                            norm(2, h)
                            add_bias(2, h)
                    fresh()

        @blk.tensor
        def _(pe):
            mm = nc.tensor.matmul

            def wait(s, L, b, k):
                pe.wait_ge(s.sem, s.at(L, b, k))

            def apart():
                pe.sem_inc(apart_pe, 1)

            pe.sem_inc(p_used.sem, 1)
            pe.sem_inc(vx_ps.sem, 1)

            pe.wait_ge(consts, 1)
            pe.wait_ge(d_vecs, 16 * len(VECS))
            nc.tensor.transpose(bank[:, X, 0:NVEC], vec_rows[0:NVEC, :], ident[0:NVEC, 0:NVEC]).then_inc(vecs_ps, 1)

            pe.wait_ge(cond_ok, 1)
            for L in range(3):
                pe.wait_ge(d_ada[L], 16 * KC)
                for m in range(ADA[L]):
                    for k in range(KC):
                        i = mm(bank[:, B + L, m * NB:(m + 1) * NB], ada_w[L][k][:, m * P:(m + 1) * P], cond_s[:, k, :],
                               start=(k == 0), stop=(k == KC - 1))
                i.then_inc(ada_ps, 1)
            pe.wait_ge(d_ctx, 16)
            for v in range(2):
                if v == 1:
                    pe.wait_ge(ctx_n, 1)
                    pe.wait_ge(ctx_ok, 2)
                for k in range(KC):
                    for g in range(2):
                        i = nc.tensor.transpose(bank[:, A + k, g * P:(g + 1) * P], ctx_tm[:, 2 * v + g, k * P:(k + 1) * P], ident[:, :])
                    i.then_inc(ctx_ps, 1)

            def transposes(L, b, j, h, bk):
                wait(xn_ok, L, b, 2 * j + h + 1)
                for k in range(KC):
                    for t in range(2):
                        i = nc.tensor.transpose(bank[:, bk, k * HT + t * P:k * HT + (t + 1) * P],
                                                xn[:, 2 * h + t, k * P:(k + 1) * P], ident[:, :])
                i.then_inc(ln_T.sem, 1)

            def tm_out(L, b, h, bk, lhs, rhs, kn, done):
                for t in (2 * h, 2 * h + 1):
                    for k in range(kn):
                        i = mm(bank[:, bk, (t % 2) * C:(t % 2 + 1) * C], lhs(k, t), rhs(k),
                               start=(k == 0), stop=(k == kn - 1))
                i.then_inc(done.sem, 1)

            for L in range(3):
                w = W[L]
                pe.wait_ge(d_w[L], 16 * N_LOADS[L])
                with pe.Fori(0, NB) as b:
                    for g, blk_no in enumerate(GATES[L]):
                        wait(diag_ok, L, b, g + 1)
                        if g == 0:
                            wait(ox_ok, L, b, 0)
                        else:
                            wait(gate_ok, L, b, g)
                        for k in range(KC):
                            i = mm(bank[:, X, k * P:(k + 1) * P], ones[:, :], diag[:, k, :], start=True, stop=True)
                        i.then_inc(gate_ps.sem, 1)
                    wait(ctx2_ok, L, b, 1)
                    wait(gate_ok, L, b, len(GATES[L]))
                    for m in range(KC):
                        for k in range(KC):
                            i = mm(bank[:, X, m * S2:(m + 1) * S2], w["kvx"][:, k, m * P:(m + 1) * P], ctx_two[:, k, 0, :],
                                   start=(k == 0), stop=(k == KC - 1))
                    i.then_inc(kx_ps.sem, 1)
                    wait(kx_ok, L, b, 1)
                    for k in range(KC):
                        i = mm(bank[:, X, 0:C], ctx_two[:, k, :, :], w["kvx"][:, k, C:2 * C], start=(k == 0), stop=(k == KC - 1))
                    i.then_inc(vx_ps.sem, 1)

                    wait(y_ok, L, b, 0)
                    for h in range(2):
                        transposes(L, b, 0, h, A + h)
                    wait(h_ok, L, b, 2)
                    for i4 in range(4):
                        m = (i4 % 2) * KC + i4 // 2
                        for k in range(KC):
                            i = mm(bank[:, B + i4, :], w["qkv"][:, k, m * P:(m + 1) * P], hT[:, k, :], start=(k == 0), stop=(k == KC - 1))
                        i.then_inc(qk_ps.sem, 1)
                    for t in range(NT):
                        for k in range(KC):
                            i = mm(bank[:, A + t // 2, (t % 2) * C:(t % 2 + 1) * C], hT[:, k, t * P:(t + 1) * P], w["qkv"][:, k, 2 * C:3 * C],
                                   start=(k == 0), stop=(k == KC - 1))
                        if t % 2:
                            i.then_inc(v_ps.sem, 1)

                    def score_tile(n):
                        g, u = n // UNITS[L], n % UNITS[L]
                        s = g % SLOTS
                        if u == 0:
                            pe.wait_ge(d_stack[s], stack_done(L, b, g))
                        if n < 2:
                            wait(v_ok, L, b, n + 1)
                        else:
                            wait(s_max, L, b, n - 1)
                        if L == 0:
                            for j in range(4):
                                cols = slice(u * P, (u + 1) * P)
                                i = mm(bank[:, A + n % 2, j * P:(j + 1) * P], q_stack[0:KS, s, j, cols], k_stack[0:KS, s, j, cols],
                                       start=True, stop=True)
                        else:
                            j, t = u // 4, u % 4
                            i = mm(bank[:, A + n % 2, :], q_stack[0:KS, s, j, t * P:(t + 1) * P], k_stack[0:KS, s, j, :],
                                   start=True, stop=True)
                        i.then_inc(s_ps.sem, 1)

                    def maxima_out(g):
                        wait(s_max, L, b, (g + 1) * UNITS[L])
                        if g > 0:
                            wait(mT_hi, L, b, g)
                            wait(mT_lo, L, b, g)
                        else:
                            wait(vx_ok, L, b, 1)
                        for t in range(NT):
                            i = nc.tensor.transpose(bank[0:4, X, t * P:(t + 1) * P], nm[:, t, 4 * g:4 * g + 4], ident[:, :])
                        i.then_inc(mT_ps.sem, 1)

                    def key_scores(w):
                        g, c = w // KCH[L], w % KCH[L]
                        s = g % SLOTS
                        if c == 0:
                            pe.wait_ge(d_mget[s], mget_done(L, b, g))
                        for hp in range(2):
                            n = 2 * w + hp
                            if n < 2:
                                wait(qk_lo, L, b, 4)
                            else:
                                wait(p_ok, L, b, n - 1)
                            for j in (2 * hp, 2 * hp + 1):
                                if L == 0:
                                    for u in range(NT):
                                        cols = slice(u * P, (u + 1) * P)
                                        i = mm(bank[:, B + j, cols], k_stack[0:KS, s, j, cols], q_stack[0:KS, s, j, cols],
                                               start=True, stop=True)
                                else:
                                    i = mm(bank[:, B + j, :], k_stack[0:KS, s, j, c * P:(c + 1) * P], q_stack[0:KS, s, j, :],
                                           start=True, stop=True)
                            i.then_inc(st_ps.sem, 1)

                    def weigh(w):
                        g, c = w // KCH[L], w % KCH[L]
                        wait(p_ok, L, b, 2 * w + 2)
                        if c == 0 and g > 0:
                            wait(o_ok, L, b, g)
                        if L == 0:
                            for u in range(NT):
                                for j in range(4):
                                    cols = slice(u * P, (u + 1) * P)
                                    i = mm(bank[32 * j:32 * j + 32, O, cols], v_aug[:, u, 4 * g + j, :], probs[:, w % 2, j, cols],
                                           start=True, stop=True)
                        else:
                            for j in range(4):
                                i = mm(bank[32 * j:32 * j + 32, O, :], v_aug[:, c, 4 * g + j, :], probs[:, w % 2, j, :],
                                       start=(c == 0), stop=(c == KCH[L] - 1))
                        i.then_inc(p_used.sem, 1)

                    steps = NQ * KCH[L]
                    for step in range(steps):
                        for n in tile_range(L, step):
                            score_tile(n)
                            for g in due_after(L, n, OUT_DELAY):
                                maxima_out(g)
                        if step == 0:
                            key_scores(0)
                        if step + 1 < steps:
                            key_scores(step + 1)
                        weigh(step)
                    wait(hd_ok, L, b, NQ)
                    wait(s_max, L, b, NQ * UNITS[L])
                    for h in range(2):
                        tm_out(L, b, h, A + h, lambda k, t: work[:, k, t * P:(t + 1) * P], lambda k: w["so"][:, k, :], NQ, y_ps)

                    def half(h):
                        return slice(h * HT, (h + 1) * HT)

                    def cross_scores(n):
                        t, k = n // KC, n % KC
                        if n % 4 == 0:
                            wait(qx_ok, L, b, n // 4 + 1)
                        if n < 2:
                            wait(y_ok, L, b, n + 1)
                        else:
                            wait(sx_sb if L == 0 else sx_max, L, b, n - 1)
                        i = mm(bank[:, A + n % 2, :], qT[:, k, t * P:(t + 1) * P], k_bd[:, k, :, :], start=True, stop=(L != 2))
                        if L == 2:
                            i = mm(bank[:, A + n % 2, :].rearrange("p (h s) -> p h s", h=8), one_row[:, :],
                                   mask_row[:, bass.ds(b, 1), :].to_broadcast([P, 8, S2]),
                                   start=False, stop=True)
                        i.then_inc(sx_ps.sem, 1)

                    def probs_T(n):
                        wait(px_tm if L == 0 else ex_ok, L, b, n + 1)
                        if n >= 2:
                            wait(px_ok, L, b, n - 1)
                        for r in range(4):
                            i = nc.tensor.transpose(bank[:, B + n % 2, r * P:(r + 1) * P], p_tm[n % 2][:, r * P:(r + 1) * P], ident[:, :])
                        i.then_inc(pxT_ps.sem, 1)

                    def cross_heads(h):
                        wait(px_ok, L, b, 4 * h + 4)
                        if h == 1:
                            wait(y_ok, L, b, 3)
                            wait(h_ok, L, b, 5)
                        for lhs, bk in ((lambda m: v_bd[:, m, :], O), (lambda m: ones_pair[:, :], X)):
                            for c in range(KC):
                                for r in range(4):
                                    i = mm(bank[32 * r:32 * r + 32, bk, c * HT:(c + 1) * HT], lhs(4 * c + r), hid[:, 4 * c + r, half(h)],
                                           start=True, stop=True)
                        i.then_inc(ox_ps.sem, 1)

                    def cross_out(h):
                        wait(ox_ok, L, b, h + 1)
                        tm_out(L, b, h, O, lambda k, t: xT[:, k, t * P:(t + 1) * P], lambda k: w["co"][:, k, :], KC, y_ps)

                    def up(h, units):
                        for u in units:
                            n = h * UNITS_UP[L] + u
                            if u == 0:
                                wait(h_ok, L, b, 5 + h)
                            if n >= 2:
                                wait(hid_ok if L == 0 else act_ok, L, b, n - 1)
                            for e in range(2):
                                m = u + e * HIDC if L == 0 else 2 * u + e
                                for k in range(KC):
                                    i = mm(bank[:, B + 2 + n % 2, e * HT:(e + 1) * HT], w["m1"][:, k, m * P:(m + 1) * P], hT[:, k, half(h)],
                                           start=(k == 0), stop=(k == KC - 1))
                            i.then_inc(up_ps.sem, 1)

                    def down(h):
                        wait(hid_ok if L == 0 else act_ok, L, b, (h + 1) * UNITS_UP[L])
                        tm_out(L, b, h, A + h, lambda k, t: hid[:, k, t * P:(t + 1) * P], lambda k: w["m2"][:, k, :], HIDC, y_ps)

                    for h in range(2):
                        transposes(L, b, 1, h, B + h)
                    for h in range(2):
                        wait(h_ok, L, b, 3 + h)
                        for m in range(KC):
                            for k in range(KC):
                                i = mm(bank[:, B + 2 + h, m * HT:(m + 1) * HT], w["qx"][:, k, m * P:(m + 1) * P], hT[:, k, half(h)],
                                       start=(k == 0), stop=(k == KC - 1))
                        i.then_inc(qx_ps.sem, 1)
                    cross_scores(0)
                    for n in range(5):
                        cross_scores(n + 1)
                        probs_T(n)
                    cross_heads(0)
                    cross_scores(6)
                    probs_T(5)
                    cross_out(0)
                    cross_scores(7)
                    pe.wait_ge(d_late[L], 16 * N_LATE[L])
                    if L == 0:
                        transposes(L, b, 2, 0, X)
                        up(0, range(2))
                        probs_T(6)
                        up(0, range(2, UNITS_UP[L]))
                        probs_T(7)
                    else:
                        probs_T(6)
                        probs_T(7)
                        transposes(L, b, 2, 0, X)
                        up(0, range(UNITS_UP[L]))
                    cross_heads(1)
                    cross_out(1)
                    down(0)
                    transposes(L, b, 2, 1, X)
                    up(1, range(UNITS_UP[L]))
                    down(1)

            L, w = 3, W[3]
            pe.wait_ge(d_w[3], 16 * N_LOADS[3])
            pe.wait_ge(d_anchor, 16 * (NX + 1))
            pe.wait_ge(y_ok.sem, y_ok.end(2))
            pe.wait_ge(act_chain, 1)
            for m in range(NX * RC + 2):
                for k in range(KC):
                    e = m // RC
                    lhs = g1_anchor[:, k, (m - NX * RC) * P:(m - NX * RC + 1) * P] if m >= NX * RC else w1_anchor[e][:, k, (m % RC) * P:(m % RC + 1) * P]
                    mm(bank[:, B, m * NB:(m + 1) * NB], lhs, cond_r[:, k, :], start=(k == 0), stop=(k == KC - 1))
            for k in range(KC):
                i = mm(bank[0:NX, B + 1, 0:NB], w["r"][:, 4 + k, :], cond_r[:, k, :], start=(k == 0), stop=(k == KC - 1))
            i.then_inc(anc_ps, 1)
            pe.wait_ge(anc_ok, 2)
            comb = lambda k: hT[:, k, :] if k < 2 else evT[:, k - 2, :]
            with pe.Fori(0, NB) as b:
                wait(ctx2_ok, L, b, 1)
                wait(f_ok, L, b, 0)
                for m in range(KC):
                    for k in range(KC):
                        i = mm(bank[:, X, m * S2:(m + 1) * S2], w["k"][:, k, m * P:(m + 1) * P], ctx_two[:, k, 0, :],
                               start=(k == 0), stop=(k == KC - 1))
                i.then_inc(kx_ps.sem, 1)
                wait(kx_ok, L, b, 1)
                for k in range(KC):
                    i = mm(bank[0:S2, X, 0:C], ctx_two[:, k, 0, :], w["v"][:, k, :], start=(k == 0), stop=(k == KC - 1))
                i.then_inc(vx_ps.sem, 1)
                for h in range(2):
                    transposes(L, b, 0, h, A + h)
                wait(h_ok, L, b, 2)
                for m in range(KC):
                    for k in range(KC):
                        i = mm(bank[:, B + m, :], w["q"][:, k, m * P:(m + 1) * P], hT[:, k, :], start=(k == 0), stop=(k == KC - 1))
                    i.then_inc(qx_ps.sem, 1)
                wait(qx_ok, L, b, 2)
                for t in range(NT):
                    for k in range(KC):
                        i = mm(bank[:, A, t * S2:(t + 1) * S2], qT[:, k, t * P:(t + 1) * P], kxT[:, k, :], start=(k == 0), stop=(k == KC - 1))
                i.then_inc(sx_ps.sem, 1)
                wait(px_tm, L, b, 1)
                wait(vx_ok, L, b, 1)
                apart()
                for t in range(NT):
                    i = nc.tensor.transpose(bank[0:S2, X, t * P:(t + 1) * P], p_tm3[:, t, :], ident[:, :])
                i.then_inc(pxT_ps.sem, 1)
                wait(px_ok, L, b, 1)
                for m in range(KC):
                    mm(bank[:, B + m, :], v3[0:S2, m * P:(m + 1) * P], pT3[0:S2, :], start=True, stop=True).then_inc(ev_ps.sem, 1)
                wait(ev_ok, L, b, 2)
                for k in range(4):
                    i = mm(bank[0:NX, X, :], w["r"][:, k, :], comb(k), start=(k == 0), stop=(k == 3))
                i.then_inc(rl_ps.sem, 1)

                def hidden(m):
                    if m >= 4:
                        wait(act_ok, L, b, m - 3)
                    for k in range(4):
                        lhs = w[f"w1_{m // RC}"][:, k, (m % RC) * P:(m % RC + 1) * P] if m < NX * RC else w["g1"][:, k, (m - NX * RC) * P:(m - NX * RC + 1) * P]
                        i = mm(bank[:, B + m % 4, :], lhs, comb(k), start=(k == 0), stop=(k == 3))
                    i.then_inc(up_ps.sem, 1)

                def expert(e):
                    wait(act_ok, L, b, RC * (e + 1))
                    for t in range(NT):
                        if t % 2 == 0 and e > 0:
                            wait(acc_ok, L, b, 2 * (e - 1) + t // 2 + 1)
                        for k in range(RC):
                            i = mm(bank[:, A + t // 2, (t % 2) * C:(t % 2 + 1) * C], hid[:, (e % 2) * RC + k, t * P:(t + 1) * P], w["w2"][:, e, k, :],
                                   start=(k == 0), stop=(k == RC - 1))
                        if t % 2:
                            i.then_inc(ex_out.sem, 1)

                for m in range(RC):
                    hidden(m)
                pe.wait_ge(d_late[3], 16 * N_LATE[3])
                wait(rl_ok, L, b, 1)
                apart()
                for t in range(NT):
                    i = nc.tensor.transpose(bank[:, X, t * NX:(t + 1) * NX], logT[:, t * P:(t + 1) * P], ident[0:NX, 0:NX])
                i.then_inc(rlT_ps.sem, 1)
                for e in range(NX):
                    if e + 1 < NX:
                        for m in range(RC):
                            hidden(RC * (e + 1) + m)
                    else:
                        hidden(NX * RC)
                        hidden(NX * RC + 1)
                    expert(e)
                wait(acc_ok, L, b, 2 * NX)
                wait(act_ok, L, b, NX * RC + 2)
                for h in range(2):
                    tm_out(L, b, h, A + h, lambda k, t: uT[:, k, t * P:(t + 1) * P], lambda k: w["g2"][:, k, :], KC, g_ps)
                for k in range(KC):
                    for t in range(NT):
                        i = nc.tensor.transpose(bank[:, B + k, t * P:(t + 1) * P], xn[:, t, k * P:(k + 1) * P], ident[:, :])
                    i.then_inc(rT_ps.sem, 1)
                wait(rT_ok, L, b, 2)
                wait(gs_in, L, b, 1)
                for h in range(2):
                    tm_out(L, b, h, A + h, lambda k, t: hT[:, k, t * P:(t + 1) * P], lambda k: w["o"][:, k, :], KC, f_ps)

        @blk.scalar
        def _(ac):
            act = nc.scalar.activation

            def wait(s, L, b, k):
                ac.wait_ge(s.sem, s.at(L, b, k))

            load_layer(ac, 0)
            load_late(ac, 0)
            ac.wait_ge(vecs_ps, 1)
            nc.scalar.copy(vecs[:, :], bank[:, X, 0:NVEC]).then_inc(vecs_ok, 1)
            ac.wait_ge(vecs_ok, 1)
            cv = VECS["cond"][1]
            cond_cols = vecs[:, cv:cv + NB * KC].rearrange("p (b k) -> p k b", b=NB)
            act(cond_s[:, :, :], cond_cols, ACT.Silu).then_inc(cond_ok, 1)
            act(cond_r[:, :, :], cond_cols, ACT.Copy).then_inc(act_chain, 1)
            for n in range(4):
                ac.wait_ge(ctx_ps, n + 1)
                nc.scalar.copy(ctxT[:, n // 2, n % 2, :], bank[:, A + n % 2, 0:NB * S2]).then_inc(ctx_ok, 1)
            ac.wait_ge(ada_ps, 3)
            load_layer(ac, 1)

            def to_feature(L, b, j, h, bk):
                wait(ln_T, L, b, 2 * j + h + 1)
                if j == 0 and h == 0 and L < 3:
                    wait(now_ok, L, b, 1)
                for k in range(KC):
                    if L == 3:
                        g, be = VECS["gamma"][1] + k, VECS["beta"][1] + k
                        s, o = vecs[:, g:g + 1], vecs[:, be:be + 1]
                    elif SCALE_OF[L][j] is None:
                        s, o = 1.0, 0.0
                    else:
                        sc, sh = SCALE_OF[L][j] + k, SHIFT_OF[L][j] + k
                        s, o = mod_now[:, sc:sc + 1], mod_now[:, sh:sh + 1]
                    i = act(hT[:, k, h * HT:(h + 1) * HT], bank[:, bk, k * HT:(k + 1) * HT], ACT.Identity, bias=o, scale=s)
                i.then_inc(h_ok.sem, 1)

            for L in range(3):
                if L > 0:
                    ac.wait_ge(y_ps.sem, y_ps.end(L - 1))
                    load_late(ac, L)
                    load_layer(ac, L + 1)
                with ac.Fori(0, NB) as b:
                    for g, blk_no in enumerate(GATES[L]):
                        wait(gate_ps, L, b, g + 1)
                        nc.scalar.copy(gate_rows[:, blk_no, :], bank[:, X, 0:C]).then_inc(gate_ok.sem, 1)
                    wait(kx_ps, L, b, 1)
                    kv = VECS[f"kx{L}"][1]
                    for m in range(KC):
                        i = act(kxT[:, m, :], bank[:, X, m * S2:(m + 1) * S2], ACT.Identity, bias=vecs[:, kv + m:kv + m + 1])
                    i.then_inc(kx_ok.sem, 1)
                    for h in range(2):
                        to_feature(L, b, 0, h, A + h)
                    qv = VECS[f"qk{L}"][1]
                    for i4 in range(4):
                        wait(qk_ps, L, b, i4 + 1)
                        if i4 >= 2:
                            ac.wait_ge(d_split[i4 % 2], split_done(L, b, i4 % 2, 1))
                        m = qv + (i4 % 2) * KC + i4 // 2
                        act(split[:, i4 % 2, 0, :].bitcast(F32R), bank[:, B + i4, :], ACT.Identity, bias=vecs[:, m:m + 1]).then_inc(qk_hi.sem, 1)
                    for s in range(2):
                        ac.wait_ge(d_split[s], split_done(L, b, s, 2))

                    def max_high(g):
                        wait(mT_ps, L, b, g + 1)
                        if g > 0:
                            s = (g - 1) % 2
                            ac.wait_ge(d_mput[s], b * 64 + (L * NB * 64 + 32 * ((g - 1) // 2 + 1)))
                        nc.scalar.copy(m_hi.bitcast(F32R), bank[0:4, X, :]).then_inc(mT_hi.sem, 1)

                    for g in outs_in(L, 0):
                        max_high(g)
                    for step in range(NQ * KCH[L]):
                        for hp in range(2):
                            wait(st_ps, L, b, 2 * step + hp + 1)
                            if step >= 2 and hp == 0:
                                wait(p_used, L, b, step - 1)
                            act(probs[:, step % 2, 2 * hp:2 * hp + 2, :], bank[:, B + 2 * hp:B + 2 * hp + 2, :], ACT.Exp, scale=SCALE).then_inc(p_ok.sem, 1)
                        for g in outs_in(L, step):
                            if step > 0:
                                max_high(g)
                    for h in range(2):
                        to_feature(L, b, 1, h, B + h)
                    qv = VECS[f"qx{L}"][1]
                    for h in range(2):
                        wait(qx_ps, L, b, h + 1)
                        for m in range(KC):
                            i = act(qT[:, m, h * HT:(h + 1) * HT], bank[:, B + 2 + h, m * HT:(m + 1) * HT], ACT.Identity, bias=vecs[:, qv + m:qv + m + 1])
                        i.then_inc(qx_ok.sem, 1)

                    def probs_T(n):
                        t, c = n // KC, n % KC
                        wait(pxT_ps, L, b, n + 1)
                        i = nc.scalar.copy(hid[:, 4 * c:4 * c + 4, t * P:(t + 1) * P],
                                           bank[:, B + n % 2, :].rearrange("p (r t) -> p r t", r=4))
                        i.then_inc(px_ok.sem, 1)

                    mv_ = VECS[f"m1{L}"][1]
                    fn = [ACT.Silu, ACT.Gelu_apprx_tanh, ACT.Gelu][L]

                    def hidden(h, units):
                        if 0 in units:
                            wait(ox_ps, L, b, h + 1)
                        for u in units:
                            n = h * UNITS_UP[L] + u
                            wait(up_ps, L, b, n + 1)
                            for e in range(1 if L == 0 else 2):
                                m = u if L == 0 else 2 * u + e
                                i = act(hid[:, m, h * HT:(h + 1) * HT], bank[:, B + 2 + n % 2, e * HT:(e + 1) * HT], fn, bias=vecs[:, mv_ + m:mv_ + m + 1])
                            i.then_inc(act_ok.sem, 1)

                    for n in range(NCT):
                        if L == 0:
                            wait(sx_ps, L, b, n + 1)
                            if n > 0:
                                wait(sx_max, L, b, n)
                            nc.scalar.copy(score_sb, bank[:, A + n % 2, :]).then_inc(sx_sb.sem, 1)
                            if n == 6:
                                to_feature(L, b, 2, 0, X)
                                hidden(0, range(2))
                            if n == 7:
                                hidden(0, range(2, UNITS_UP[L]))
                        wait(sx_max, L, b, n + 1)
                        e = exp_sb if L == 0 else p_tm[n % 2]
                        act(e, e, ACT.Exp, scale=SCALE).then_inc(ex_ok.sem, 1)
                        if n > 0:
                            probs_T(n - 1)
                    probs_T(NCT - 1)
                    if L > 0:
                        to_feature(L, b, 2, 0, X)
                        hidden(0, range(UNITS_UP[L]))
                    to_feature(L, b, 2, 1, X)
                    hidden(1, range(UNITS_UP[L]))
            L = 3
            ac.dma_start(router_in[:, :], a["L3_xcond_router_b"].rearrange("(e o) -> e o", o=1), allow_slow_non_contiguous=True).then_inc(d_rb, 16)
            ac.wait_ge(y_ps.sem, y_ps.end(2))
            load_late(ac, 3)
            for e in range(NX):
                ac.dma_start(w1_anchor[e], kxn(a["L3_xcond_e_w1"][e, 4 * P:6 * P, :])).then_inc(d_anchor, 16)
            ac.dma_start(g1_anchor, kxn(a["L3_xcond_gate_w1"][4 * P:6 * P, :])).then_inc(d_anchor, 16)
            with ac.Fori(0, NB) as b:
                wait(kx_ps, L, b, 1)
                nc.scalar.copy(kxT[:, :, :], bank[:, X, 0:KC * S2].rearrange("p (k s) -> p k s", k=KC)).then_inc(kx_ok.sem, 1)
                for h in range(2):
                    to_feature(L, b, 0, h, A + h)
                for m in range(KC):
                    wait(qx_ps, L, b, m + 1)
                    nc.scalar.copy(qT[:, m, :], bank[:, B + m, :]).then_inc(qx_ok.sem, 1)
                wait(sx_max, L, b, 1)
                for t in range(NT):
                    i = act(p_tm3[:, t, :], bank[:, A, t * S2:(t + 1) * S2], ACT.Exp, bias=sm[:, 1, t:t + 1], scale=float(C) ** -0.5,
                            accum_out=sm[:, 2, t:t + 1])
                i.then_inc(ex_ok.sem, 1)
                wait(pxT_ps, L, b, 1)
                nc.scalar.copy(pT3[0:S2, :], bank[0:S2, X, :]).then_inc(px_ok.sem, 1)
                for m in range(KC):
                    wait(ev_ps, L, b, m + 1)
                    nc.scalar.copy(evT[:, m, :], bank[:, B + m, :]).then_inc(ev_ok.sem, 1)
                wait(rl_ps, L, b, 1)
                act(logT, bank[0:NX, X, :], ACT.Identity, bias=router_now[:, :]).then_inc(rl_ok.sem, 1)
                wait(rm_ok, L, b, 1)
                act(pr[:, :, :], lg[:, :, :], ACT.Exp).then_inc(re_ok.sem, 1)
                for m in range(NX * RC + 2):
                    wait(up_ps, L, b, m + 1)
                    if m < NX * RC:
                        e = m // RC
                        if e >= 2 and m % RC == 0:
                            wait(ex_out, L, b, 2 * (e - 1))
                        dst = hid[:, (e % 2) * RC + m % RC, :]
                    else:
                        dst = uT[:, m - NX * RC, :]
                    act(dst, bank[:, B + m % 4, :], ACT.Silu, bias=anchor_now[:, m:m + 1]).then_inc(act_ok.sem, 1)
                for k in range(KC):
                    wait(rT_ps, L, b, k + 1)
                    nc.scalar.copy(hT[:, k, :], bank[:, B + k, :]).then_inc(rT_ok.sem, 1)
                wait(gs_in, L, b, 1)
                act(g_tm, g_tm, ACT.Sigmoid).then_inc(gs_ok.sem, 1)

        @blk.vector
        def _(dv):
            n = [0]
            V = nc.vector

            def link(ins):
                n[0] += 1
                ins.then_inc(dve_chain, 1)
                dv.wait_ge(dve_chain, n[0])

            def fresh():
                n[0] = 0
                dv.sem_clear(dve_chain)

            def wait(s, L, b, k):
                dv.wait_ge(s.sem, s.at(L, b, k))

            def apart():
                dv.sem_inc(apart_dve, 1)

            dv.sem_inc(ox_ok.sem, 1)
            dv.sem_inc(y_ok.sem, 1)
            dv.sem_inc(f_ok.sem, 1)
            dv.wait_ge(consts, 1)
            for s in range(SLOTS):
                link(V.tensor_scalar(k_stack[0:KS, s, :, :].rearrange("p h (a t) -> p (h a) t", a=2), zeros[0:KS, :].unsqueeze(1).to_broadcast([KS, 8, C]), 1.0, None, ALU.add))
            for s in range(SLOTS):
                link(V.tensor_copy(q_stack[0:KS, s, :, :].rearrange("p h (a t) -> p (h a) t", a=2), zeros[0:KS, :].unsqueeze(1).to_broadcast([KS, 8, C])))
            link(V.tensor_scalar(one_row[:, :], zeros[:, 0:P], ident[:, 0:1], None, ALU.add))
            dv.wait_ge(d_mask, 16)
            link(V.tensor_copy(mask_row[:, :, :], zeros[:, 0:NB * S2].rearrange("p (b s) -> p b s", b=NB)))
            link(V.tensor_scalar(mask_row[0:1, :, :], mrow_words[:, :].bitcast(U8).rearrange("p (b s) -> p b s", b=NB), MASKED, None, ALU.mult))
            V.memset(sm[:, :, :], 0.0).then_inc(const_r, 1)
            dv.wait_ge(d_ctx, 16)
            for g in range(2):
                link(V.bn_stats(stats[:, g, :], ctx_tm[:, g, :]))
            link(V.bn_aggr(mv[:, 0, :], stats[:, 0, :]))
            V.bn_aggr(mv[:, 1, :], stats[:, 1, :]).then_inc(ctx_var, 1)
            dv.wait_ge(ctx_rstd, 1)
            for g in range(2):
                i = V.tensor_scalar(ctx_tm[:, 2 + g, :], ctx_tm[:, g, :], mv[:, g, 0:1], rstd[:, g:g + 1], ALU.subtract, ALU.mult)
                if g == 0:
                    link(i)
            i.then_inc(ctx_n, 1)
            dv.wait_ge(vecs_ok, 1)
            for L in range(3):
                dv.wait_ge(ada_ps, L + 1)
                av = VECS[f"ada{L}"][1]
                ms = mod[:, ADA_AT[L]:ADA_AT[L] + ADA[L], :]
                link(V.tensor_tensor(ms, bank[:, B + L, 0:ADA[L] * NB].rearrange("p (m b) -> p m b", b=NB),
                                     vecs[:, av:av + ADA[L]].unsqueeze(2).to_broadcast([P, ADA[L], NB]), ALU.add))
                for j in range(3):
                    if SCALE_OF[L][j] is not None:
                        sc = ADA_AT[L] + SCALE_OF[L][j]
                        link(V.tensor_scalar(mod[:, sc:sc + KC, :], mod[:, sc:sc + KC, :], 1.0, None, ALU.add))
            dv.wait_ge(ctx_ok, 4)
            dv.wait_ge(d_x, 16 * 3 * NB)

            def moments(L, b, j, h, xv):
                for t in (2 * h, 2 * h + 1):
                    V.bn_stats(stats[:, t, :], xv[:, t, :]).then_inc(dve_chain, 1)
                n[0] += 2
                dv.wait_ge(dve_chain, n[0])
                link(V.bn_aggr(mv[:, 2 * h, :], stats[:, 2 * h, :]))
                V.bn_aggr(mv[:, 2 * h + 1, :], stats[:, 2 * h + 1, :]).then_inc(ln_var.sem, 1)

            def normalise(L, b, j, h, xv):
                wait(ln_rstd, L, b, 2 * j + h + 1)
                for t in (2 * h, 2 * h + 1):
                    i = V.tensor_scalar(xn[:, t, :], xv[:, t, :], mv[:, t, 0:1], rstd[:, t:t + 1], ALU.subtract, ALU.mult)
                i.then_inc(xn_ok.sem, 1)

            def norms(L, b, j, xv):
                for h in range(2):
                    moments(L, b, j, h, xv)
                for h in range(2):
                    normalise(L, b, j, h, xv)

            def residual(L, b, j, h, bk, xv):
                if j > 0:
                    wait(xb_ok, L, b, 2 * (j - 1) + h + 1)
                wait(y_ps, L, b, 2 * j + h + 1)
                ps = bank[:, bk, :].rearrange("p (t c) -> p t c", t=2)
                xh = xv[:, 2 * h:2 * h + 2, :]
                if j in GATES[L]:
                    link(V.tensor_tensor(ps, ps, gate_rows[:, j, :].unsqueeze(1).to_broadcast([P, 2, C]), ALU.mult))
                link(V.tensor_tensor(xh, ps, xh, ALU.add))
                dv.sem_inc(y_ok.sem, 1)

            for L in range(3):
                w = W[L]
                dv.wait_ge(d_w[L], 16 * N_LOADS[L])
                fresh()
                with dv.Fori(0, NB) as b:
                    xv = x_all[:, bass.ds(b * (NT * C), NT * C)].rearrange("p (t c) -> p t c", t=NT)
                    V.tensor_copy(mod_now[:, 0:ADA[L]], mod[:, ADA_AT[L]:ADA_AT[L] + ADA[L], bass.ds(b, 1)].rearrange("p m o -> p (m o)")).then_inc(now_ok.sem, 1)
                    wait(now_ok, L, b, 1)
                    for g, blk_no in enumerate(GATES[L]):
                        gc = GATE_OF[L][blk_no]
                        if g > 0:
                            wait(gate_ps, L, b, g)
                        link(V.tensor_scalar(diag[:, 0, :], ident[:, :], mod_now[:, gc:gc + 1], None, ALU.mult))
                        V.tensor_scalar(diag[:, 1, :], ident[:, :], mod_now[:, gc + 1:gc + 2], None, ALU.mult).then_inc(diag_ok.sem, 1)
                    norms(L, b, 0, xv)
                    wait(vx_ps, L, b, 1)
                    for h in range(2):
                        ps = bank[h * S2:(h + 1) * S2, X, 0:C].rearrange("p (r e d) -> p r e d", e=2, d=HD)[:, :, h, :]
                        bv = w["bvx"].rearrange("p (r e d) -> p r e d", e=2, d=HD)[h * S2:(h + 1) * S2, :, h, :]
                        i = V.tensor_tensor(v_bd[h * S2:(h + 1) * S2, :, h * HD:(h + 1) * HD], ps, bv, ALU.add)
                        if h == 0:
                            link(i)
                    i.then_inc(vx_ok.sem, 1)
                    qv = VECS[f"qk{L}"][1]
                    for i4 in range(4):
                        wait(qk_hi, L, b, i4 + 1)
                        m = qv + (i4 % 2) * KC + i4 // 2
                        V.scalar_tensor_tensor(out=split[:, i4 % 2, 1, :].bitcast(F32R), in0=bank[:, B + i4, :], scalar=vecs[:, m:m + 1],
                                               in1=split[:, i4 % 2, 0, :], op0=ALU.add, op1=ALU.subtract).then_inc(qk_lo.sem, 1)
                    for h in range(2):
                        wait(v_ps, L, b, h + 1)
                        for t in range(2):
                            i = V.tensor_tensor(v_aug[:, 2 * h + t, :, 0:HD],
                                                bank[:, A + h, t * C:(t + 1) * C].rearrange("p (h d) -> p h d", d=HD),
                                                w["bv"].rearrange("p (h d) -> p h d", d=HD), ALU.add)
                            if t == 0:
                                link(i)
                        i.then_inc(v_ok.sem, 1)

                    def tile_maxima(n):
                        g, u = n // UNITS[L], n % UNITS[L]
                        wait(s_ps, L, b, n + 1)
                        if L == 0:
                            i = V.tensor_reduce(nm[:, u, 4 * g:4 * g + 4], bank[:, A + n % 2, :].rearrange("p (h s) -> p h s", h=4),
                                                AX.X, ALU.max, negate=True)
                        else:
                            h, t = 4 * g + u // 4, u % 4
                            i = V.tensor_reduce(nm[:, t, h:h + 1], bank[:, A + n % 2, :], AX.X, ALU.max, negate=True)
                        i.then_inc(s_max.sem, 1)

                    def max_low(g):
                        wait(mT_hi, L, b, g + 1)
                        if g > 0:
                            s = (g - 1) % 2
                            dv.wait_ge(d_mput[s], b * 64 + (L * NB * 64 + 32 * ((g - 1) // 2 + 1)))
                        V.tensor_tensor(m_lo.bitcast(F32R), bank[0:4, X, :], m_hi, ALU.subtract).then_inc(mT_lo.sem, 1)

                    def heads(g):
                        if g > 0:
                            wait(hd_ok, L, b, g)
                        wait(p_used, L, b, (g + 1) * KCH[L])
                        V.transpose(p_one[:, :], bank[:, O, :]).then_inc(o_ok.sem, 1)
                        wait(o_ok, L, b, g + 1)
                        blocks = p_one[:, :].rearrange("p (n d) -> p n d", d=32)
                        link(V.reciprocal(block_r[:, :].unsqueeze(2), blocks[:, :, HD:HD + 1]))
                        link(V.tensor_tensor(blocks, blocks, block_r[:, :].unsqueeze(2).to_broadcast([P, T // 32, 32]), ALU.mult))
                        V.transpose(work[:, g, :], p_one[:, :]).then_inc(hd_ok.sem, 1)

                    for step in range(NQ * KCH[L]):
                        tiles = tile_range(L, step)
                        turn = step > 0 and step % KCH[L] == 0
                        if turn and not len(tiles):
                            heads(step // KCH[L] - 1)
                        for tile in tiles:
                            tile_maxima(tile)
                            if turn and tile == tiles[min(1, len(tiles) - 1)]:
                                heads(step // KCH[L] - 1)
                            for g in due_after(L, tile, LOW_DELAY[L]):
                                max_low(g)
                    heads(NQ - 1)
                    for h in range(2):
                        residual(L, b, 0, h, A + h, xv)
                        moments(L, b, 1, h, xv)
                        normalise(L, b, 1, h, xv)

                    def hidden(h, units):
                        mv_ = VECS["m10"][1] + HIDC
                        for m in units:
                            u = h * UNITS_UP[L] + m
                            wait(act_ok, L, b, u + 1)
                            V.scalar_tensor_tensor(out=hid[:, m, h * HT:(h + 1) * HT], in0=bank[:, B + 2 + u % 2, HT:2 * HT],
                                                   scalar=vecs[:, mv_ + m:mv_ + m + 1], in1=hid[:, m, h * HT:(h + 1) * HT],
                                                   op0=ALU.add, op1=ALU.mult).then_inc(hid_ok.sem, 1)

                    def cross_tile(m):
                        if L > 0:
                            wait(sx_ps, L, b, m + 1)
                            ps = bank[:, A + m % 2, :].rearrange("p (h s) -> p h s", h=8)
                            mx = nm[:, m // KC, 8 * (m % KC):8 * (m % KC) + 8]
                            link(V.tensor_reduce(mx, ps, AX.X, ALU.max, negate=True))
                            if m >= 2:
                                wait(pxT_ps, L, b, m - 1)
                            V.tensor_tensor(p_tm[m % 2].rearrange("p (h s) -> p h s", h=8), ps,
                                            mx.unsqueeze(2).to_broadcast([P, 8, S2]), ALU.add).then_inc(sx_max.sem, 1)
                            return
                        wait(sx_sb, L, b, m + 1)
                        sc = score_sb.rearrange("p (h s) -> p h s", h=8)
                        rs = rest_sb.rearrange("p (h s) -> p h s", h=8)
                        if m > 0:
                            wait(px_tm, L, b, m)
                        apart()
                        for step in range(4):
                            for h in range(8):
                                if step == 0:
                                    i = V.max(top[:, h, 0, :], sc[:, h, :])
                                elif step == 1:
                                    i = V.match_replace(rs[:, h, :], top[:, h, 0, :], sc[:, h, :], -LARGE)
                                elif step == 2:
                                    i = V.max(top[:, h, 1, :], rs[:, h, :])
                                else:
                                    i = V.match_replace(rs[:, h, :], top[:, h, 1, :], rs[:, h, :], -LARGE)
                                i.then_inc(dve_chain, 1)
                            n[0] += 8
                            dv.wait_ge(dve_chain, n[0])
                            if m == NCT - 1:
                                hidden(0, (2 * step, 2 * step + 1))
                        V.tensor_tensor(exp_sb.rearrange("p (h s) -> p h s", h=8), sc,
                                        top[:, :, 0, 0:1].to_broadcast([P, 8, S2]), ALU.subtract).then_inc(sx_max.sem, 1)
                        wait(ex_ok, L, b, m + 1)
                        if m >= 2:
                            wait(pxT_ps, L, b, m - 1)
                        V.scalar_tensor_tensor(out=p_tm[m % 2], in0=rest_sb, scalar=-LARGE, in1=exp_sb,
                                               op0=ALU.is_equal, op1=ALU.mult).then_inc(px_tm.sem, 1)

                    def cross_heads(h):
                        wait(ox_ps, L, b, h + 1)
                        link(V.reciprocal(xsum[:, :], bank[:, X, :]))
                        V.tensor_tensor(xT[:, :, h * HT:(h + 1) * HT], bank[:, O, :].rearrange("p (k t) -> p k t", k=KC),
                                        xsum[:, :].rearrange("p (k t) -> p k t", k=KC), ALU.mult).then_inc(ox_ok.sem, 1)

                    for m in range(5):
                        cross_tile(m)
                    cross_heads(0)
                    cross_tile(5)
                    residual(L, b, 1, 0, O, xv)
                    moments(L, b, 2, 0, xv)
                    if L == 0:
                        normalise(L, b, 2, 0, xv)
                        cross_tile(6)
                        cross_tile(7)
                    else:
                        cross_tile(6)
                        normalise(L, b, 2, 0, xv)
                        cross_tile(7)
                    cross_heads(1)
                    residual(L, b, 1, 1, O, xv)
                    moments(L, b, 2, 1, xv)
                    normalise(L, b, 2, 1, xv)
                    residual(L, b, 2, 0, A, xv)
                    if L == 0:
                        hidden(1, range(UNITS_UP[L]))
                    residual(L, b, 2, 1, A + 1, xv)
                    fresh()

            L, w = 3, W[3]
            dv.wait_ge(d_w[3], 16 * N_LOADS[3])
            dv.wait_ge(anc_ps, 1)
            ev = VECS["eb1"][1]
            V.tensor_tensor(anchor_b[:, 0:NX * RC, :], bank[:, B, 0:NX * RC * NB].rearrange("p (m b) -> p m b", b=NB),
                            vecs[:, ev:ev + NX * RC].unsqueeze(2).to_broadcast([P, NX * RC, NB]), ALU.add).then_inc(dve_chain, 1)
            gv = VECS["gb1"][1]
            V.tensor_tensor(anchor_b[:, NX * RC:, :], bank[:, B, NX * RC * NB:(NX * RC + 2) * NB].rearrange("p (m b) -> p m b", b=NB),
                            vecs[:, gv:gv + 2].unsqueeze(2).to_broadcast([P, 2, NB]), ALU.add).then_inc(anc_ok, 1)
            V.tensor_copy(router_b[:, :], bank[0:NX, B + 1, 0:NB]).then_inc(anc_ok, 1)
            dv.wait_ge(anc_ok, 2)
            dv.wait_ge(dve_chain, 1)
            dv.wait_ge(d_rb, 16)
            n[0] = 1
            link(V.tensor_scalar(router_b[:, :], router_b[:, :], router_in[:, :], None, ALU.add))
            fresh()
            with dv.Fori(0, NB) as b:
                xv = x_all[:, bass.ds(b * (NT * C), NT * C)].rearrange("p (t c) -> p t c", t=NT)
                link(V.tensor_copy(anchor_now[:, :], anchor_b[:, :, bass.ds(b, 1)].rearrange("p m o -> p (m o)")))
                V.tensor_copy(router_now[:, :], router_b[:, bass.ds(b, 1)]).then_inc(now_ok.sem, 1)
                norms(L, b, 0, xv)
                wait(vx_ps, L, b, 1)
                V.tensor_copy(v3[0:S2, :], bank[0:S2, X, 0:C]).then_inc(vx_ok.sem, 1)
                wait(sx_ps, L, b, 1)
                link(V.tensor_reduce(sm[:, 0, :], bank[:, A, 0:NT * S2].rearrange("p (t s) -> p t s", t=NT), AX.X, ALU.max, negate=True))
                V.tensor_scalar(sm[:, 1, :], sm[:, 0, :], float(C) ** -0.5, None, ALU.mult).then_inc(sx_max.sem, 1)
                wait(ex_ok, L, b, 1)
                link(V.reciprocal(sm[:, 3, :], sm[:, 2, :]))
                V.tensor_tensor(p_tm3, p_tm3, sm[:, 3, :].unsqueeze(2).to_broadcast([P, NT, S2]), ALU.mult).then_inc(px_tm.sem, 1)
                wait(rlT_ps, L, b, 1)
                link(V.tensor_copy(lg[:, :, :], bank[:, X, 0:NT * NX].rearrange("p (t e) -> p t e", t=NT)))
                link(V.tensor_reduce(sm[:, 4, :], lg[:, :, :], AX.X, ALU.max))
                V.tensor_tensor(lg[:, :, :], lg[:, :, :], sm[:, 4, :].unsqueeze(2).to_broadcast([P, NT, NX]), ALU.subtract).then_inc(rm_ok.sem, 1)
                wait(re_ok, L, b, 1)
                link(V.tensor_reduce(sm[:, 5, :], pr[:, :, :], AX.X, ALU.add))
                link(V.reciprocal(sm[:, 5, :], sm[:, 5, :]))
                link(V.tensor_tensor(pr[:, :, :], pr[:, :, :], sm[:, 5, :].unsqueeze(2).to_broadcast([P, NT, NX]), ALU.mult))
                for e in range(NX):
                    for t in range(NT):
                        if e == 0:
                            V.tensor_scalar(xn[:, t, :], w["b2"][:, 0, :], pr[:, t, 0:1], None, ALU.mult).then_inc(dve_chain, 1)
                        else:
                            V.scalar_tensor_tensor(out=xn[:, t, :], in0=w["b2"][:, e, :], scalar=pr[:, t, e:e + 1], in1=xn[:, t, :],
                                                   op0=ALU.mult, op1=ALU.add).then_inc(dve_chain, 1)
                    n[0] += NT
                    dv.wait_ge(dve_chain, n[0])
                for e in range(NX):
                    for h in range(2):
                        wait(ex_out, L, b, 2 * e + h + 1)
                        if e > 0:
                            wait(acc_ok, L, b, 2 * (e - 1) + h + 1)
                        for t in (2 * h, 2 * h + 1):
                            i = V.scalar_tensor_tensor(out=xn[:, t, :], in0=bank[:, A + h, (t % 2) * C:(t % 2 + 1) * C], scalar=pr[:, t, e:e + 1],
                                                       in1=xn[:, t, :], op0=ALU.mult, op1=ALU.add)
                            if t % 2 == 0:
                                link(i)
                        i.then_inc(acc_ok.sem, 1)
                for h in range(2):
                    wait(g_ps, L, b, h + 1)
                    i = V.tensor_tensor(g_tm[:, 2 * h:2 * h + 2, :], bank[:, A + h, :].rearrange("p (t c) -> p t c", t=2),
                                        w["gb2"].unsqueeze(1).to_broadcast([P, 2, C]), ALU.add)
                    if h == 0:
                        link(i)
                i.then_inc(gs_in.sem, 1)
                wait(gs_ok, L, b, 1)
                for h in range(2):
                    wait(f_ps, L, b, h + 1)
                    ps = bank[:, A + h, :].rearrange("p (t c) -> p t c", t=2)
                    xh = xv[:, 2 * h:2 * h + 2, :]
                    link(V.tensor_tensor(ps, ps, w["ob"].unsqueeze(1).to_broadcast([P, 2, C]), ALU.add))
                    link(V.tensor_tensor(ps, ps, g_tm[:, 2 * h:2 * h + 2, :], ALU.mult))
                    i = V.tensor_tensor(xh, ps, xh, ALU.add)
                    if h == 0:
                        link(i)
                i.then_inc(f_ok.sem, 1)
                fresh()


_OUT = (NB, T, C)


def kernel(**inputs):
    import concourse.bacc as bacc
    from concourse.bass_utils import run_bass_kernel_spmd as run

    nc = bacc.Bacc("TRN2", target_bir_lowering=False, num_devices=1)
    arrays, aps = {}, {}
    for name, v in inputs.items():
        v = np.ascontiguousarray(v)
        if v.dtype == np.bool_:
            v = v.view(np.uint32)
        arrays[f"in_{name}"] = v
        aps[name] = nc.dram_tensor(f"in_{name}", v.shape, mybir.dt.from_np(v.dtype), kind="ExternalInput").ap()
    out = nc.dram_tensor("out_x", _OUT, F32, kind="ExternalOutput").ap()
    build(nc, aps, out)
    r = run(nc, [arrays], core_ids=[0])
    return r.results[0]["out_x"]
```

```python
from contextlib import ExitStack

import numpy as np

import concourse.bass as bass
from concourse import mybir

F32 = mybir.dt.float32
F32R = mybir.dt.float32r
U8 = mybir.dt.uint8
U32 = mybir.dt.uint32
ALU = mybir.AluOpType
ACT = mybir.ActivationFunctionType
AX = mybir.AxisListType

P = 128
NB, T, C = 4, 512, 256
NT, KC = T // P, C // P
NH, HD = 16, 16
NQ = NH // 4
S2 = 64
SHIFT, TOPK = 64, 16
SCALE = float(HD) ** -0.5
LARGE = float(np.float32(3.0e38))
MASKED = -1.0e30
EPS = [1e-6, 1e-6, 1e-6, 1e-5]
NX = 3
RH = 512
RC = RH // P

VECS = {}
_at = 0
for _name, _inp, _first, _n in [
    ("ada0", "L0_xcond_b_ada", 0, 18), ("qk0", "L0_xcond_b_qkv", 0, 4), ("qx0", "L0_xcond_b_q", 0, 2),
    ("kx0", "L0_xcond_b_kv", 0, 2), ("m10", "L0_xcond_b_m1", 0, 16),
    ("ada1", "L1_xcond_b_mod", 0, 12), ("qk1", "L1_xcond_b_qkv", 0, 4), ("qx1", "L1_xcond_b_qc", 0, 2),
    ("kx1", "L1_xcond_b_kvc", 0, 2), ("m11", "L1_xcond_b_mlp1", 0, 8),
    ("ada2", "L2_xcond_ada_b", 0, 12), ("qk2", "L2_xcond_qkv_b", 0, 4), ("qx2", "L2_xcond_q_b", 0, 2),
    ("kx2", "L2_xcond_kv_b", 0, 2), ("m12", "L2_xcond_fc1_b", 0, 8),
    ("gamma", "L3_xcond_ln_gamma", 0, 2), ("beta", "L3_xcond_ln_beta", 0, 2),
    ("gb1", "L3_xcond_gate_b1", 0, 2), ("eb1", "L3_xcond_e_b1", 0, NX * RC), ("cond", "cond_1024", 0, NB * KC),
]:
    VECS[_name] = (_inp, _at, _n)
    _at += _n
NVEC = _at
assert NVEC <= P

ADA = [18, 12, 12]
ADA_AT = [0, 18, 30]
SHIFT_OF = [(0, 6, 12), (0, None, 6), (0, None, 6)]
SCALE_OF = [(2, 8, 14), (2, None, 8), (2, None, 8)]
GATE_OF = [(4, 10, 16), (4, None, 10), (4, None, 10)]
GATES = [[0, 1, 2], [0, 2], [0, 2]]
HIDC = 8
UP = [16, 8, 8]

UNITS = [4, 16, 16]
KCH = [1, 4, 4]
HT = T // 2
UNITS_UP = [8, 4, 4]
NCT = NT * KC
EARLY = 1536 + NQ * C + 2 * C + 4 * C + 2 * C + 4 * C
EARLY1 = EARLY + UP[0] * KC * P + HIDC * C
WORDS = EARLY1 + EARLY
SLOTS = 3
KS = 96
MAX_ROW = 64
LEAD = [3, 7, 7]
OUT_DELAY, LOW_DELAY = [1, 1, 1], [1, 2, 1]
SHARES = [
    {"moments_a": 1.146, "norm_a": 0.6, "input_a": 0.5, "qk": 2.49, "v": 1.313, "split_done": 2.383, "heads": 1.143,
     "last_heads": 2, "maxima": 0.3, "diag": 0.1, "gate": 1.279, "keys_x": 1.2, "values_x": 0.964, "out_s": 1.8,
     "norm_x0": 1, "norm_x1": 3.454, "input_x": 1.257, "query_x": 5.384, "probs_x": 1.2, "heads_x": 10.147,
     "out_x": 4.5, "norm_mlp": 0.636, "input_mlp": 1.949, "up": 1.7, "moments_x": 0.357, "scores_x": 1.2,
     "top_x": 6.443, "exp_x": 1, "tile": 0.898, "keys": 1.7, "weigh": 1.042, "down": 1.7},
    {"moments_a": 0.82, "norm_a": 1.017, "input_a": 0.5, "qk": 1.438, "v": 1.448, "split_done": 1.02, "heads": 1,
     "last_heads": 1.792, "maxima": 0.3, "diag": 0.109, "gate": 1.308, "keys_x": 1.147, "values_x": 1.2,
     "out_s": 1.8, "norm_x0": 0.671, "norm_x1": 0.815, "input_x": 1.5, "query_x": 2.314, "probs_x": 0.641,
     "heads_x": 7.784, "out_x": 6.597, "norm_mlp": 1, "input_mlp": 1.5, "up": 1.764, "moments_x": 0.453,
     "scores_x": 1.2, "top_x": 5, "exp_x": 1, "tile": 0.852, "keys": 1.351, "weigh": 1.363, "down": 1.849},
]
SHARES.append(SHARES[1])


def tiles_before(L, step):
    return min(NQ * UNITS[L], UNITS[L] * (step // KCH[L] + 1) + (step % KCH[L]) * UNITS[L] // KCH[L] + LEAD[L])


def due_after(L, n, delay):
    return [g for g in range(NQ) if n == min(NQ * UNITS[L] - 1, (g + 1) * UNITS[L] - 1 + delay)]


def attention_stages(L):
    share = SHARES[L]
    out = [("now", 0, 0.1)] + [("moments_a", h, share["moments_a"]) for h in range(2)] + [("norm_a", h, share["norm_a"]) for h in range(2)]
    out += [("input_a", h, share["input_a"]) for h in range(2)]
    out += [(stage, n, share[stage]) for stage, n in (("qk", 0), ("qk", 1), ("v", 0), ("v", 1), ("qk", 2), ("qk", 3), ("split_done", 0))]

    def tiles(r):
        for n in r:
            out.append(("tile", n, share["tile"]))
            out.extend(("max_out", g, share["maxima"]) for g in due_after(L, n, OUT_DELAY[L]))
            out.extend(("max_low", g, share["maxima"]) for g in due_after(L, n, LOW_DELAY[L]))

    tiles(range(tiles_before(L, 0)))
    steps = NQ * KCH[L]
    for step in range(steps):
        now, later = tiles_before(L, step), tiles_before(L, step + 1) if step + 1 < steps else tiles_before(L, step)
        mid = (now + later) // 2
        out.append(("keys", (step, 0), share["keys"]))
        if step > 0 and step % KCH[L] == 0:
            out.append(("heads", step // KCH[L] - 1, share["heads"]))
        tiles(range(now, mid))
        out.append(("keys", (step, 1), share["keys"]))
        tiles(range(mid, later))
        out.append(("weigh", step, share["weigh"]))
    out.append(("heads", NQ - 1, share["last_heads"]))
    return out


def rest_stages(L):
    share = SHARES[L]
    out = [("now_r", 0, 0.1)] + [("diag", g, share["diag"]) for g in range(len(GATES[L]))]
    out += [("gate", g, share["gate"]) for g in range(len(GATES[L]))]
    out += [("keys_x", 0, share["keys_x"]), ("values_x", 0, share["values_x"])]
    out += [("out_s", (h, t), share["out_s"]) for h in range(2) for t in range(2)] + [("norm_r", (1, 0), share["norm_x0"])]
    for h in range(2):
        if h == 1:
            out.append(("norm_r", (1, 1), share["norm_x1"]))
        out += [("input_r", (1, h), share["input_x"]), ("query_x", h, share["query_x"])]
        for n in range(4 * h, 4 * h + 4):
            if n == 4 * h:
                out += [("scores_x", n, share["scores_x"])]
            out += [("top_x", n, share["top_x"])] if L == 0 else []
            if n < 4 * h + 3:
                out += [("scores_x", n + 1, share["scores_x"])]
            out += [("exp_x", n, share["exp_x"]), ("probs_x", n, share["probs_x"])]
        out += [("heads_x", h, share["heads_x"]), ("out_x", h, share["out_x"])]
        out += [("norm_r", (2, h), share["norm_mlp"]), ("input_r", (2, h), share["input_mlp"])]
        out += [("up", h, share["up"] * UNITS_UP[L])]
        if h == 0:
            out.append(("moments_r", (1, 1), share["moments_x"]))
        out += [("down", (h, t, part), share["down"]) for t in range(2) for part in range(2)]
    return out


def stage_order(first, second):
    out, i, j = [], 0, 0
    all_first, all_second = sum(x[2] for x in first), sum(x[2] for x in second)
    at_first = at_second = 0.0
    while i < len(first) or j < len(second):
        if j >= len(second) or (i < len(first) and at_first * all_second <= at_second * all_first):
            out.append(first[i][:2])
            at_first += first[i][2]
            i += 1
        else:
            out.append(second[j][:2])
            at_second += second[j][2]
            j += 1
    return out


def times(b, n, more=0):
    register, ahead = b if isinstance(b, tuple) else (b, 0)
    return register * n + (ahead * n + more)


def batch_of(b, n):
    return slice(b * n, (b + 1) * n) if isinstance(b, int) else bass.ds(times(b, n), n)


class Signal:

    def __init__(self, sem, per, first=0):
        self.sem, self.per, self.first = sem, per, first

    def at(self, layer, b, k):
        base = self.first + sum(NB * n for n in self.per[:layer])
        assert base + k > 0
        return times(b, self.per[layer], base + k)

    def end(self, layer):
        return self.first + sum(NB * n for n in self.per[: layer + 1])


def build(nc, a, out):
    with ExitStack() as ctx:
        def sb(name, shape, dt=F32):
            return ctx.enter_context(nc.sbuf_tensor(name, shape, dt))

        def sem(name):
            return ctx.enter_context(nc.semaphore(name))

        def sig(name, *per, first=0):
            return Signal(sem(name), per, first)

        x_all = sb("x_all", [P, NB * NT * C])
        weights = sb("weights", [P, WORDS])
        q_stack = sb("q_stack", [P, SLOTS, 4, T], F32R)
        k_stack = sb("k_stack", [P, SLOTS, 4, T], F32R)
        probs = sb("probs", [P, 4, T])
        hid = sb("hid", [P, 8, HT])
        p_tm_all = sb("p_tm_all", [P, 2, T])
        work = sb("work", [P, 4, T])
        hT = sb("hT", [P, KC, T])
        hR = sb("hR", [P, KC, HT])
        xn = sb("xn", [P, NT, C])
        v_aug = sb("v_aug", [P, NT, NH, 2 * HD])
        k_bd = sb("k_bd", [P, KC, 8, S2])
        v_bd = sb("v_bd", [P, 8, 2 * HD])
        gate_rows = sb("gate_rows", [P, 3, C])
        bg_rows = sb("bg_rows", [P, 2, C])
        ident = sb("ident", [P, P])
        ones = sb("ones", [P, P])
        zeros = sb("zeros", [P, C])
        ones_pair = sb("ones_pair", [P, 2 * HD])
        head_mask = sb("head_mask", [P, 8])
        vec_rows = hT[:, 0, 0:P]
        vecs = sb("vecs", [P, NVEC])
        cond_s = sb("cond_s", [P, KC, NB])
        cond_r = sb("cond_r", [P, KC, NB])
        mod = sb("mod", [P, sum(ADA), NB])
        mod_now = sb("mod_now", [P, 18])
        ctx_tm = xn
        ctxT = sb("ctxT", [P, 2, KC, NB * S2])
        ctx_two = sb("ctx_two", [P, KC, 2, S2])
        kxT = sb("kxT", [P, KC, S2])
        stats = sb("stats", [P, NT, 6])
        mv = sb("mv", [P, NT, 2])
        var_eps = sb("var_eps", [P, NT])
        rstd = sb("rstd", [P, NT])
        half_neg = sb("half_neg", [P, NT])
        block_r = sb("block_r", [P, T // 32])
        nm = sb("nm", [P, NT, NH])
        diag = [p_tm_all[:, i // 2, (i % 2) * C:(i % 2 + 1) * C].rearrange("p (k n) -> p k n", k=KC) for i in range(3)]
        stats_r = sb("stats_r", [P, NT, 6])
        mv_r = sb("mv_r", [P, NT, 2])
        var_eps_r = sb("var_eps_r", [P, NT])
        rstd_r = sb("rstd_r", [P, NT])
        nm_x = sb("nm_x", [P, 8])
        mod_rest = sb("mod_rest", [P, 18])
        top = sb("top", [P, 8, 2, 8])
        mrow_words = sb("mrow_words", [1, NB * S2 // 4], U32)
        mask_row = sb("mask_row", [P, NB, S2], F32R)
        one_row = sb("one_row", [P, P], F32R)
        anchor_b = sb("anchor_b", [P, 14, NB])
        anchor_now = sb("anchor_now", [P, 14])
        router_b = sb("router_b", [NX, NB])
        router_now = sb("router_now", [NX, 1])
        router_diag = sb("router_diag", [NX, NX])
        router_in = sb("router_in", [NX, 1])
        lg = sb("lg", [P, NT, NX])
        pr = sb("pr", [P, NT, NX])
        sm = sb("sm", [P, 6, NT])

        bank = ctx.enter_context(nc.psum_tensor("bank", [P, 8, T], F32))
        S, K, R, O, X = 0, 2, 4, 6, 7
        A, B = 0, 2

        def place(at, *shape):
            n = int(np.prod(shape))
            v = weights[:, at:at + n]
            if len(shape) == 2:
                v = v.rearrange("p (k n) -> p k n", k=shape[0])
            if len(shape) == 3:
                v = v.rearrange("p (e k n) -> p e k n", e=shape[0], k=shape[1])
            return v, at + n

        W = [dict() for _ in range(4)]
        for L in range(3):
            at = (0, EARLY1, 0)[L]
            for name, shape in [("qkv", (KC, 3 * C)), ("so", (NQ, C)), ("qx", (KC, C)), ("kvx", (KC, 2 * C)),
                                ("co", (KC, C)), ("bv", (C,)), ("bvx", (C,)), ("bco", (C,)), ("bm2", (C,))]:
                W[L][name], at = place(at, *shape)
            assert at == (0, EARLY1, 0)[L] + EARLY
            if L == 1:
                at = EARLY
            if L == 2:
                at = EARLY + 2 * 2048
            W[L]["m1"], at = place(at, KC, UP[L] * P)
            if L == 2:
                at = EARLY1
            W[L]["m2"], at = place(at, HIDC, C)
        at = EARLY
        for name, shape in [("q", (KC, C)), ("k", (KC, C)), ("v", (KC, C)), ("g1", (4, C)), ("g2", (KC, C)), ("o", (KC, C)),
                            ("gb2", (C,)), ("ob", (C,))]:
            W[3][name], at = place(at, *shape)
        assert at <= EARLY + 2 * 2048
        at = EARLY1 + 2048
        for name, shape in [("w1_0", (4, RH)), ("r", (6, NX)), ("b2", (NX, C))]:
            W[3][name], at = place(at, *shape)
        assert at <= WORDS
        W[3]["w2"], at = place(0, NX, RC, C)
        assert at <= EARLY
        at = EARLY + 2 * 2048
        for e in (1, 2):
            W[3][f"w1_{e}"], at = place(at, 4, RH)
        assert at <= EARLY1 + 2048
        pf = probs[:, :, :].rearrange("p a t -> p (a t)")
        hf = hid[:, :, :].rearrange("p a t -> p (a t)")
        wf = work[:, :, :].rearrange("p a t -> p (a t)")
        vf = v_aug[:, :, :, :].rearrange("p a b t -> p (a b t)")
        n0, n1 = ADA[0] * P, ADA[1] * P
        spare = weights[:, EARLY1:WORDS]
        ada_w = [[spare[:, 0:n0], spare[:, n0:2 * n0]], [pf[:, 0:n1], hf[:, 0:n1]], [wf[:, 0:n1], vf[:, 0:n1]]]
        assert 2 * n0 <= EARLY and n1 <= 4 * T
        anchor_of = lambda v, i: v[:, i * KC * RH:(i + 1) * KC * RH].rearrange("p (k n) -> p k n", k=KC)
        w1_anchor = [anchor_of(pf, 0), anchor_of(pf, 1), anchor_of(vf, 0)]
        g1_anchor = vf[:, KC * RH:KC * RH + KC * C].rearrange("p (k n) -> p k n", k=KC)

        split = pf.rearrange("p (r s t) -> p r s t", r=2, s=2)
        hid3 = [probs, hf.rearrange("p (m t) -> p m t", m=4)]
        score_sb = hR[:, :, :].rearrange("p k t -> p (k t)")
        rest_sb = sb("rest_sb", [P, T])
        xT = hR
        evT = work[:, 0:2, :]
        uT = work[:, 2:4, :]
        xf = xn[:, :, :].rearrange("p t c -> p (t c)")
        m_hi, m_lo = hT[0:4, 0, :], hT[0:4, 1, :]
        qT = sb("qT", [P, KC, HT])
        wqT = qT[:, :, :].rearrange("p k t -> p (k t)").rearrange("p (m c) -> p m c", m=KC)
        kqT = rest_sb[:, 0:KC * S2].rearrange("p (k s) -> p k s", k=KC)
        g_tm = k_bd[:, :, :, :].rearrange("p k h s -> p (k h s)").rearrange("p (t c) -> p t c", t=NT)
        p_one = sb("p_one", [P, T])
        p_tm = [p_tm_all[:, 0, :], p_tm_all[:, 1, :]]
        xsum = p_tm[0]
        p_tm3 = p_one[:, 0:NT * S2].rearrange("p (t s) -> p t s", t=NT)
        pT3 = p_tm[1]
        v3 = v_aug[:, 0, :, :].rearrange("p h d -> p (h d)")[:, 0:C]

        q_scratch = nc.dram_tensor("q_scratch", [KC, P, 2, T], F32, kind="Internal").ap()
        k_scratch = nc.dram_tensor("k_scratch", [KC, P, 2, T], F32, kind="Internal").ap()
        kl_scratch = nc.dram_tensor("kl_scratch", [KC, P, T], F32, kind="Internal").ap()
        m_scratch = nc.dram_tensor("m_scratch", [2, 2, 4, T], F32, kind="Internal").ap()
        q_src = q_scratch.rearrange("c (h d) s t -> c (d s) h t", d=HD)
        q_hi_src = q_scratch.rearrange("c (h d) s t -> c s d h t", d=HD)
        k_src = k_scratch.rearrange("c (h d) s t -> c (d s) h t", d=HD)
        kl_src = kl_scratch.rearrange("c (h d) t -> c d h t", d=HD)

        d_vecs = sem("d_vecs"); d_ctx = sem("d_ctx"); d_x = sem("d_x"); d_mask = sem("d_mask")
        d_ada = [sem(f"d_ada{i}") for i in range(3)]
        d_w = [sem(f"d_w{i}") for i in range(4)]
        d_late = [sem(f"d_late{i}") for i in range(4)]
        d_anchor = sem("d_anchor")
        d_split = [sem("d_split0"), sem("d_split1")]; d_stack = [sem(f"d_stack{i}") for i in range(SLOTS)]
        d_mput = [sem("d_mput0"), sem("d_mput1")]; d_mget = [sem(f"d_mget{i}") for i in range(SLOTS)]
        d_out = sem("d_out")
        pool_chain = sem("pool_chain"); dve_chain = sem("dve_chain"); act_chain = sem("act_chain")
        apart_pe = sem("apart_pe"); apart_pool = sem("apart_pool"); apart_dve = sem("apart_dve"); apart_sp = sem("apart_sp")
        consts = sem("consts"); const_r = sem("const_r")
        vecs_ps = sem("vecs_ps"); vecs_ok = sem("vecs_ok"); cond_ok = sem("cond_ok")
        ctx_ps = sem("ctx_ps"); ctx_ok = sem("ctx_ok"); ctx_var = sem("ctx_var"); ctx_rstd = sem("ctx_rstd")
        ctx_n = sem("ctx_n")
        ada_ps = sem("ada_ps"); ada_ok = sem("ada_ok"); v_ones = sem("v_ones")
        so_zero = sem("so_zero")
        anc_ps = sem("anc_ps"); anc_ok = sem("anc_ok")
        d_rb = sem("d_rb")

        def stack_done(L, b, g):
            uses = len(range(g % SLOTS, NQ, SLOTS))
            return times(b, uses * 80, L * NB * uses * 80 + 80 * (g // SLOTS + 1))

        def mget_done(L, b, g):
            uses = len(range(g % SLOTS, NQ, SLOTS))
            return times(b, uses * 16, L * NB * uses * 16 + 16 * (g // SLOTS + 1))

        def mput_done(L, b, g):
            return times(b, 64, L * NB * 64 + 32 * (g // 2 + 1))

        def split_done(L, b, q_or_k, half):
            each = 16 * (1 + q_or_k)
            return times(b, 2 * each, L * NB * 2 * each + each * half)

        now_ok = sig("now_ok", 1, 1, 1, 1)
        var_a = sig("var_a", 2, 2, 2, 2)
        rstd_a = sig("rstd_a", 2, 2, 2, 2)
        xa_ok = sig("xa_ok", 2, 2, 2, 2)
        aT_ps = sig("aT_ps", 2, 2, 2, 2)
        ha_ok = sig("ha_ok", 2, 2, 2, 2)
        var_r = sig("var_r", 4, 4, 4, 0)
        rstd_r_ok = sig("rstd_r_ok", 4, 4, 4, 0)
        xr_ok = sig("xr_ok", 4, 4, 4, 0)
        rT_in = sig("rT_in", 4, 4, 4, 0, first=1)
        hr_ok = sig("hr_ok", 4, 4, 4, 0)
        nth = lambda j, h: 2 * h + j
        now_r_ok = sig("now_r_ok", 1, 1, 1, 0)
        diag_ok = sig("diag_ok", 1, 1, 1, 0)
        gate_ps = sig("gate_ps", 3, 2, 2, 0)
        gate_ok = sig("gate_ok", 3, 2, 2, 0)
        bg_ok = sig("bg_ok", 2, 1, 1, 0)
        qk_ps = sig("qk_ps", 4, 4, 4, 0)
        qk_hi = sig("qk_hi", 4, 4, 4, 0)
        qk_lo = sig("qk_lo", 4, 4, 4, 0)
        v_ps = sig("v_ps", 2, 2, 2, 0)
        v_ok = sig("v_ok", 2, 2, 2, 0)
        s_ps = sig("s_ps", *(NQ * u for u in UNITS), 0)
        s_max = sig("s_max", *(NQ * u for u in UNITS), 0)
        mT_ps = sig("mT_ps", NQ, NQ, NQ, 0)
        mT_hi = sig("mT_hi", NQ, NQ, NQ, 0)
        mT_lo = sig("mT_lo", NQ, NQ, NQ, 0)
        st_ps = sig("st_ps", *(NQ * 2 * k for k in KCH), 0)
        p_ok = sig("p_ok", *(NQ * 2 * k for k in KCH), 0)
        p_used = sig("p_used", *(NQ * k for k in KCH), 0, first=1)
        o_ok = sig("o_ok", NQ, NQ, NQ, 0)
        hd_ok = sig("hd_ok", NQ, NQ, NQ, 0)
        y_ps = sig("y_ps", 6, 6, 6, 0)
        y_ok = sig("y_ok", 6, 6, 6, 0, first=1)
        xb_ok = sig("xb_ok", 4, 4, 4, 0)
        ctx2_ok = sig("ctx2_ok", 1, 1, 1, 1)
        kx_ps = sig("kx_ps", 1, 1, 1, 1)
        kx_ok = sig("kx_ok", 1, 1, 1, 1)
        kbd_ok = sig("kbd_ok", 1, 1, 1, 0)
        vx_ps = sig("vx_ps", 1, 1, 1, 1, first=1)
        vx_ok = sig("vx_ok", 1, 1, 1, 1)
        qx_ps = sig("qx_ps", 2, 2, 2, 1)
        qx_ok = sig("qx_ok", 2, 2, 2, 1)
        sx_ps = sig("sx_ps", 8, 8, 8, 1)
        sx_sb = sig("sx_sb", 8, 0, 0, 0)
        sx_max = sig("sx_max", 8, 8, 8, 1)
        ex_ok = sig("ex_ok", 8, 8, 8, 1)
        px_tm = sig("px_tm", 8, 0, 0, 1)
        pxT_ps = sig("pxT_ps", 8, 8, 8, 1)
        px_ok = sig("px_ok", 8, 8, 8, 1)
        ox_ps = sig("ox_ps", 2, 2, 2, 0)
        ox_ok = sig("ox_ok", 2, 2, 2, 0, first=1)
        up_ps = sig("up_ps", 16, 8, 8, NX * RC + 2)
        act_ok = sig("act_ok", 16, 8, 8, NX * RC + 2)
        hid_ok = sig("hid_ok", 16, 0, 0, 0)
        ev_ps = sig("ev_ps", 0, 0, 0, 2); ev_ok = sig("ev_ok", 0, 0, 0, 2)
        rl_ps = sig("rl_ps", 0, 0, 0, 1); re_ok = sig("re_ok", 0, 0, 0, 1); rm_ok = sig("rm_ok", 0, 0, 0, 1)
        ex_out = sig("ex_out", 0, 0, 0, 2 * NX); acc_ok = sig("acc_ok", 0, 0, 0, 2 * NX)
        g_ps = sig("g_ps", 0, 0, 0, 2); gs_in = sig("gs_in", 0, 0, 0, 1); gs_ok = sig("gs_ok", 0, 0, 0, 1)
        rT_ps = sig("rT_ps", 0, 0, 0, 2); rT_ok = sig("rT_ok", 0, 0, 0, 2)
        f_ps = sig("f_ps", 0, 0, 0, 2); f_ok = sig("f_ok", 0, 0, 0, 1, first=1)

        n_w = [0, 0, 0, 0]
        blk = ctx.enter_context(nc.Block())

        def kxn(ap):
            return ap.rearrange("(k p) n -> p k n", p=P)

        LOADS = [
            [("qkv", kxn(a["L0_xcond_w_qkv"])), ("qx", kxn(a["L0_xcond_w_q"])), ("kvx", kxn(a["L0_xcond_w_kv"])),
             ("co", kxn(a["L0_xcond_w_co"]))],
            [("qkv", kxn(a["L1_xcond_W_qkv"])), ("qx", kxn(a["L1_xcond_W_qc"])), ("kvx", kxn(a["L1_xcond_W_kvc"])),
             ("co", kxn(a["L1_xcond_W_cproj"]))],
            [("qkv", kxn(a["L2_xcond_qkv_w"])), ("qx", kxn(a["L2_xcond_q_w"])), ("kvx", kxn(a["L2_xcond_kv_w"])),
             ("co", kxn(a["L2_xcond_ca_proj_w"]))],
            [("q", kxn(a["L3_xcond_Wq"])), ("k", kxn(a["L3_xcond_Wk"])), ("v", kxn(a["L3_xcond_Wv"])),
             ("g1", kxn(a["L3_xcond_gate_w1"][0:4 * P, :])), ("g2", kxn(a["L3_xcond_gate_w2"])),
             ("o", kxn(a["L3_xcond_out_w"])), ("r", kxn(a["L3_xcond_router_W"])),
             ("w1_0", kxn(a["L3_xcond_e_w1"][0, 0:4 * P, :]))],
        ]
        LATE = [
            [("m1", kxn(a["L0_xcond_w_m1"])), ("m2", kxn(a["L0_xcond_w_m2"]))],
            [("m1", kxn(a["L1_xcond_W_mlp1"])), ("m2", kxn(a["L1_xcond_W_mlp2"]))],
            [("m1", kxn(a["L2_xcond_fc1_w"])), ("m2", kxn(a["L2_xcond_fc2_w"]))],
            [("w1_1", kxn(a["L3_xcond_e_w1"][1, 0:4 * P, :])), ("w1_2", kxn(a["L3_xcond_e_w1"][2, 0:4 * P, :]))],
        ]
        SO = [a["L0_xcond_w_so"], a["L1_xcond_W_proj"], a["L2_xcond_sa_proj_w"]]
        BSO = [a["L0_xcond_b_so"], a["L1_xcond_b_proj"], a["L2_xcond_sa_proj_b"]]
        ROWS = [
            [("bv", a["L0_xcond_b_qkv"][2 * C:]), ("bvx", a["L0_xcond_b_kv"][C:]), ("bco", a["L0_xcond_b_co"]),
             ("bm2", a["L0_xcond_b_m2"])],
            [("bv", a["L1_xcond_b_qkv"][2 * C:]), ("bvx", a["L1_xcond_b_kvc"][C:]), ("bco", a["L1_xcond_b_cproj"]),
             ("bm2", a["L1_xcond_b_mlp2"])],
            [("bv", a["L2_xcond_qkv_b"][2 * C:]), ("bvx", a["L2_xcond_kv_b"][C:]), ("bco", a["L2_xcond_ca_proj_b"]),
             ("bm2", a["L2_xcond_fc2_b"])],
            [("gb2", a["L3_xcond_gate_b2"]), ("ob", a["L3_xcond_out_b"])],
        ]
        ORDER = {(0, None): stage_order(attention_stages(0), []), (None, 2): stage_order([], rest_stages(2))}
        for L in range(3):
            ORDER[L, L] = stage_order(attention_stages(L), rest_stages(L))
            if L > 0:
                ORDER[L, L - 1] = stage_order(attention_stages(L), rest_stages(L - 1))
        N_LOADS = [len(LOADS[L]) + 5 + len(ROWS[L]) for L in range(3)] + [len(LOADS[3]) + len(ROWS[3]) + NX]
        N_LATE = [2, 2, 2, 2 + NX]

        def load_layer(eng, L):
            for name, src in LOADS[L]:
                eng.dma_start(W[L][name], src).then_inc(d_w[L], 16)
            for name, src in ROWS[L]:
                eng.dma_start(W[L][name], src.partition_broadcast(P)).then_inc(d_w[L], 16)
            if L < 3:
                eng.wait_ge(so_zero, L + 1)
                so = SO[L].rearrange("(q j d) n -> j d q n", j=4, d=HD)
                for j in range(4):
                    eng.dma_start(W[L]["so"][32 * j:32 * j + HD, :, :], so[j]).then_inc(d_w[L], 16)
                eng.dma_start(W[L]["so"][HD:HD + 1, 0, :], BSO[L].rearrange("(a n) -> a n", a=1)).then_inc(d_w[L], 16)
            else:
                for e in range(NX):
                    eng.dma_start(W[3]["b2"][:, e, :], a["L3_xcond_e_b2"][e].partition_broadcast(P)).then_inc(d_w[3], 16)

        def load_late(eng, L):
            for name, src in LATE[L]:
                eng.dma_start(W[L][name], src).then_inc(d_late[L], 16)
            if L == 3:
                for e in range(NX):
                    eng.dma_start(W[3]["w2"][:, e, :, :], kxn(a["L3_xcond_e_w2"][e])).then_inc(d_late[3], 16)

        ADA_SRC = [a["L0_xcond_w_ada"], a["L1_xcond_W_mod"], a["L2_xcond_ada_w"]]
        FULL = slice(SHIFT, T - SHIFT)

        @blk.sync
        def _(sp):
            for name, (inp, at, n) in VECS.items():
                src = a[inp]
                if len(src.shape) == 2:
                    src = src.rearrange("b n -> (b n)")
                sp.dma_start(vec_rows[at:at + n, :], src[0:n * P].rearrange("(m p) -> m p", p=P)).then_inc(d_vecs, 16)
            for k in range(KC):
                sp.dma_start(ada_w[0][k], kxn(ADA_SRC[0])[:, k, :]).then_inc(d_ada[0], 16)
            sp.dma_start(ctx_tm[:, 0:2, :], a["ctx_1024"].rearrange("(g b) s c -> (b s) g c", g=2)).then_inc(d_ctx, 16)
            for b in range(NB):
                xv = x_all[:, b * NT * C:(b + 1) * NT * C].rearrange("p (t c) -> p t c", t=NT)
                sp.dma_start(xv[:, 0:NT - 1, :], a["x"][b, FULL, :].rearrange("(t p) c -> p t c", p=P)).then_inc(d_x, 16)
                sp.dma_start(xv[0:SHIFT, NT - 1, :], a["x"][b, T - SHIFT:, :]).then_inc(d_x, 16)
                sp.dma_start(xv[SHIFT:P, NT - 1, :], a["x"][b, 0:SHIFT, :]).then_inc(d_x, 16)
            sp.dma_start(mrow_words[:, :], a["mask_BxS2_bf0"].rearrange("(o b) s -> o (b s)", o=1)).then_inc(d_mask, 16)
            for L in (1, 2):
                for k in range(KC):
                    sp.dma_start(ada_w[L][k], kxn(ADA_SRC[L])[:, k, :]).then_inc(d_ada[L], 16)
            for L in range(3):
                if L == 0:
                    sp.wait_ge(const_r, 1)
                def attention(b):
                    def put(i):
                        sp.wait_ge(qk_hi.sem, qk_hi.at(L, b, i + 1))
                        sp.wait_ge(qk_lo.sem, qk_lo.at(L, b, i + 1))
                        if i < 2:
                            sp.wait_ge(p_used.sem, p_used.at(L, b, 0))
                        c = i // 2
                        if i % 2 == 0:
                            sp.dma_start(q_scratch[c], split[:, 0, :, :]).then_inc(d_split[0], 16)
                        else:
                            sp.dma_start(k_scratch[c], split[:, 1, 0:1, :].to_broadcast([P, 2, T])).then_inc(d_split[1], 16)
                            sp.dma_start(kl_scratch[c], split[:, 1, 1, :]).then_inc(d_split[1], 16)

                    def stack(g):
                        c, h0, s = g // 2, 4 * (g % 2), g % SLOTS
                        if g % 2 == 0:
                            for i in range(2):
                                sp.wait_ge(d_split[i], split_done(L, b, i, c + 1))
                                sp.sem_inc(apart_sp, 1)
                        if g >= SLOTS:
                            sp.wait_ge(st_ps.sem, st_ps.at(L, b, (g - SLOTS + 1) * 2 * KCH[L]))
                        sp.dma_start(q_stack[MAX_ROW:MAX_ROW + 2, s, :, :].bitcast(F32).rearrange("p h (a t) -> p (h a) t", a=2),
                                     zeros[64:66, :].unsqueeze(1).to_broadcast([2, 8, C])).then_inc(d_stack[s], 16)
                        sp.dma_start(q_stack[0:32, s, :, :].bitcast(F32), q_src[c, :, h0:h0 + 4, :]).then_inc(d_stack[s], 16)
                        sp.dma_start(k_stack[0:32, s, :, :].bitcast(F32), k_src[c, :, h0:h0 + 4, :]).then_inc(d_stack[s], 16)
                        sp.dma_start(q_stack[32:48, s, :, :].bitcast(F32), q_hi_src[c, 0, :, h0:h0 + 4, :]).then_inc(d_stack[s], 16)
                        sp.dma_start(k_stack[32:48, s, :, :].bitcast(F32), kl_src[c, :, h0:h0 + 4, :]).then_inc(d_stack[s], 16)

                    def maxima(g):
                        sp.wait_ge(mT_hi.sem, mT_hi.at(L, b, g + 1))
                        sp.wait_ge(mT_lo.sem, mT_lo.at(L, b, g + 1))
                        for s, src in enumerate((m_hi, m_lo)):
                            sp.dma_start(m_scratch[g % 2, s], src).then_inc(d_mput[g % 2], 16)
                        sp.wait_ge(d_mput[g % 2], mput_done(L, b, g))
                        sp.dma_start(q_stack[MAX_ROW:MAX_ROW + 2, g % SLOTS, :, :].bitcast(F32), m_scratch[g % 2]).then_inc(d_mget[g % SLOTS], 16)

                    for i in range(2):
                        put(i)
                    stack(0)
                    stack(1)
                    for i in range(2, 4):
                        put(i)
                    stack(2)
                    maxima(0)
                    maxima(1)
                    stack(3)
                    maxima(2)
                    maxima(3)

                attention(0)
                with sp.Fori(0, NB - 1) as r:
                    attention((r, 1))
            sp.wait_ge(hd_ok.sem, hd_ok.end(2))
            for e in range(NX):
                sp.dma_start(w1_anchor[e], kxn(a["L3_xcond_e_w1"][e, 4 * P:6 * P, :])).then_inc(d_anchor, 16)
            sp.dma_start(g1_anchor, kxn(a["L3_xcond_gate_w1"][4 * P:6 * P, :])).then_inc(d_anchor, 16)
            with sp.Fori(0, NB) as b:
                sp.wait_ge(f_ok.sem, f_ok.at(3, b, 1))
                sp.sem_inc(apart_sp, 1)
                xv = x_all[:, bass.ds(b * (NT * C), NT * C)].rearrange("p (t c) -> p t c", t=NT)
                ob = out[bass.ds(b, 1), :, :].rearrange("o s c -> (o s) c")
                sp.dma_start(ob[FULL, :].rearrange("(t p) c -> p t c", p=P), xv[:, 0:NT - 1, :]).then_inc(d_out, 16)
                sp.dma_start(ob[T - SHIFT:T, :], xv[0:SHIFT, NT - 1, :]).then_inc(d_out, 16)
                sp.dma_start(ob[0:SHIFT, :], xv[SHIFT:P, NT - 1, :]).then_inc(d_out, 16)
            sp.wait_ge(d_out, 16 * 3 * NB)

        @blk.gpsimd
        def _(po):
            n = [0]

            def link(ins):
                n[0] += 1
                ins.then_inc(pool_chain, 1)
                po.wait_ge(pool_chain, n[0])

            def fresh():
                n[0] = 0
                po.sem_clear(pool_chain)

            def apart():
                po.sem_inc(apart_pool, 1)

            def band(t, groups, width, step, base):
                link(po.affine_select(out=t, in_=t, compare_op=ALU.is_ge, fill=0.0, base=base,
                                      pattern=[[-step, groups]], channel_multiplier=1))
                link(po.affine_select(out=t, in_=t, compare_op=ALU.is_ge, fill=0.0, base=width - 1 - base,
                                      pattern=[[step, groups]], channel_multiplier=-1))

            link(po.memset(ident[:, :], 1.0))
            link(po.affine_select(out=ident[:, :], in_=ident[:, :], compare_op=ALU.is_equal, fill=0.0, base=0,
                                  pattern=[[-1, P]], channel_multiplier=1))
            link(po.memset(ones[:, :], 1.0))
            link(po.memset(zeros[:, :], 0.0))
            po.memset(W[0]["so"], 0.0).then_inc(so_zero, 1)
            po.wait_ge(so_zero, 1)
            link(po.memset(head_mask[:, :], 1.0))
            band(head_mask[:, :], 8, HD, HD, 0)
            link(po.memset(ones_pair[:, :], 0.0))
            link(po.memset(ones_pair[0:S2, 0:HD], 1.0))
            link(po.memset(ones_pair[S2:P, HD:2 * HD], 1.0))
            link(po.memset(v_bd[:, :, :], 0.0))
            link(po.memset(half_neg[:, :], -0.5))
            po.sem_inc(consts, 1)
            po.wait_ge(ctx_var, 1)
            link(po.tensor_scalar(var_eps[:, 0:2], mv[:, 0:2, 1], EPS[1], None, ALU.add))
            po.tensor_tensor(rstd[:, 0:2], var_eps[:, 0:2], half_neg[:, 0:2], ALU.pow).then_inc(ctx_rstd, 1)
            fresh()
            po.wait_ge(ada_ps, 3)
            po.memset(W[1]["so"], 0.0).then_inc(so_zero, 1)
            po.memset(v_aug[:, :, :, HD:2 * HD], 1.0).then_inc(v_ones, 1)

            def context(L, b):
                po.wait_ge(vx_ps.sem, vx_ps.at(L, b, 0))
                po.wait_ge(ctx_ok, 4)
                for k in range(KC):
                    for h in range(2):
                        i = po.tensor_copy(ctx_two[:, k, h, :], ctxT[:, 1 if L == 1 else 0, k, batch_of(b, S2)])
                        if 2 * k + h < 3:
                            link(i)
                i.then_inc(ctx2_ok.sem, 1)

            def rstd_of(L, h, eps_of, var, out, done):
                ts = slice(2 * h, 2 * h + 2)
                link(po.tensor_scalar(eps_of[:, ts], var[:, ts, 1], EPS[L], None, ALU.add))
                po.tensor_tensor(out[:, ts], eps_of[:, ts], half_neg[:, ts], ALU.pow).then_inc(done.sem, 1)

            def norm_a(L, b, h):
                po.wait_ge(var_a.sem, var_a.at(L, b, h + 1))
                apart()
                rstd_of(L, h, var_eps, mv, rstd, rstd_a)

            def attention(L, b):
                return {"moments_a": lambda h: norm_a(L, b, h)}

            def rest(L, b):
                xv = x_all[:, batch_of(b, NT * C)].rearrange("p (t c) -> p t c", t=NT)

                def now_r(_):
                    context(L, b)

                def norm_r(j, h):
                    po.wait_ge(var_r.sem, var_r.at(L, b, nth(j, h)))
                    apart()
                    rstd_of(L, h, var_eps_r, mv_r, rstd_r, rstd_r_ok)

                def add_bias(j, h):
                    po.wait_ge(xr_ok.sem, xr_ok.at(L, b, nth(j, h)))
                    apart()
                    row = bg_rows[:, j - 1, :] if j in GATES[L] else W[L]["bco"]
                    xh = xv[:, 2 * h:2 * h + 2, :]
                    po.tensor_tensor(xh, xh, row.unsqueeze(1).to_broadcast([P, 2, C]), ALU.add).then_inc(xb_ok.sem, 1)

                def gate(g):
                    blk_no = GATES[L][g]
                    if blk_no > 0:
                        po.wait_ge(gate_ok.sem, gate_ok.at(L, b, g + 1))
                        row = W[L]["bco"] if blk_no == 1 else W[L]["bm2"]
                        po.tensor_tensor(bg_rows[:, blk_no - 1, :], row, gate_rows[:, blk_no, :], ALU.mult).then_inc(bg_ok.sem, 1)
                        po.wait_ge(bg_ok.sem, bg_ok.at(L, b, sum(x > 0 for x in GATES[L][:g + 1])))

                def values_x(_):
                    po.wait_ge(kx_ok.sem, kx_ok.at(L, b, 1))
                    for k in range(KC):
                        i = po.tensor_tensor(k_bd[:, k, :, :], kxT[:, k, :].unsqueeze(1).to_broadcast([P, 8, S2]),
                                             head_mask[:, :].unsqueeze(2).to_broadcast([P, 8, S2]), ALU.mult)
                        if k == 0:
                            link(i)
                    i.then_inc(kbd_ok.sem, 1)

                return {"now_r": now_r, "gate": gate, "values_x": values_x,
                        "out_s": lambda ht: norm_r(1, 0) if ht == (0, 1) else None,
                        "moments_r": lambda jh: norm_r(*jh),
                        "out_x": lambda h: norm_r(2, h),
                        "norm_r": lambda jh: add_bias(*jh)}

            def both(L, b, L_rest, b_rest):
                mine = attention(L, b) | (rest(L_rest, b_rest) if L_rest is not None else {})
                for stage, arg in ORDER[L, L_rest]:
                    if stage in mine:
                        mine[stage](arg)
                fresh()

            for L in range(3):
                po.wait_ge(d_w[L], 16 * N_LOADS[L])
                both(L, 0, L - 1 if L else None, NB - 1)
                if L == 1:
                    po.wait_ge(so_zero, 2)
                    po.wait_ge(y_ps.sem, y_ps.end(0))
                    po.memset(W[2]["so"], 0.0).then_inc(so_zero, 1)
                    po.wait_ge(so_zero, 3)
                with po.Fori(0, NB - 1) as r:
                    both(L, (r, 1), L, r)
            alone = rest(2, NB - 1)
            for stage, arg in ORDER[None, 2]:
                if stage in alone:
                    alone[stage](arg)
            fresh()
            with po.Fori(0, NB) as b:
                context(3, b)
                norm_a(3, b, 0)
                norm_a(3, b, 1)
                fresh()

        @blk.tensor
        def _(pe):
            mm = nc.tensor.matmul

            def wait(s, L, b, k):
                pe.wait_ge(s.sem, s.at(L, b, k))

            def apart():
                pe.sem_inc(apart_pe, 1)

            pe.sem_inc(p_used.sem, 1)
            pe.sem_inc(vx_ps.sem, 1)
            pe.sem_inc(rT_in.sem, 1)

            pe.wait_ge(consts, 1)
            pe.wait_ge(d_vecs, 16 * len(VECS))
            nc.tensor.transpose(bank[:, X, 0:NVEC], vec_rows[0:NVEC, :], ident[0:NVEC, 0:NVEC]).then_inc(vecs_ps, 1)

            pe.wait_ge(cond_ok, 1)
            for L in range(3):
                pe.wait_ge(d_ada[L], 16 * KC)
                for m in range(ADA[L]):
                    for k in range(KC):
                        i = mm(bank[:, B + L, m * NB:(m + 1) * NB], ada_w[L][k][:, m * P:(m + 1) * P], cond_s[:, k, :],
                               start=(k == 0), stop=(k == KC - 1))
                i.then_inc(ada_ps, 1)
            pe.wait_ge(d_ctx, 16)
            for v in range(2):
                if v == 1:
                    pe.wait_ge(ctx_n, 1)
                    pe.wait_ge(ctx_ok, 2)
                for k in range(KC):
                    for g in range(2):
                        i = nc.tensor.transpose(bank[:, A + k, g * P:(g + 1) * P], ctx_tm[:, 2 * v + g, k * P:(k + 1) * P], ident[:, :])
                    i.then_inc(ctx_ps, 1)

            def transposes(h, bk, done):
                for k in range(KC):
                    for t in range(2):
                        i = nc.tensor.transpose(bank[:, bk, k * HT + t * P:k * HT + (t + 1) * P],
                                                xn[:, 2 * h + t, k * P:(k + 1) * P], ident[:, :])
                i.then_inc(done.sem, 1)

            def tm_out(L, b, h, bk, lhs, rhs, kn, done, tile=None, part=None):
                for t in (0, 1) if tile is None else (tile,):
                    for k in range(kn) if part is None else range(part * kn // 2, (part + 1) * kn // 2):
                        i = mm(bank[:, bk, t * C:(t + 1) * C], lhs(k, 2 * h + t), rhs(k),
                               start=(k == 0), stop=(k == kn - 1))
                if t == 1 and k == kn - 1:
                    i.then_inc(done.sem, 1)

            def attention(L, b):
                w = W[L]

                def input_a(h):
                    wait(xa_ok, L, b, h + 1)
                    transposes(h, S + h, aT_ps)

                def qk(i):
                    if i == 0:
                        wait(ha_ok, L, b, 2)
                    if i >= 2:
                        wait(qk_lo, L, b, i - 1)
                    m = (i % 2) * KC + i // 2
                    for k in range(KC):
                        ins = mm(bank[:, K + i % 2, :], w["qkv"][:, k, m * P:(m + 1) * P], hT[:, k, :], start=(k == 0), stop=(k == KC - 1))
                    ins.then_inc(qk_ps.sem, 1)

                def v(h):
                    for t in (2 * h, 2 * h + 1):
                        for k in range(KC):
                            i = mm(bank[:, S + h, (t % 2) * C:(t % 2 + 1) * C], hT[:, k, t * P:(t + 1) * P], w["qkv"][:, k, 2 * C:3 * C],
                                   start=(k == 0), stop=(k == KC - 1))
                    i.then_inc(v_ps.sem, 1)

                def tile(n):
                    g, u = n // UNITS[L], n % UNITS[L]
                    s = g % SLOTS
                    if u == 0:
                        pe.wait_ge(d_stack[s], stack_done(L, b, g))
                    if n < 2:
                        wait(v_ok, L, b, n + 1)
                    else:
                        wait(s_max, L, b, n - 1)
                    if L == 0:
                        for j in range(4):
                            cols = slice(u * P, (u + 1) * P)
                            i = mm(bank[:, S + n % 2, j * P:(j + 1) * P], q_stack[0:KS, s, j, cols], k_stack[0:KS, s, j, cols],
                                   start=True, stop=True)
                    else:
                        j, t = u // 4, u % 4
                        i = mm(bank[:, S + n % 2, :], q_stack[0:KS, s, j, t * P:(t + 1) * P], k_stack[0:KS, s, j, :],
                               start=True, stop=True)
                    i.then_inc(s_ps.sem, 1)

                def max_out(g):
                    wait(s_max, L, b, (g + 1) * UNITS[L])
                    if g > 0:
                        wait(mT_hi, L, b, g)
                        wait(mT_lo, L, b, g)
                    for t in range(NT):
                        i = nc.tensor.transpose(bank[0:4, X, t * P:(t + 1) * P], nm[:, t, 4 * g:4 * g + 4], ident[:, :])
                    i.then_inc(mT_ps.sem, 1)

                def keys(arg):
                    step, pair = arg
                    g, c = step // KCH[L], step % KCH[L]
                    s = g % SLOTS
                    if c == 0 and pair == 0:
                        pe.wait_ge(d_mget[s], mget_done(L, b, g))
                    n = 2 * step + pair
                    if n > 0:
                        wait(p_ok, L, b, n)
                    else:
                        wait(qk_lo, L, b, 4)
                    for j in (2 * pair, 2 * pair + 1):
                        if L == 0:
                            for u in range(NT):
                                cols = slice(u * P, (u + 1) * P)
                                i = mm(bank[:, K + j % 2, cols], k_stack[0:KS, s, j, cols], q_stack[0:KS, s, j, cols],
                                       start=True, stop=True)
                        else:
                            i = mm(bank[:, K + j % 2, :], k_stack[0:KS, s, j, c * P:(c + 1) * P], q_stack[0:KS, s, j, :],
                                   start=True, stop=True)
                    i.then_inc(st_ps.sem, 1)

                def weigh(step):
                    g, c = step // KCH[L], step % KCH[L]
                    wait(p_ok, L, b, 2 * step + 2)
                    if c == 0 and g > 0:
                        wait(o_ok, L, b, g)
                    if L == 0:
                        for u in range(NT):
                            for j in range(4):
                                cols = slice(u * P, (u + 1) * P)
                                i = mm(bank[32 * j:32 * j + 32, O, cols], v_aug[:, u, 4 * g + j, :], probs[:, j, cols],
                                       start=True, stop=True)
                    else:
                        for j in range(4):
                            i = mm(bank[32 * j:32 * j + 32, O, :], v_aug[:, c, 4 * g + j, :], probs[:, j, :],
                                   start=(c == 0), stop=(c == KCH[L] - 1))
                    i.then_inc(p_used.sem, 1)

                return {"input_a": input_a, "qk": qk, "v": v, "tile": tile, "max_out": max_out, "keys": keys, "weigh": weigh}

            def rest(L, b):
                w = W[L]
                n_gates = len(GATES[L])

                def gate(g):
                    if g == 0:
                        wait(diag_ok, L, b, 1)
                        wait(y_ok, L, b, 0)
                    elif g == 2:
                        wait(gate_ok, L, b, 1)
                    for k in range(KC):
                        i = mm(bank[:, R + g % 2, k * P:(k + 1) * P], ones[:, :], diag[g][:, k, :], start=True, stop=True)
                    i.then_inc(gate_ps.sem, 1)

                def keys_x(_):
                    wait(ctx2_ok, L, b, 1)
                    wait(gate_ok, L, b, n_gates)
                    for m in range(KC):
                        for k in range(KC):
                            i = mm(bank[:, R + 1, m * S2:(m + 1) * S2], w["kvx"][:, k, m * P:(m + 1) * P], ctx_two[:, k, 0, :],
                                   start=(k == 0), stop=(k == KC - 1))
                    i.then_inc(kx_ps.sem, 1)

                def values_x(_):
                    for k in range(KC):
                        i = mm(bank[:, R, 0:C], ctx_two[:, k, :, :], w["kvx"][:, k, C:2 * C], start=(k == 0), stop=(k == KC - 1))
                    i.then_inc(vx_ps.sem, 1)

                def out_s(arg):
                    h, t = arg
                    if t == 0:
                        if h == 0:
                            wait(hd_ok, L, b, NQ)
                            wait(kx_ok, L, b, 1)
                        else:
                            wait(vx_ok, L, b, 1)
                    tm_out(L, b, h, R + 1 - h, lambda k, t: work[:, k, t * P:(t + 1) * P], lambda k: w["so"][:, k, :], NQ, y_ps, t)

                def input_r(arg):
                    j, h = arg
                    wait(xr_ok, L, b, nth(j, h))
                    if j == 1 and h == 0:
                        wait(y_ok, L, b, 1)
                    transposes(h, R + 1, rT_in)

                def query_x(h):
                    wait(hr_ok, L, b, nth(1, h))
                    wait(y_ok, L, b, 2 + 2 * h)
                    for m in range(KC):
                        for k in range(KC):
                            i = mm(bank[:, R, m * HT:(m + 1) * HT], w["qx"][:, k, m * P:(m + 1) * P], hR[:, k, :],
                                   start=(k == 0), stop=(k == KC - 1))
                    i.then_inc(qx_ps.sem, 1)

                def scores_x(n):
                    t, k = n // KC % 2, n % KC
                    if n % 4 == 0:
                        wait(qx_ok, L, b, n // 4 + 1)
                    else:
                        wait(sx_sb if L == 0 else sx_max, L, b, n)
                    if n == 0:
                        wait(kbd_ok, L, b, 1)
                    i = mm(bank[:, R, :], qT[:, k, t * P:(t + 1) * P], k_bd[:, k, :, :], start=True, stop=(L != 2))
                    if L == 2:
                        i = mm(bank[:, R, :].rearrange("p (h s) -> p h s", h=8), one_row[:, :],
                               mask_row[:, batch_of(b, 1), :].to_broadcast([P, 8, S2]),
                               start=False, stop=True)
                    i.then_inc(sx_ps.sem, 1)

                def probs_x(n):
                    wait(px_tm if L == 0 else ex_ok, L, b, n + 1)
                    if n % 4 > 0:
                        wait(px_ok, L, b, n)
                    for r in range(4):
                        i = nc.tensor.transpose(bank[:, R + 1, r * P:(r + 1) * P], p_tm[n % 2][:, r * P:(r + 1) * P], ident[:, :])
                    i.then_inc(pxT_ps.sem, 1)

                def heads_x(h):
                    wait(px_ok, L, b, 4 * h + 4)
                    for lhs, bk in ((lambda m: v_bd[:, m, :], R), (lambda m: ones_pair[:, :], R + 1)):
                        for c in range(KC):
                            for r in range(4):
                                i = mm(bank[32 * r:32 * r + 32, bk, c * HT:(c + 1) * HT], lhs(4 * c + r), hid[:, 4 * c + r, :],
                                       start=True, stop=True)
                    i.then_inc(ox_ps.sem, 1)

                def out_x(h):
                    wait(ox_ok, L, b, h + 1)
                    tm_out(L, b, h, R, lambda k, t: xT[:, k, (t % 2) * P:(t % 2 + 1) * P], lambda k: w["co"][:, k, :], KC, y_ps)

                def up(h):
                    pe.wait_ge(d_late[L], 16 * N_LATE[L])
                    wait(hr_ok, L, b, nth(2, h))
                    wait(y_ok, L, b, 3 + 2 * h)
                    for u in range(UNITS_UP[L]):
                        if u >= 2:
                            wait(hid_ok if L == 0 else act_ok, L, b, h * UNITS_UP[L] + u - 1)
                        for e in range(2):
                            m = u + e * HIDC if L == 0 else 2 * u + e
                            for k in range(KC):
                                i = mm(bank[:, R + u % 2, e * HT:(e + 1) * HT], w["m1"][:, k, m * P:(m + 1) * P], hR[:, k, :],
                                       start=(k == 0), stop=(k == KC - 1))
                        i.then_inc(up_ps.sem, 1)

                def down(arg):
                    h, tile, part = arg
                    if tile == 0 and part == 0:
                        wait(hid_ok if L == 0 else act_ok, L, b, (h + 1) * UNITS_UP[L])
                    tm_out(L, b, h, R, lambda k, t: hid[:, k, (t % 2) * P:(t % 2 + 1) * P], lambda k: w["m2"][:, k, :], HIDC, y_ps, tile, part)

                return {"gate": gate, "keys_x": keys_x, "values_x": values_x, "out_s": out_s, "input_r": input_r,
                        "query_x": query_x, "scores_x": scores_x, "probs_x": probs_x, "heads_x": heads_x, "out_x": out_x,
                        "up": up, "down": down}

            def both(L, b, L_rest, b_rest):
                mine = attention(L, b) | (rest(L_rest, b_rest) if L_rest is not None else {})
                for stage, arg in ORDER[L, L_rest]:
                    if stage in mine:
                        mine[stage](arg)

            for L in range(3):
                pe.wait_ge(d_w[L], 16 * N_LOADS[L])
                both(L, 0, L - 1 if L else None, NB - 1)
                with pe.Fori(0, NB - 1) as r:
                    both(L, (r, 1), L, r)
            L, w = 3, W[3]

            def from_anchor(m):
                for k in range(KC):
                    if m < NX * RC:
                        mm(bank[:, B, m * NB:(m + 1) * NB], w1_anchor[m // RC][:, k, (m % RC) * P:(m % RC + 1) * P], cond_r[:, k, :],
                           start=(k == 0), stop=(k == KC - 1))
                    elif m < NX * RC + 2:
                        mm(bank[:, B, m * NB:(m + 1) * NB], g1_anchor[:, k, (m - NX * RC) * P:(m - NX * RC + 1) * P], cond_r[:, k, :],
                           start=(k == 0), stop=(k == KC - 1))
                    else:
                        mm(bank[0:NX, B + 1, 0:NB], w["r"][:, 4 + k, :], cond_r[:, k, :], start=(k == 0), stop=(k == KC - 1))

            alone = rest(2, NB - 1)
            chunks = list(range(NX * RC + 3))
            each = -(-len(chunks) // (NCT - 1))
            for stage, arg in ORDER[None, 2]:
                if stage == "scores_x" and arg > 0:
                    if arg == 1:
                        pe.wait_ge(d_w[3], 16 * N_LOADS[3])
                        pe.wait_ge(d_anchor, 16 * (NX + 1))
                        pe.wait_ge(act_chain, 1)
                    for m in chunks[(arg - 1) * each:arg * each]:
                        from_anchor(m)
                if stage in alone:
                    alone[stage](arg)

            for m in range(KC):
                for k in range(KC):
                    i = nc.tensor.transpose(bank[:, A, m * C + k * P:m * C + (k + 1) * P], w["q"][:, k, m * P:(m + 1) * P], ident[:, :])
            i.then_inc(anc_ps, 1)
            pe.wait_ge(y_ok.sem, y_ok.end(2))
            pe.wait_ge(anc_ok, 3)
            comb = lambda k: hT[:, k, :] if k < 2 else evT[:, k - 2, :]
            with pe.Fori(0, NB) as b:
                wait(ctx2_ok, L, b, 1)
                apart()
                for m in range(KC):
                    for k in range(KC):
                        i = mm(bank[:, X, m * S2:(m + 1) * S2], w["k"][:, k, m * P:(m + 1) * P], ctx_two[:, k, 0, :],
                               start=(k == 0), stop=(k == KC - 1))
                i.then_inc(kx_ps.sem, 1)
                wait(kx_ok, L, b, 1)
                for k in range(KC):
                    for m in range(KC):
                        i = mm(bank[:, O, k * S2:(k + 1) * S2], wqT[:, m, k * P:(k + 1) * P], kxT[:, m, :], start=(m == 0), stop=(m == KC - 1))
                i.then_inc(qx_ps.sem, 1)
                for k in range(KC):
                    i = mm(bank[0:S2, X, 0:C], ctx_two[:, k, 0, :], w["v"][:, k, :], start=(k == 0), stop=(k == KC - 1))
                i.then_inc(vx_ps.sem, 1)
                wait(f_ok, L, b, 0)
                for h in range(2):
                    wait(xa_ok, L, b, h + 1)
                    transposes(h, A + h, aT_ps)
                wait(qx_ok, L, b, 1)
                wait(ha_ok, L, b, 2)
                for t in range(NT):
                    for k in range(KC):
                        i = mm(bank[:, A, t * S2:(t + 1) * S2], hT[:, k, t * P:(t + 1) * P], kqT[:, k, :], start=(k == 0), stop=(k == KC - 1))
                i.then_inc(sx_ps.sem, 1)

                def hidden_part(m, ks):
                    for k in ks:
                        lhs = w[f"w1_{m // RC}"][:, k, (m % RC) * P:(m % RC + 1) * P] if m < NX * RC else w["g1"][:, k, (m - NX * RC) * P:(m - NX * RC + 1) * P]
                        i = mm(bank[:, B + m % 4, :], lhs, comb(k), start=(k == 0), stop=(k == 3))
                    return i

                hidden_part(0, (0, 1))
                hidden_part(1, (0, 1))
                wait(px_tm, L, b, 1)
                wait(vx_ok, L, b, 1)
                apart()
                for t in range(NT):
                    i = nc.tensor.transpose(bank[0:S2, X, t * P:(t + 1) * P], p_tm3[:, t, :], ident[:, :])
                i.then_inc(pxT_ps.sem, 1)
                hidden_part(2, (0, 1))
                wait(px_ok, L, b, 1)
                for m in range(KC):
                    mm(bank[:, A + m, :], v3[0:S2, m * P:(m + 1) * P], pT3[0:S2, :], start=True, stop=True).then_inc(ev_ps.sem, 1)
                hidden_part(3, (0, 1))
                wait(ev_ok, L, b, 2)
                for t in range(NT):
                    for k in range(4):
                        mm(bank[:, X, t * NX:(t + 1) * NX], comb(k)[:, t * P:(t + 1) * P], w["r"][:, k, :], start=(k == 0), stop=False)
                    i = mm(bank[:, X, t * NX:(t + 1) * NX], ones[0:NX, 0:P], router_diag[:, :], start=False, stop=True)
                i.then_inc(rl_ps.sem, 1)

                def hidden(m):
                    if m >= 4:
                        wait(act_ok, L, b, m - 3)
                    hidden_part(m, (0, 1, 2, 3) if m >= 4 else (2, 3)).then_inc(up_ps.sem, 1)

                def expert(e):
                    wait(act_ok, L, b, RC * (e + 1))
                    for t in range(NT):
                        if t % 2 == 0 and e > 0:
                            wait(acc_ok, L, b, 2 * (e - 1) + t // 2 + 1)
                        for k in range(RC):
                            i = mm(bank[:, A + t // 2, (t % 2) * C:(t % 2 + 1) * C], hid3[e % 2][:, k, t * P:(t + 1) * P], w["w2"][:, e, k, :],
                                   start=(k == 0), stop=(k == RC - 1))
                        if t % 2:
                            i.then_inc(ex_out.sem, 1)

                for m in range(RC):
                    hidden(m)
                pe.wait_ge(d_late[3], 16 * N_LATE[3])
                for e in range(NX):
                    if e + 1 < NX:
                        for m in range(RC):
                            hidden(RC * (e + 1) + m)
                    else:
                        hidden(NX * RC)
                        hidden(NX * RC + 1)
                    expert(e)
                wait(acc_ok, L, b, 2 * NX)
                wait(act_ok, L, b, NX * RC + 2)
                for h in range(2):
                    tm_out(L, b, h, A + h, lambda k, t: uT[:, k, t * P:(t + 1) * P], lambda k: w["g2"][:, k, :], KC, g_ps)
                for k in range(KC):
                    for t in range(NT):
                        i = nc.tensor.transpose(bank[:, B + k, t * P:(t + 1) * P], xn[:, t, k * P:(k + 1) * P], ident[:, :])
                    i.then_inc(rT_ps.sem, 1)
                wait(rT_ok, L, b, 2)
                wait(gs_in, L, b, 1)
                for h in range(2):
                    tm_out(L, b, h, A + h, lambda k, t: hT[:, k, t * P:(t + 1) * P], lambda k: w["o"][:, k, :], KC, f_ps)

        @blk.scalar
        def _(ac):
            act = nc.scalar.activation

            def wait(s, L, b, k):
                ac.wait_ge(s.sem, s.at(L, b, k))

            load_layer(ac, 0)
            load_late(ac, 0)
            ac.wait_ge(vecs_ps, 1)
            nc.scalar.copy(vecs[:, :], bank[:, X, 0:NVEC]).then_inc(vecs_ok, 1)
            ac.wait_ge(vecs_ok, 1)
            cv = VECS["cond"][1]
            cond_cols = vecs[:, cv:cv + NB * KC].rearrange("p (b k) -> p k b", b=NB)
            act(cond_s[:, :, :], cond_cols, ACT.Silu).then_inc(cond_ok, 1)
            act(cond_r[:, :, :], cond_cols, ACT.Copy).then_inc(act_chain, 1)
            for n in range(4):
                ac.wait_ge(ctx_ps, n + 1)
                nc.scalar.copy(ctxT[:, n // 2, n % 2, :], bank[:, A + n % 2, 0:NB * S2]).then_inc(ctx_ok, 1)
            ac.wait_ge(ada_ps, 3)
            load_layer(ac, 1)

            def to_feature(L, j, out, bk, columns, done):
                for k in range(KC):
                    if L == 3:
                        g, be = VECS["gamma"][1] + k, VECS["beta"][1] + k
                        s, o = vecs[:, g:g + 1], vecs[:, be:be + 1]
                    elif SCALE_OF[L][j] is None:
                        s, o = 1.0, 0.0
                    else:
                        sc, sh = SCALE_OF[L][j] + k, SHIFT_OF[L][j] + k
                        s, o = columns[:, sc:sc + 1], columns[:, sh:sh + 1]
                    i = act(out(k), bank[:, bk, k * HT:(k + 1) * HT], ACT.Identity, bias=o, scale=s)
                i.then_inc(done.sem, 1)

            def attention(L, b):
                def input_a(h):
                    wait(aT_ps, L, b, h + 1)
                    if h == 0:
                        wait(now_ok, L, b, 1)
                        if L > 0 or not isinstance(b, int):
                            for s in range(2):
                                ac.wait_ge(d_mput[s], times(b, 64, L * NB * 64))
                    to_feature(L, 0, lambda k: hT[:, k, h * HT:(h + 1) * HT], S + h, mod_now, ha_ok)

                def qk(i):
                    qv = VECS[f"qk{L}"][1]
                    wait(qk_ps, L, b, i + 1)
                    if i >= 2:
                        ac.wait_ge(d_split[i % 2], split_done(L, b, i % 2, 1))
                    m = qv + (i % 2) * KC + i // 2
                    act(split[:, i % 2, 0, :].bitcast(F32R), bank[:, K + i % 2, :], ACT.Identity, bias=vecs[:, m:m + 1]).then_inc(qk_hi.sem, 1)

                def max_high(g):
                    wait(mT_ps, L, b, g + 1)
                    if g > 0:
                        ac.wait_ge(d_mput[(g - 1) % 2], mput_done(L, b, g - 1))
                    nc.scalar.copy(m_hi.bitcast(F32R), bank[0:4, X, :]).then_inc(mT_hi.sem, 1)

                def exp(arg):
                    step, pair = arg
                    if step == 0 and pair == 0:
                        for s in range(2):
                            ac.wait_ge(d_split[s], split_done(L, b, s, 2))
                    wait(st_ps, L, b, 2 * step + pair + 1)
                    if step > 0 and pair == 0:
                        wait(p_used, L, b, step)
                    act(probs[:, 2 * pair:2 * pair + 2, :], bank[:, K:K + 2, :], ACT.Exp, scale=SCALE).then_inc(p_ok.sem, 1)

                return {"input_a": input_a, "qk": qk, "max_out": max_high, "keys": exp}

            def rest(L, b):
                def gate(g):
                    wait(gate_ps, L, b, g + 1)
                    nc.scalar.copy(gate_rows[:, GATES[L][g], :], bank[:, R + g % 2, 0:C]).then_inc(gate_ok.sem, 1)

                def keys_x(_):
                    wait(kx_ps, L, b, 1)
                    kv = VECS[f"kx{L}"][1]
                    for m in range(KC):
                        i = act(kxT[:, m, :], bank[:, R + 1, m * S2:(m + 1) * S2], ACT.Identity, bias=vecs[:, kv + m:kv + m + 1])
                    i.then_inc(kx_ok.sem, 1)

                def input_r(arg):
                    j, h = arg
                    wait(rT_in, L, b, nth(j, h))
                    wait(now_r_ok, L, b, 1)
                    if h > 0 and j == 1:
                        wait(up_ps, L, b, UNITS_UP[L])
                    to_feature(L, j, lambda k: hR[:, k, :], R + 1, mod_rest, hr_ok)

                def query_x(h):
                    qv = VECS[f"qx{L}"][1]
                    wait(qx_ps, L, b, h + 1)
                    for m in range(KC):
                        i = act(qT[:, m, :], bank[:, R, m * HT:(m + 1) * HT], ACT.Identity, bias=vecs[:, qv + m:qv + m + 1])
                    i.then_inc(qx_ok.sem, 1)

                def scores_x(n):
                    if L == 0:
                        wait(sx_ps, L, b, n + 1)
                        if n > 0:
                            wait(sx_max, L, b, n)
                        nc.scalar.copy(score_sb, bank[:, R, :]).then_inc(sx_sb.sem, 1)

                def exp_x(n):
                    wait(sx_max, L, b, n + 1)
                    act(p_tm[n % 2], p_tm[n % 2], ACT.Exp, scale=SCALE).then_inc(ex_ok.sem, 1)

                def probs_x(n):
                    t, c = n // KC % 2, n % KC
                    wait(pxT_ps, L, b, n + 1)
                    i = nc.scalar.copy(hid[:, 4 * c:4 * c + 4, t * P:(t + 1) * P],
                                       bank[:, R + 1, :].rearrange("p (r t) -> p r t", r=4))
                    i.then_inc(px_ok.sem, 1)

                def hidden(h):
                    mv_ = VECS[f"m1{L}"][1]
                    fn = [ACT.Silu, ACT.Gelu_apprx_tanh, ACT.Gelu][L]
                    for u in range(UNITS_UP[L]):
                        wait(up_ps, L, b, h * UNITS_UP[L] + u + 1)
                        for e in range(1 if L == 0 else 2):
                            m = u if L == 0 else 2 * u + e
                            i = act(hid[:, m, :], bank[:, R + u % 2, e * HT:(e + 1) * HT], fn, bias=vecs[:, mv_ + m:mv_ + m + 1])
                        i.then_inc(act_ok.sem, 1)

                return {"gate": gate, "keys_x": keys_x, "input_r": input_r, "query_x": query_x, "scores_x": scores_x,
                        "exp_x": exp_x, "probs_x": probs_x, "up": hidden}

            def both(L, b, L_rest, b_rest):
                mine = attention(L, b) | (rest(L_rest, b_rest) if L_rest is not None else {})
                for stage, arg in ORDER[L, L_rest]:
                    if stage in mine:
                        mine[stage](arg)

            for L in range(3):
                both(L, 0, L - 1 if L else None, NB - 1)
                if L > 0:
                    ac.wait_ge(y_ps.sem, y_ps.end(L - 1))
                    load_late(ac, L)
                    load_layer(ac, L + 1)
                with ac.Fori(0, NB - 1) as r:
                    both(L, (r, 1), L, r)
            alone = rest(2, NB - 1)
            for stage, arg in ORDER[None, 2]:
                if stage in alone:
                    alone[stage](arg)
            L = 3
            ac.dma_start(router_in[:, :], a["L3_xcond_router_b"].rearrange("(e o) -> e o", o=1), allow_slow_non_contiguous=True).then_inc(d_rb, 16)
            ac.wait_ge(y_ps.sem, y_ps.end(2))
            load_late(ac, 3)
            with ac.Fori(0, NB) as b:
                wait(kx_ps, L, b, 1)
                nc.scalar.copy(kxT[:, :, :], bank[:, X, 0:KC * S2].rearrange("p (k s) -> p k s", k=KC)).then_inc(kx_ok.sem, 1)
                wait(qx_ps, L, b, 1)
                nc.scalar.copy(kqT, bank[:, O, 0:KC * S2].rearrange("p (k s) -> p k s", k=KC)).then_inc(qx_ok.sem, 1)
                for h in range(2):
                    wait(aT_ps, L, b, h + 1)
                    to_feature(L, 0, lambda k: hT[:, k, h * HT:(h + 1) * HT], A + h, None, ha_ok)
                wait(sx_max, L, b, 1)
                for t in range(NT):
                    i = act(p_tm3[:, t, :], bank[:, A, t * S2:(t + 1) * S2], ACT.Exp, bias=sm[:, 1, t:t + 1], scale=float(C) ** -0.5,
                            accum_out=sm[:, 2, t:t + 1])
                i.then_inc(ex_ok.sem, 1)
                wait(pxT_ps, L, b, 1)
                nc.scalar.copy(pT3[0:S2, :], bank[0:S2, X, :]).then_inc(px_ok.sem, 1)
                for m in range(KC):
                    wait(ev_ps, L, b, m + 1)
                    nc.scalar.copy(evT[:, m, :], bank[:, A + m, :]).then_inc(ev_ok.sem, 1)
                wait(rm_ok, L, b, 1)
                act(pr[:, :, :], lg[:, :, :], ACT.Exp).then_inc(re_ok.sem, 1)
                for m in range(NX * RC + 2):
                    wait(up_ps, L, b, m + 1)
                    if m < NX * RC:
                        e = m // RC
                        if e >= 2 and m % RC == 0:
                            wait(ex_out, L, b, 2 * (e - 1))
                        dst = hid3[e % 2][:, m % RC, :]
                    else:
                        dst = uT[:, m - NX * RC, :]
                    act(dst, bank[:, B + m % 4, :], ACT.Silu, bias=anchor_now[:, m:m + 1]).then_inc(act_ok.sem, 1)
                for k in range(KC):
                    wait(rT_ps, L, b, k + 1)
                    nc.scalar.copy(hT[:, k, :], bank[:, B + k, :]).then_inc(rT_ok.sem, 1)
                wait(gs_in, L, b, 1)
                act(g_tm, g_tm, ACT.Sigmoid).then_inc(gs_ok.sem, 1)

        @blk.vector
        def _(dv):
            n = [0]
            V = nc.vector

            def link(ins):
                n[0] += 1
                ins.then_inc(dve_chain, 1)
                dv.wait_ge(dve_chain, n[0])

            def fresh():
                n[0] = 0
                dv.sem_clear(dve_chain)

            def wait(s, L, b, k):
                dv.wait_ge(s.sem, s.at(L, b, k))

            def apart():
                dv.sem_inc(apart_dve, 1)

            dv.sem_inc(ox_ok.sem, 1)
            dv.sem_inc(y_ok.sem, 1)
            dv.sem_inc(f_ok.sem, 1)
            dv.wait_ge(consts, 1)
            for s in range(SLOTS):
                link(V.tensor_scalar(k_stack[0:KS, s, :, :].rearrange("p h (a t) -> p (h a) t", a=2), zeros[0:KS, :].unsqueeze(1).to_broadcast([KS, 8, C]), 1.0, None, ALU.add))
            for s in range(SLOTS):
                link(V.tensor_copy(q_stack[0:KS, s, :, :].rearrange("p h (a t) -> p (h a) t", a=2), zeros[0:KS, :].unsqueeze(1).to_broadcast([KS, 8, C])))
            link(V.tensor_scalar(one_row[:, :], zeros[:, 0:P], ident[:, 0:1], None, ALU.add))
            dv.wait_ge(d_mask, 16)
            link(V.tensor_copy(mask_row[:, :, :], zeros[:, 0:NB * S2].rearrange("p (b s) -> p b s", b=NB)))
            link(V.tensor_scalar(mask_row[0:1, :, :], mrow_words[:, :].bitcast(U8).rearrange("p (b s) -> p b s", b=NB), MASKED, None, ALU.mult))
            V.memset(sm[:, :, :], 0.0).then_inc(const_r, 1)
            dv.wait_ge(d_ctx, 16)
            for g in range(2):
                link(V.bn_stats(stats[:, g, :], ctx_tm[:, g, :]))
            link(V.bn_aggr(mv[:, 0, :], stats[:, 0, :]))
            V.bn_aggr(mv[:, 1, :], stats[:, 1, :]).then_inc(ctx_var, 1)
            dv.wait_ge(ctx_rstd, 1)
            for g in range(2):
                i = V.tensor_scalar(ctx_tm[:, 2 + g, :], ctx_tm[:, g, :], mv[:, g, 0:1], rstd[:, g:g + 1], ALU.subtract, ALU.mult)
                if g == 0:
                    link(i)
            i.then_inc(ctx_n, 1)
            dv.wait_ge(vecs_ok, 1)
            for L in range(3):
                dv.wait_ge(ada_ps, L + 1)
                av = VECS[f"ada{L}"][1]
                ms = mod[:, ADA_AT[L]:ADA_AT[L] + ADA[L], :]
                link(V.tensor_tensor(ms, bank[:, B + L, 0:ADA[L] * NB].rearrange("p (m b) -> p m b", b=NB),
                                     vecs[:, av:av + ADA[L]].unsqueeze(2).to_broadcast([P, ADA[L], NB]), ALU.add))
                for j in range(3):
                    if SCALE_OF[L][j] is not None:
                        sc = ADA_AT[L] + SCALE_OF[L][j]
                        link(V.tensor_scalar(mod[:, sc:sc + KC, :], mod[:, sc:sc + KC, :], 1.0, None, ALU.add))
            dv.wait_ge(ctx_ok, 4)
            dv.wait_ge(d_x, 16 * 3 * NB)

            def x_of(b):
                return x_all[:, batch_of(b, NT * C)].rearrange("p (t c) -> p t c", t=NT)

            def moments(h, xv, st, m_v, done):
                for t in (2 * h, 2 * h + 1):
                    V.bn_stats(st[:, t, :], xv[:, t, :]).then_inc(dve_chain, 1)
                n[0] += 2
                dv.wait_ge(dve_chain, n[0])
                link(V.bn_aggr(m_v[:, 2 * h, :], st[:, 2 * h, :]))
                V.bn_aggr(m_v[:, 2 * h + 1, :], st[:, 2 * h + 1, :]).then_inc(done.sem, 1)

            def normalise(h, xv, m_v, r_std, done):
                for t in (2 * h, 2 * h + 1):
                    i = V.tensor_scalar(xn[:, t, :], xv[:, t, :], m_v[:, t, 0:1], r_std[:, t:t + 1], ALU.subtract, ALU.mult)
                i.then_inc(done.sem, 1)

            def attention(L, b):
                w, xv = W[L], x_of(b)

                def now(_):
                    V.tensor_copy(mod_now[:, 0:ADA[L]], mod[:, ADA_AT[L]:ADA_AT[L] + ADA[L], batch_of(b, 1)].rearrange("p m o -> p (m o)")).then_inc(now_ok.sem, 1)

                def norm_a(h):
                    if h == 0 and L + (not isinstance(b, int)) > 0:
                        before = (L, (b[0], 0)) if isinstance(b, tuple) else (L - 1, NB - 1)
                        wait(rT_in, *before, 0)
                    wait(rstd_a, L, b, h + 1)
                    apart()
                    normalise(h, xv, mv, rstd, xa_ok)

                def qk(i):
                    m = VECS[f"qk{L}"][1] + (i % 2) * KC + i // 2
                    wait(qk_hi, L, b, i + 1)
                    V.scalar_tensor_tensor(out=split[:, i % 2, 1, :].bitcast(F32R), in0=bank[:, K + i % 2, :], scalar=vecs[:, m:m + 1],
                                           in1=split[:, i % 2, 0, :], op0=ALU.add, op1=ALU.subtract).then_inc(qk_lo.sem, 1)

                def v(h):
                    wait(v_ps, L, b, h + 1)
                    for t in range(2):
                        i = V.tensor_tensor(v_aug[:, 2 * h + t, :, 0:HD],
                                            bank[:, S + h, t * C:(t + 1) * C].rearrange("p (h d) -> p h d", d=HD),
                                            w["bv"].rearrange("p (h d) -> p h d", d=HD), ALU.add)
                        if t == 0:
                            link(i)
                    i.then_inc(v_ok.sem, 1)

                def tile(m):
                    g, u = m // UNITS[L], m % UNITS[L]
                    wait(s_ps, L, b, m + 1)
                    if L == 0:
                        i = V.tensor_reduce(nm[:, u, 4 * g:4 * g + 4], bank[:, S + m % 2, :].rearrange("p (h s) -> p h s", h=4),
                                            AX.X, ALU.max, negate=True)
                    else:
                        h, t = 4 * g + u // 4, u % 4
                        i = V.tensor_reduce(nm[:, t, h:h + 1], bank[:, S + m % 2, :], AX.X, ALU.max, negate=True)
                    i.then_inc(s_max.sem, 1)

                def max_low(g):
                    wait(mT_hi, L, b, g + 1)
                    if g > 0:
                        dv.wait_ge(d_mput[(g - 1) % 2], mput_done(L, b, g - 1))
                    V.tensor_tensor(m_lo.bitcast(F32R), bank[0:4, X, :], m_hi, ALU.subtract).then_inc(mT_lo.sem, 1)

                def heads(g):
                    if g > 0:
                        wait(hd_ok, L, b, g)
                    wait(p_used, L, b, (g + 1) * KCH[L])
                    V.transpose(p_one[:, :], bank[:, O, :]).then_inc(o_ok.sem, 1)
                    wait(o_ok, L, b, g + 1)
                    blocks = p_one[:, :].rearrange("p (n d) -> p n d", d=32)
                    link(V.reciprocal(block_r[:, :].unsqueeze(2), blocks[:, :, HD:HD + 1]))
                    link(V.tensor_tensor(blocks, blocks, block_r[:, :].unsqueeze(2).to_broadcast([P, T // 32, 32]), ALU.mult))
                    V.transpose(work[:, g, :], p_one[:, :]).then_inc(hd_ok.sem, 1)

                return {"now": now, "moments_a": lambda h: moments(h, xv, stats, mv, var_a), "norm_a": norm_a, "qk": qk, "v": v,
                        "tile": tile, "max_low": max_low, "heads": heads}

            def rest(L, b):
                w, xv = W[L], x_of(b)

                def now_r(_):
                    V.tensor_copy(mod_rest[:, 0:ADA[L]], mod[:, ADA_AT[L]:ADA_AT[L] + ADA[L], batch_of(b, 1)].rearrange("p m o -> p (m o)")).then_inc(now_r_ok.sem, 1)

                def make_diag(g):
                    if g == 0:
                        wait(now_r_ok, L, b, 1)
                    gc = GATE_OF[L][GATES[L][g]]
                    for k in range(KC):
                        i = V.tensor_scalar(diag[g][:, k, :], ident[:, :], mod_rest[:, gc + k:gc + k + 1], None, ALU.mult)
                        if k + 1 < KC or g + 1 < len(GATES[L]):
                            link(i)
                    if g + 1 == len(GATES[L]):
                        i.then_inc(diag_ok.sem, 1)

                def values_x(_):
                    wait(vx_ps, L, b, 1)
                    for h in range(2):
                        ps = bank[h * S2:(h + 1) * S2, R, 0:C].rearrange("p (r e d) -> p r e d", e=2, d=HD)[:, :, h, :]
                        bv = w["bvx"].rearrange("p (r e d) -> p r e d", e=2, d=HD)[h * S2:(h + 1) * S2, :, h, :]
                        i = V.tensor_tensor(v_bd[h * S2:(h + 1) * S2, :, h * HD:(h + 1) * HD], ps, bv, ALU.add)
                        if h == 0:
                            link(i)
                    i.then_inc(vx_ok.sem, 1)

                def residual(j, h, nth_out, bk):
                    if j > 0:
                        wait(xb_ok, L, b, nth(j, h))
                    wait(y_ps, L, b, nth_out)
                    ps = bank[:, bk, :].rearrange("p (t c) -> p t c", t=2)
                    xh = xv[:, 2 * h:2 * h + 2, :]
                    if j in GATES[L]:
                        if j == 0 and h == 0:
                            wait(gate_ok, L, b, len(GATES[L]))
                        link(V.tensor_tensor(ps, ps, gate_rows[:, j, :].unsqueeze(1).to_broadcast([P, 2, C]), ALU.mult))
                    link(V.tensor_tensor(xh, ps, xh, ALU.add))
                    dv.sem_inc(y_ok.sem, 1)

                def out_s(arg):
                    h, t = arg
                    if t == 1:
                        residual(0, h, h + 1, R + 1 - h)
                        if h == 0:
                            moments(0, xv, stats_r, mv_r, var_r)

                def norm_r(arg):
                    j, h = arg
                    if j == 1 and h == 0:
                        wait(aT_ps, *A_OF[0], 2)
                    wait(rstd_r_ok, L, b, nth(j, h))
                    apart()
                    normalise(h, xv, mv_r, rstd_r, xr_ok)

                def scores_x(m):
                    if L > 0:
                        wait(sx_ps, L, b, m + 1)
                        ps = bank[:, R, :].rearrange("p (h s) -> p h s", h=8)
                        link(V.tensor_reduce(nm_x[:, :], ps, AX.X, ALU.max, negate=True))
                        if m >= 2:
                            wait(pxT_ps, L, b, m - 1)
                        V.tensor_tensor(p_tm[m % 2].rearrange("p (h s) -> p h s", h=8), ps,
                                        nm_x[:, :].unsqueeze(2).to_broadcast([P, 8, S2]), ALU.add).then_inc(sx_max.sem, 1)
                        return
                    wait(sx_sb, L, b, m + 1)
                    apart()
                    top_steps((0,))

                def top_steps(steps):
                    sc = score_sb.rearrange("p (h s) -> p h s", h=8)
                    rs = rest_sb[:, :].rearrange("p (h s) -> p h s", h=8)
                    for step in steps:
                        for h in range(8):
                            if step == 0:
                                i = V.max(top[:, h, 0, :], sc[:, h, :])
                            elif step == 1:
                                i = V.match_replace(rs[:, h, :], top[:, h, 0, :], sc[:, h, :], -LARGE)
                            elif step == 2:
                                i = V.max(top[:, h, 1, :], rs[:, h, :])
                            else:
                                i = V.match_replace(rs[:, h, :], top[:, h, 1, :], rs[:, h, :], -LARGE)
                            i.then_inc(dve_chain, 1)
                        n[0] += 8
                        dv.wait_ge(dve_chain, n[0])

                def top_x(m):
                    if m > 0:
                        wait(px_tm, L, b, m)
                        apart()
                    top_steps((1, 2, 3))
                    sc = score_sb.rearrange("p (h s) -> p h s", h=8)
                    if m >= 2:
                        wait(pxT_ps, L, b, m - 1)
                    V.tensor_tensor(p_tm[m % 2].rearrange("p (h s) -> p h s", h=8), sc,
                                    top[:, :, 0, 0:1].to_broadcast([P, 8, S2]), ALU.subtract).then_inc(sx_max.sem, 1)

                def exp_x(m):
                    if L == 0:
                        wait(ex_ok, L, b, m + 1)
                        V.scalar_tensor_tensor(out=p_tm[m % 2], in0=rest_sb[:, :], scalar=-LARGE, in1=p_tm[m % 2],
                                               op0=ALU.is_equal, op1=ALU.mult).then_inc(px_tm.sem, 1)

                def heads_x(h):
                    wait(ox_ps, L, b, h + 1)
                    link(V.reciprocal(xsum, bank[:, R + 1, :]))
                    V.tensor_tensor(xT[:, :, :], bank[:, R, :].rearrange("p (k t) -> p k t", k=KC),
                                    xsum.rearrange("p (k t) -> p k t", k=KC), ALU.mult).then_inc(ox_ok.sem, 1)

                def out_x(h):
                    residual(1, h, (3, 5)[h], R)
                    moments(h, xv, stats_r, mv_r, var_r)

                def hidden(h):
                    if L == 0:
                        mv_ = VECS["m10"][1] + HIDC
                        for m in range(UNITS_UP[L]):
                            wait(act_ok, L, b, h * UNITS_UP[L] + m + 1)
                            V.scalar_tensor_tensor(out=hid[:, m, :], in0=bank[:, R + m % 2, HT:2 * HT],
                                                   scalar=vecs[:, mv_ + m:mv_ + m + 1], in1=hid[:, m, :],
                                                   op0=ALU.add, op1=ALU.mult).then_inc(hid_ok.sem, 1)

                def down(arg):
                    h, tile, part = arg
                    if tile == 1 and part == 1:
                        residual(2, h, (4, 6)[h], R)

                return {"now_r": now_r, "diag": make_diag, "values_x": values_x, "out_s": out_s, "norm_r": norm_r,
                        "moments_r": lambda jh: moments(1, xv, stats_r, mv_r, var_r),
                        "scores_x": scores_x, "top_x": top_x, "exp_x": exp_x, "heads_x": heads_x, "out_x": out_x,
                        "up": hidden, "down": down}

            A_OF = [None]

            def both(L, b, L_rest, b_rest):
                A_OF[0] = (L, b)
                mine = attention(L, b) | (rest(L_rest, b_rest) if L_rest is not None else {})
                for stage, arg in ORDER[L, L_rest]:
                    if stage in mine:
                        mine[stage](arg)
                fresh()

            dv.wait_ge(v_ones, 1)
            for L in range(3):
                dv.wait_ge(d_w[L], 16 * N_LOADS[L])
                fresh()
                both(L, 0, L - 1 if L else None, NB - 1)
                with dv.Fori(0, NB - 1) as r:
                    both(L, (r, 1), L, r)
            alone = rest(2, NB - 1)
            A_OF[0] = (2, NB - 1)
            for stage, arg in ORDER[None, 2]:
                if stage in alone:
                    alone[stage](arg)
            fresh()

            L, w = 3, W[3]
            dv.wait_ge(d_w[3], 16 * N_LOADS[3])
            dv.wait_ge(anc_ps, 1)
            ev = VECS["eb1"][1]
            V.tensor_tensor(anchor_b[:, 0:NX * RC, :], bank[:, B, 0:NX * RC * NB].rearrange("p (m b) -> p m b", b=NB),
                            vecs[:, ev:ev + NX * RC].unsqueeze(2).to_broadcast([P, NX * RC, NB]), ALU.add).then_inc(dve_chain, 1)
            gv = VECS["gb1"][1]
            V.tensor_tensor(anchor_b[:, NX * RC:, :], bank[:, B, NX * RC * NB:(NX * RC + 2) * NB].rearrange("p (m b) -> p m b", b=NB),
                            vecs[:, gv:gv + 2].unsqueeze(2).to_broadcast([P, 2, NB]), ALU.add).then_inc(anc_ok, 1)
            V.tensor_copy(router_b[:, :], bank[0:NX, B + 1, 0:NB]).then_inc(anc_ok, 1)
            V.tensor_copy(wqT, bank[:, A, :].rearrange("p (m c) -> p m c", m=KC)).then_inc(anc_ok, 1)
            dv.wait_ge(anc_ok, 3)
            dv.wait_ge(dve_chain, 1)
            dv.wait_ge(d_rb, 16)
            n[0] = 1
            link(V.tensor_scalar(router_b[:, :], router_b[:, :], router_in[:, :], None, ALU.add))
            fresh()
            with dv.Fori(0, NB) as b:
                xv = x_all[:, bass.ds(b * (NT * C), NT * C)].rearrange("p (t c) -> p t c", t=NT)
                link(V.tensor_copy(anchor_now[:, :], anchor_b[:, :, bass.ds(b, 1)].rearrange("p m o -> p (m o)")))
                link(V.tensor_copy(router_now[:, :], router_b[:, bass.ds(b, 1)]))
                V.tensor_scalar(router_diag[:, :], ident[0:NX, 0:NX], router_now[:, :], None, ALU.mult).then_inc(now_ok.sem, 1)
                for h in range(2):
                    moments(h, xv, stats, mv, var_a)
                for h in range(2):
                    wait(rstd_a, L, b, h + 1)
                    apart()
                    normalise(h, xv, mv, rstd, xa_ok)
                wait(vx_ps, L, b, 1)
                V.tensor_copy(v3[0:S2, :], bank[0:S2, X, 0:C]).then_inc(vx_ok.sem, 1)
                wait(sx_ps, L, b, 1)
                link(V.tensor_reduce(sm[:, 0, :], bank[:, A, 0:NT * S2].rearrange("p (t s) -> p t s", t=NT), AX.X, ALU.max, negate=True))
                V.tensor_scalar(sm[:, 1, :], sm[:, 0, :], float(C) ** -0.5, None, ALU.mult).then_inc(sx_max.sem, 1)
                wait(ex_ok, L, b, 1)
                link(V.reciprocal(sm[:, 3, :], sm[:, 2, :]))
                V.tensor_tensor(p_tm3, p_tm3, sm[:, 3, :].unsqueeze(2).to_broadcast([P, NT, S2]), ALU.mult).then_inc(px_tm.sem, 1)
                wait(rl_ps, L, b, 1)
                link(V.tensor_copy(lg[:, :, :], bank[:, X, 0:NT * NX].rearrange("p (t e) -> p t e", t=NT)))
                link(V.tensor_reduce(sm[:, 4, :], lg[:, :, :], AX.X, ALU.max))
                V.tensor_tensor(lg[:, :, :], lg[:, :, :], sm[:, 4, :].unsqueeze(2).to_broadcast([P, NT, NX]), ALU.subtract).then_inc(rm_ok.sem, 1)
                wait(re_ok, L, b, 1)
                link(V.tensor_reduce(sm[:, 5, :], pr[:, :, :], AX.X, ALU.add))
                link(V.reciprocal(sm[:, 5, :], sm[:, 5, :]))
                link(V.tensor_tensor(pr[:, :, :], pr[:, :, :], sm[:, 5, :].unsqueeze(2).to_broadcast([P, NT, NX]), ALU.mult))
                for e in range(NX):
                    for t in range(NT):
                        if e == 0:
                            V.tensor_scalar(xn[:, t, :], w["b2"][:, 0, :], pr[:, t, 0:1], None, ALU.mult).then_inc(dve_chain, 1)
                        else:
                            V.scalar_tensor_tensor(out=xn[:, t, :], in0=w["b2"][:, e, :], scalar=pr[:, t, e:e + 1], in1=xn[:, t, :],
                                                   op0=ALU.mult, op1=ALU.add).then_inc(dve_chain, 1)
                    n[0] += NT
                    dv.wait_ge(dve_chain, n[0])
                for e in range(NX):
                    for h in range(2):
                        wait(ex_out, L, b, 2 * e + h + 1)
                        if e > 0:
                            wait(acc_ok, L, b, 2 * (e - 1) + h + 1)
                        for t in (2 * h, 2 * h + 1):
                            i = V.scalar_tensor_tensor(out=xn[:, t, :], in0=bank[:, A + h, (t % 2) * C:(t % 2 + 1) * C], scalar=pr[:, t, e:e + 1],
                                                       in1=xn[:, t, :], op0=ALU.mult, op1=ALU.add)
                            if t % 2 == 0:
                                link(i)
                        i.then_inc(acc_ok.sem, 1)
                for h in range(2):
                    wait(g_ps, L, b, h + 1)
                    i = V.tensor_tensor(g_tm[:, 2 * h:2 * h + 2, :], bank[:, A + h, :].rearrange("p (t c) -> p t c", t=2),
                                        w["gb2"].unsqueeze(1).to_broadcast([P, 2, C]), ALU.add)
                    if h == 0:
                        link(i)
                i.then_inc(gs_in.sem, 1)
                wait(gs_ok, L, b, 1)
                for h in range(2):
                    wait(f_ps, L, b, h + 1)
                    ps = bank[:, A + h, :].rearrange("p (t c) -> p t c", t=2)
                    xh = xv[:, 2 * h:2 * h + 2, :]
                    link(V.tensor_tensor(ps, ps, w["ob"].unsqueeze(1).to_broadcast([P, 2, C]), ALU.add))
                    link(V.tensor_tensor(ps, ps, g_tm[:, 2 * h:2 * h + 2, :], ALU.mult))
                    i = V.tensor_tensor(xh, ps, xh, ALU.add)
                    if h == 0:
                        link(i)
                i.then_inc(f_ok.sem, 1)
                fresh()


_OUT = (NB, T, C)


def kernel(**inputs):
    import concourse.bacc as bacc
    from concourse.bass_utils import run_bass_kernel_spmd as run

    nc = bacc.Bacc("TRN2", target_bir_lowering=False, num_devices=1)
    arrays, aps = {}, {}
    for name, v in inputs.items():
        v = np.ascontiguousarray(v)
        if v.dtype == np.bool_:
            v = v.view(np.uint32)
        arrays[f"in_{name}"] = v
        aps[name] = nc.dram_tensor(f"in_{name}", v.shape, mybir.dt.from_np(v.dtype), kind="ExternalInput").ap()
    out = nc.dram_tensor("out_x", _OUT, F32, kind="ExternalOutput").ap()
    build(nc, aps, out)
    r = run(nc, [arrays], core_ids=[0])
    return r.results[0]["out_x"]
```
